# Optimizing a Trainium2 kernel written in Bass

```python
import numpy as np
import jax
import jax.numpy as jnp

def _softmax(x, axis=-1):
    return jax.nn.softmax(x, axis=axis)

def _gelu(x):
    return jax.nn.gelu(x, approximate=True)

def _silu(x):
    return jax.nn.silu(x)

def _sigmoid(x):
    return jax.nn.sigmoid(x)

def _layernorm(x, axis=-1, eps=1e-05):
    m = jnp.mean(x, axis=axis, keepdims=True)
    v = jnp.var(x, axis=axis, keepdims=True)
    return (x - m) / jnp.sqrt(v + eps)

def _scatter_add(tgt, idx, src, axis=0):
    return tgt.at[idx].add(src)

def _segment_sum(src, seg, n):
    return jax.ops.segment_sum(src, seg, n)
kernel_name = 'mk_seq_postln_d2_jaxref_r8_664370'

def setup_inputs(seed: int=0):
    np.random.seed(seed)
    _w = jnp.asarray

    def _L0_attn_setup():
        import jax, jax.numpy as jnp
        import numpy as np
        D_MODEL = 128
        N_LAYERS = 2
        D_STATE = 64
        D_CONV = 4
        EXPAND = 2
        D_INNER = EXPAND * D_MODEL
        HEADDIM = D_STATE
        NHEADS = D_INNER // HEADDIM
        CONV_DIM = D_INNER + 2 * D_STATE
        D_IN_PROJ = 2 * D_INNER + 2 * D_STATE + NHEADS
        EPS = 1e-05

        def _layernorm(x, w, b):
            m = x.mean(-1, keepdims=True)
            v = ((x - m) ** 2).mean(-1, keepdims=True)
            return (x - m) * jax.lax.rsqrt(v + EPS) * w + b

        def _mamba2(u, in_w, conv_w, conv_b, dt_bias, A_log, Dp, rms_w, out_w):
            b, l, _ = u.shape
            zxbcdt = u @ in_w.T
            z, xBC, dt = jnp.split(zxbcdt, [D_INNER, D_INNER + CONV_DIM], axis=-1)
            dt = jax.nn.softplus(dt + dt_bias)
            xBC = jnp.transpose(xBC, (0, 2, 1))
            xBC = jax.lax.conv_general_dilated(xBC, conv_w[:, None, :], (1,), [(D_CONV - 1, 0)], dimension_numbers=('NCH', 'OIH', 'NCH'), feature_group_count=CONV_DIM)
            xBC = jnp.transpose(xBC, (0, 2, 1)) + conv_b
            xBC = jax.nn.silu(xBC)
            xh, Bm, Cm = jnp.split(xBC, [D_INNER, D_INNER + D_STATE], axis=-1)
            xh = xh.reshape(b, l, NHEADS, HEADDIM)
            A = -jnp.exp(A_log)
            dA = jnp.exp(dt * A)

            def step(state, inputs):
                dA_t, dt_t, x_t, B_t, C_t = inputs
                state = dA_t[:, :, None, None] * state + (dt_t[:, :, None] * x_t)[..., None] * B_t[:, None, None, :]
                y_t = jnp.einsum('bhpn,bn->bhp', state, C_t)
                return (state, y_t)
            xs = (jnp.moveaxis(dA, 1, 0), jnp.moveaxis(dt, 1, 0), jnp.moveaxis(xh, 1, 0), jnp.moveaxis(Bm, 1, 0), jnp.moveaxis(Cm, 1, 0))
            init = jnp.zeros((b, NHEADS, HEADDIM, D_STATE), u.dtype)
            _, ys = jax.lax.scan(step, init, xs)
            y = jnp.moveaxis(ys, 0, 1) + Dp[None, None, :, None] * xh
            y = y.reshape(b, l, D_INNER)
            y = y * jax.nn.silu(z)
            y = y * jax.lax.rsqrt(jnp.mean(y * y, -1, keepdims=True) + EPS) * rms_w
            return y @ out_w.T
        key = jax.random.key(seed)
        ks = jax.random.split(key, 8)
        B, L = (2, 512)
        return {'x': jax.random.normal(ks[0], (B, L, D_MODEL), jnp.float32), 'ln_w': jnp.ones((N_LAYERS, D_MODEL), jnp.float32), 'ln_b': jnp.zeros((N_LAYERS, D_MODEL), jnp.float32), 'in_proj_w': jax.random.normal(ks[1], (N_LAYERS, D_IN_PROJ, D_MODEL), jnp.float32) * D_MODEL ** (-0.5), 'conv_w': jax.random.normal(ks[2], (N_LAYERS, CONV_DIM, D_CONV), jnp.float32) * D_CONV ** (-0.5), 'conv_b': jnp.zeros((N_LAYERS, CONV_DIM), jnp.float32), 'dt_bias': jax.random.normal(ks[3], (N_LAYERS, NHEADS), jnp.float32) * 0.5, 'A_log': jnp.log(jax.random.uniform(ks[4], (N_LAYERS, NHEADS), jnp.float32, 1.0, 16.0)), 'D': jnp.ones((N_LAYERS, NHEADS), jnp.float32), 'rms_w': jnp.ones((N_LAYERS, D_INNER), jnp.float32), 'out_proj_w': jax.random.normal(ks[5], (N_LAYERS, D_MODEL, D_INNER), jnp.float32) * D_INNER ** (-0.5)}
    _L0_attn_in = _L0_attn_setup()

    def _L0_ffn_setup():
        import jax, jax.numpy as jnp
        import numpy as np
        EPS = 1e-08

        def _ternary_linear(x, w):
            alpha = jnp.mean(jnp.abs(w))
            w_t = jnp.sign(w) * (jnp.abs(w) > 0.5 * alpha).astype(w.dtype)
            w_q = w + jax.lax.stop_gradient(w_t - w)
            d = x.shape[-1]
            rms = jnp.sqrt(jnp.sum(x * x, axis=-1, keepdims=True)) / jnp.sqrt(jnp.asarray(d, x.dtype))
            x_norm = x / (rms + EPS)
            return jnp.einsum('bsd,fd->bsf', x_norm, w_q)
        key = jax.random.key(seed)
        k1, k2, k3 = jax.random.split(key, 3)
        d_model, d_ff = (128, 512)
        B, S = (4, 512)
        x = jax.random.normal(k1, (B, S, d_model), dtype=jnp.float32)
        w_up = jax.random.normal(k2, (d_ff, d_model), dtype=jnp.float32) * 0.02
        w_down = jax.random.normal(k3, (d_model, d_ff), dtype=jnp.float32) * 0.02
        return {'x': x, 'w_up': w_up, 'w_down': w_down}
    _L0_ffn_in = _L0_ffn_setup()

    def _L1_attn_setup():
        import math
        import jax, jax.numpy as jnp
        import numpy as np
        N, T, C = (4, 256, 128)
        H, HS = (16, 64)
        LAYER_ID, N_LAYERS = (1, 12)
        _EPS = math.exp(-LAYER_ID / N_LAYERS)
        EPS_R = _EPS / 2.0
        EPS_K = _EPS + 0.3 * LAYER_ID / (N_LAYERS - 1)
        EPS_V = _EPS

        def _time_interp(x, eps):
            Tn = x.shape[1]
            curr = jnp.pad(x, ((0, 0), (1, 0), (0, 0)))[:, :Tn]
            prev = jnp.pad(x, ((0, 0), (0, 1), (0, 0)))[:, 1:]
            return eps * curr + (1.0 - eps) * prev
        key = jax.random.key(seed)
        ks = jax.random.split(key, 9)
        s = 1.0 / math.sqrt(C)
        return {'x': jax.random.normal(ks[0], (N, T, C), dtype=jnp.float32), 'Wr': jax.random.normal(ks[1], (H * HS, C), dtype=jnp.float32) * s, 'br': jax.random.normal(ks[2], (H * HS,), dtype=jnp.float32) * 0.01, 'Wk': jax.random.normal(ks[3], (H * HS, C), dtype=jnp.float32) * s, 'bk': jax.random.normal(ks[4], (H * HS,), dtype=jnp.float32) * 0.01, 'Wv': jax.random.normal(ks[5], (H * HS, C), dtype=jnp.float32) * s, 'bv': jax.random.normal(ks[6], (H * HS,), dtype=jnp.float32) * 0.01, 'Wo': jax.random.normal(ks[7], (C, H * HS), dtype=jnp.float32) * s, 'bo': jax.random.normal(ks[8], (C,), dtype=jnp.float32) * 0.01, 'time_decay': jnp.full((H * HS,), 0.1, dtype=jnp.float32), 'U': jnp.full((H * HS,), 0.1, dtype=jnp.float32)}
    _L1_attn_in = _L1_attn_setup()

    def _L1_ffn_setup():
        import jax, jax.numpy as jnp
        import numpy as np
        TOP_K = 4
        N_GROUP = 4
        TOPK_GROUP = 2
        ROUTED_SCALING = 1.0

        def _route(x_flat, gate_weight, e_bias):
            T = x_flat.shape[0]
            E = gate_weight.shape[0]
            logits = jnp.einsum('th,eh->te', x_flat, gate_weight)
            scores = jax.nn.sigmoid(logits)
            scores_for_choice = scores + e_bias[None, :]
            grp = scores_for_choice.reshape(T, N_GROUP, E // N_GROUP)
            top2, _ = jax.lax.top_k(grp, 2)
            group_scores = top2.sum(axis=-1)
            _, group_idx = jax.lax.top_k(group_scores, TOPK_GROUP)
            group_mask = jax.nn.one_hot(group_idx, N_GROUP, dtype=scores.dtype).sum(axis=1)
            score_mask = jnp.repeat(group_mask, E // N_GROUP, axis=1)
            tmp_scores = jnp.where(score_mask > 0, scores_for_choice, 0.0)
            _, topk_idx = jax.lax.top_k(tmp_scores, TOP_K)
            topk_weight = jnp.take_along_axis(scores, topk_idx, axis=1)
            denom = topk_weight.sum(axis=-1, keepdims=True) + 1e-20
            topk_weight = topk_weight / denom * ROUTED_SCALING
            return (topk_idx, topk_weight)
        key = jax.random.key(seed)
        k1, k2, k3, k4, k5 = jax.random.split(key, 5)
        B, S, H, I, E = (1, 256, 128, 64, 16)
        hidden_states = jax.random.normal(k1, (B, S, H), dtype=jnp.float32)
        gate_weight = jax.random.normal(k2, (E, H), dtype=jnp.float32) * (1.0 / np.sqrt(H))
        e_bias = jnp.zeros((E,), dtype=jnp.float32)
        gate_proj = jax.random.normal(k3, (E, I, H), dtype=jnp.float32) * 0.02
        up_proj = jax.random.normal(k4, (E, I, H), dtype=jnp.float32) * 0.02
        down_proj = jax.random.normal(k5, (E, H, I), dtype=jnp.float32) * 0.02
        return {'hidden_states': hidden_states, 'gate_weight': gate_weight, 'e_bias': e_bias, 'gate_proj': gate_proj, 'up_proj': up_proj, 'down_proj': down_proj}
    _L1_ffn_in = _L1_ffn_setup()
    _d = {'L0_attn_x': _L0_attn_in['x'], 'L0_attn_ln_w': _L0_attn_in['ln_w'], 'L0_attn_ln_b': _L0_attn_in['ln_b'], 'L0_attn_in_proj_w': _L0_attn_in['in_proj_w'], 'L0_attn_conv_w': _L0_attn_in['conv_w'], 'L0_attn_conv_b': _L0_attn_in['conv_b'], 'L0_attn_dt_bias': _L0_attn_in['dt_bias'], 'L0_attn_A_log': _L0_attn_in['A_log'], 'L0_attn_D': _L0_attn_in['D'], 'L0_attn_rms_w': _L0_attn_in['rms_w'], 'L0_attn_out_proj_w': _L0_attn_in['out_proj_w'], 'L0_ffn_w_up': _L0_ffn_in['w_up'], 'L0_ffn_w_down': _L0_ffn_in['w_down'], 'L1_attn_Wr': _L1_attn_in['Wr'], 'L1_attn_br': _L1_attn_in['br'], 'L1_attn_Wk': _L1_attn_in['Wk'], 'L1_attn_bk': _L1_attn_in['bk'], 'L1_attn_Wv': _L1_attn_in['Wv'], 'L1_attn_bv': _L1_attn_in['bv'], 'L1_attn_Wo': _L1_attn_in['Wo'], 'L1_attn_bo': _L1_attn_in['bo'], 'L1_attn_time_decay': _L1_attn_in['time_decay'], 'L1_attn_U': _L1_attn_in['U'], 'L1_ffn_gate_weight': _L1_ffn_in['gate_weight'], 'L1_ffn_e_bias': _L1_ffn_in['e_bias'], 'L1_ffn_gate_proj': _L1_ffn_in['gate_proj'], 'L1_ffn_up_proj': _L1_ffn_in['up_proj'], 'L1_ffn_down_proj': _L1_ffn_in['down_proj']}
    _x0 = _d['L0_attn_x']
    _d['L0_attn_x'] = jax.random.normal(jax.random.fold_in(jax.random.key(seed), 1), (2, 1024, 128), dtype=_x0.dtype)
    del _x0
    return _d

def reference(L0_attn_x, L0_attn_ln_w, L0_attn_ln_b, L0_attn_in_proj_w, L0_attn_conv_w, L0_attn_conv_b, L0_attn_dt_bias, L0_attn_A_log, L0_attn_D, L0_attn_rms_w, L0_attn_out_proj_w, L0_ffn_w_up, L0_ffn_w_down, L1_attn_Wr, L1_attn_br, L1_attn_Wk, L1_attn_bk, L1_attn_Wv, L1_attn_bv, L1_attn_Wo, L1_attn_bo, L1_attn_time_decay, L1_attn_U, L1_ffn_gate_weight, L1_ffn_e_bias, L1_ffn_gate_proj, L1_ffn_up_proj, L1_ffn_down_proj):

    def _L0_attn_ref(x, ln_w, ln_b, in_proj_w, conv_w, conv_b, dt_bias, A_log, D, rms_w, out_proj_w):
        import jax, jax.numpy as jnp
        import numpy as np
        D_MODEL = 128
        N_LAYERS = 2
        D_STATE = 64
        D_CONV = 4
        EXPAND = 2
        D_INNER = EXPAND * D_MODEL
        HEADDIM = D_STATE
        NHEADS = D_INNER // HEADDIM
        CONV_DIM = D_INNER + 2 * D_STATE
        D_IN_PROJ = 2 * D_INNER + 2 * D_STATE + NHEADS
        EPS = 1e-05

        def _layernorm(x, w, b):
            m = x.mean(-1, keepdims=True)
            v = ((x - m) ** 2).mean(-1, keepdims=True)
            return (x - m) * jax.lax.rsqrt(v + EPS) * w + b

        def _mamba2(u, in_w, conv_w, conv_b, dt_bias, A_log, Dp, rms_w, out_w):
            b, l, _ = u.shape
            zxbcdt = u @ in_w.T
            z, xBC, dt = jnp.split(zxbcdt, [D_INNER, D_INNER + CONV_DIM], axis=-1)
            dt = jax.nn.softplus(dt + dt_bias)
            xBC = jnp.transpose(xBC, (0, 2, 1))
            xBC = jax.lax.conv_general_dilated(xBC, conv_w[:, None, :], (1,), [(D_CONV - 1, 0)], dimension_numbers=('NCH', 'OIH', 'NCH'), feature_group_count=CONV_DIM)
            xBC = jnp.transpose(xBC, (0, 2, 1)) + conv_b
            xBC = jax.nn.silu(xBC)
            xh, Bm, Cm = jnp.split(xBC, [D_INNER, D_INNER + D_STATE], axis=-1)
            xh = xh.reshape(b, l, NHEADS, HEADDIM)
            A = -jnp.exp(A_log)
            dA = jnp.exp(dt * A)

            def step(state, inputs):
                dA_t, dt_t, x_t, B_t, C_t = inputs
                state = dA_t[:, :, None, None] * state + (dt_t[:, :, None] * x_t)[..., None] * B_t[:, None, None, :]
                y_t = jnp.einsum('bhpn,bn->bhp', state, C_t)
                return (state, y_t)
            xs = (jnp.moveaxis(dA, 1, 0), jnp.moveaxis(dt, 1, 0), jnp.moveaxis(xh, 1, 0), jnp.moveaxis(Bm, 1, 0), jnp.moveaxis(Cm, 1, 0))
            init = jnp.zeros((b, NHEADS, HEADDIM, D_STATE), u.dtype)
            _, ys = jax.lax.scan(step, init, xs)
            y = jnp.moveaxis(ys, 0, 1) + Dp[None, None, :, None] * xh
            y = y.reshape(b, l, D_INNER)
            y = y * jax.nn.silu(z)
            y = y * jax.lax.rsqrt(jnp.mean(y * y, -1, keepdims=True) + EPS) * rms_w
            return y @ out_w.T
        h = x
        for i in range(N_LAYERS):
            res = h
            h = _layernorm(h, ln_w[i], ln_b[i])
            h = _mamba2(h, in_proj_w[i], conv_w[i], conv_b[i], dt_bias[i], A_log[i], D[i], rms_w[i], out_proj_w[i])
            h = h + res
        return h

    def _L0_ffn_ref(x, w_up, w_down):
        import jax, jax.numpy as jnp
        import numpy as np
        EPS = 1e-08

        def _ternary_linear(x, w):
            alpha = jnp.mean(jnp.abs(w))
            w_t = jnp.sign(w) * (jnp.abs(w) > 0.5 * alpha).astype(w.dtype)
            w_q = w + jax.lax.stop_gradient(w_t - w)
            d = x.shape[-1]
            rms = jnp.sqrt(jnp.sum(x * x, axis=-1, keepdims=True)) / jnp.sqrt(jnp.asarray(d, x.dtype))
            x_norm = x / (rms + EPS)
            return jnp.einsum('bsd,fd->bsf', x_norm, w_q)
        h = jax.nn.gelu(_ternary_linear(x, w_up), approximate=False)
        return _ternary_linear(h, w_down)

    def _L1_attn_ref(x, Wr, br, Wk, bk, Wv, bv, Wo, bo, time_decay, U):
        import math
        import jax, jax.numpy as jnp
        import numpy as np
        N, T, C = (4, 256, 128)
        H, HS = (16, 64)
        LAYER_ID, N_LAYERS = (1, 12)
        _EPS = math.exp(-LAYER_ID / N_LAYERS)
        EPS_R = _EPS / 2.0
        EPS_K = _EPS + 0.3 * LAYER_ID / (N_LAYERS - 1)
        EPS_V = _EPS

        def _time_interp(x, eps):
            Tn = x.shape[1]
            curr = jnp.pad(x, ((0, 0), (1, 0), (0, 0)))[:, :Tn]
            prev = jnp.pad(x, ((0, 0), (0, 1), (0, 0)))[:, 1:]
            return eps * curr + (1.0 - eps) * prev
        n, t, c = x.shape
        R = (_time_interp(x, EPS_R) @ Wr.T + br).reshape(n, t, H, HS)
        K = (_time_interp(x, EPS_K) @ Wk.T + bk).reshape(n, t, H, HS)
        V = (_time_interp(x, EPS_V) @ Wv.T + bv).reshape(n, t, H, HS)
        w = jax.nn.relu(time_decay).reshape(1, 1, H, HS)
        t_rem = (t - jnp.arange(1, t + 1, dtype=x.dtype)).reshape(1, t, 1, 1)
        W = -w * t_rem
        e = jnp.exp(jnp.clip(W + K, -20.0, 10.0))
        past_attention = jnp.cumsum(e * V, axis=1)
        past_energy = jnp.cumsum(e, axis=1)
        shift = lambda a: jnp.pad(a, ((0, 0), (1, 0), (0, 0), (0, 0)))[:, :t]
        eu = jnp.exp(jnp.clip(U.reshape(1, 1, H, HS) + K, -20.0, 10.0))
        A = shift(past_attention) + eu * V
        B = shift(past_energy) + eu
        WKV = A / B
        out = (jax.nn.sigmoid(R) * WKV).reshape(n, t, -1) @ Wo.T + bo
        return out

    def _L1_ffn_ref(hidden_states, gate_weight, e_bias, gate_proj, up_proj, down_proj):
        import jax, jax.numpy as jnp
        import numpy as np
        TOP_K = 4
        N_GROUP = 4
        TOPK_GROUP = 2
        ROUTED_SCALING = 1.0

        def _route(x_flat, gate_weight, e_bias):
            T = x_flat.shape[0]
            E = gate_weight.shape[0]
            logits = jnp.einsum('th,eh->te', x_flat, gate_weight)
            scores = jax.nn.sigmoid(logits)
            scores_for_choice = scores + e_bias[None, :]
            grp = scores_for_choice.reshape(T, N_GROUP, E // N_GROUP)
            top2, _ = jax.lax.top_k(grp, 2)
            group_scores = top2.sum(axis=-1)
            _, group_idx = jax.lax.top_k(group_scores, TOPK_GROUP)
            group_mask = jax.nn.one_hot(group_idx, N_GROUP, dtype=scores.dtype).sum(axis=1)
            score_mask = jnp.repeat(group_mask, E // N_GROUP, axis=1)
            tmp_scores = jnp.where(score_mask > 0, scores_for_choice, 0.0)
            _, topk_idx = jax.lax.top_k(tmp_scores, TOP_K)
            topk_weight = jnp.take_along_axis(scores, topk_idx, axis=1)
            denom = topk_weight.sum(axis=-1, keepdims=True) + 1e-20
            topk_weight = topk_weight / denom * ROUTED_SCALING
            return (topk_idx, topk_weight)
        B, S, H = hidden_states.shape
        E = gate_proj.shape[0]
        x = hidden_states.reshape(-1, H).astype(jnp.float32)
        topk_idx, topk_weight = _route(x, gate_weight, e_bias)
        combine = (jax.nn.one_hot(topk_idx, E, dtype=x.dtype) * topk_weight[..., None]).sum(axis=1)
        g = jnp.einsum('th,eih->tei', x, gate_proj)
        u = jnp.einsum('th,eih->tei', x, up_proj)
        act = jax.nn.silu(g) * u
        expert_out = jnp.einsum('tei,ehi->teh', act, down_proj)
        y = jnp.einsum('teh,te->th', expert_out, combine)
        return y.reshape(B, S, H)
    x = L0_attn_x
    x = _layernorm(x + _L0_attn_ref(x, L0_attn_ln_w, L0_attn_ln_b, L0_attn_in_proj_w, L0_attn_conv_w, L0_attn_conv_b, L0_attn_dt_bias, L0_attn_A_log, L0_attn_D, L0_attn_rms_w, L0_attn_out_proj_w), axis=-1)
    x = _layernorm(x + _L0_ffn_ref(x, L0_ffn_w_up, L0_ffn_w_down), axis=-1)
    x = _layernorm(x + _L1_attn_ref(x, L1_attn_Wr, L1_attn_br, L1_attn_Wk, L1_attn_bk, L1_attn_Wv, L1_attn_bv, L1_attn_Wo, L1_attn_bo, L1_attn_time_decay, L1_attn_U), axis=-1)
    x = _layernorm(x + _L1_ffn_ref(x, L1_ffn_gate_weight, L1_ffn_e_bias, L1_ffn_gate_proj, L1_ffn_up_proj, L1_ffn_down_proj), axis=-1)
    return x

_drawn_inputs = setup_inputs


def setup_inputs(seed=0):
    import zlib

    import numpy as np

    out = dict(_drawn_inputs(seed))
    spreads = {'L0_attn_ln_w': (1.0, 0.2),
     'L0_attn_ln_b': (0.0, 0.1),
     'L0_attn_conv_b': (0.0, 0.1),
     'L0_attn_D': (1.0, 0.2),
     'L0_attn_rms_w': (1.0, 0.2),
     'L1_attn_time_decay': (0.10000000149011612, 0.6),
     'L1_attn_U': (0.10000000149011612, 0.6),
     'L1_ffn_e_bias': (0.0, 0.8)}
    factors = {'L1_attn_br': 8.0,
     'L1_attn_bk': 8.0,
     'L1_attn_bv': 5.869,
     'L1_attn_bo': 8.0,
     'L1_ffn_gate_weight': 8.0,
     'L1_ffn_gate_proj': 8.0,
     'L1_ffn_up_proj': 8.0,
     'L1_ffn_down_proj': 8.0}
    for name, (base, spread) in spreads.items():
        noise = np.random.default_rng([zlib.crc32(name.encode()), seed]).standard_normal(out[name].shape)
        drawn = base * np.exp(spread * noise) if base else spread * noise
        out[name] = jnp.asarray(drawn.astype(out[name].dtype))
    for name, factor in factors.items():
        out[name] = (out[name] * factor).astype(out[name].dtype)
    return out
```

```python
import math
from contextlib import ExitStack

import numpy as np
import concourse.bass as bass
from concourse import mybir

F32 = mybir.dt.float32
ACT = mybir.ActivationFunctionType
ALU = mybir.AluOpType
AX = mybir.AxisListType

P = 128
D = 128
NB = 2
T = 1024
TT = 512
NT = T // TT
NL = 2
DI = 256
DS = 64
NH = DI // DS
Q = 128
NC = TT // Q
DC = 4
LN_EPS = 1e-5
START = 1
C_LNW, C_LNB, C_CW, C_CB, C_D, C_RW, N_PAR = 0, 1, 2, 14, 17, 19, 21


def tensors(nc, ctx):
    sems = []

    def give_back():
        nc.clear_and_free_semaphores(sems)
        nc.all_engine_barrier()

    ctx.callback(give_back)

    def sb(name, shape, dt=F32):
        return ctx.enter_context(nc.sbuf_tensor(name, shape, dt))

    def ps(name, shape, dt=F32):
        return ctx.enter_context(nc.psum_tensor(name, shape, dt))

    def sem(name):
        sems.append(nc.alloc_semaphore(name=name))
        return sems[-1]

    def start(but=()):
        engines = (nc.vector, nc.scalar, nc.tensor, nc.gpsimd, nc.sync)
        for i, s in enumerate(x for x in sems if not any(x is y for y in but)):
            engines[i % len(engines)].sem_inc(s, START)
        nc.all_engine_barrier()
    sem.start = start
    return sb, ps, sem


def mamba(nc, X, H, cst, x_dram, win_d, wout_d, par_d, row_d, c_dram, later=(), s_later=None):
    with ExitStack() as ctx:
        sb, ps, sem = tensors(nc, ctx)
        tri, low, ones, ident, mean_w, rms_w = cst
        win = sb("m_win", [P, 2 * DI + 2 * DS + NH])
        wout = sb("m_wout", [P, 2, D])
        par = sb("m_par", [P, N_PAR])
        row = sb("m_row", [P, 2, NH])
        arow = sb("m_arow", [P, NH])
        eps = sb("m_eps", [P, 1])
        two = lambda name, shape: [sb(f"m_{name}{b}", shape) for b in range(NB)]
        xc, sq, rstd, u = two("xc", [P, TT]), two("sq", [P, TT]), two("rstd", [P, TT]), two("u", [P, TT])
        pre = two("pre", [P, 3, DC - 1 + TT])
        acc = two("acc", [P, 3, TT])
        xs, bt, ct, zs = two("xs", [P, 2, TT]), two("bt", [DS, TT]), two("ct", [DS, TT]), two("zs", [P, 2, TT])
        raw, neg, l1p = two("raw", [P, NC, NH]), two("neg", [P, NC, NH]), two("l1p", [P, NC, NH])
        dt, a, decay, ddt = two("dt", [P, NC, NH]), two("a", [P, NC, NH]), two("decay", [P, 3, NC, NH]), two("ddt", [P, NC, NH])
        state, faded = two("state", [DS, NH, DS]), two("faded", [DS, NH, DS])
        y, sq2, o = two("y", [P, 2, TT]), two("sq2", [P, 2, TT]), two("o", [P, TT])
        par2 = lambda name, shape: [sb(f"m_{name}{k}", shape) for k in range(2)]
        steps, L, gm, mt = par2("steps", [P, NH, Q]), par2("L", [P, NH, Q]), par2("gm", [P, Q]), par2("mt", [P, NH, Q])
        xdt, xdec, btok = par2("xdt", [P, NH, DS]), par2("xdec", [P, NH, DS]), par2("btok", [P, DS])
        yo, yt = par2("yo", [P, NH, DS]), par2("yt", [P, NH * DS])

        pa = [ps(f"m_pa{k}", [P, TT]) for k in range(2)]
        p_small = ps("m_psmall", [P, 512])
        p_diff = ps("m_pdiff", [P, NH, Q])
        p_gt = ps("m_pgt", [P, 512])
        p_y = ps("m_py", [P, 2, NH, DS])
        p_ds = ps("m_pds", [P, 512])
        p_yt = ps("m_pyt", [P, 2, 2, Q])
        p_dt = p_small[:, 0:NC * NH]
        p_cum = p_small[:, 16:16 + 3 * NC * NH]
        p_g = p_gt[:, 0:Q]
        p_xtok = p_gt[:, Q:Q + NH * DS]
        p_btok = p_gt[:, Q + NH * DS:Q + NH * DS + DS]

        ORDER = [(n, b) for part in (("mean", "var", "x0", "x1", "bc"), ("z0", "z1"), ("ms", "out"))
                 for b in range(NB) for n in part]
        SLOT = {k: n for n, k in enumerate(ORDER)}
        PER_BANK = len(ORDER) // 2

        s_const, s_x, s_w, s_eps = sem("m_s_const"), sem("m_s_x"), sem("m_s_w"), sem("m_s_eps")
        s_prep, s_aexp = sem("m_s_prep"), sem("m_s_aexp")
        pa_full, pa_free = [sem(f"m_pa_full{k}") for k in range(2)], [sem(f"m_pa_free{k}") for k in range(2)]
        each = lambda name: [sem(f"m_{name}{b}") for b in range(NB)]
        xc_ready, sq_ready, lnv_ready, rstd_ready, u1_ready, u_ready = map(each, ("xc_r", "sq_r", "lnv_r", "rstd_r", "u1_r", "u_r"))
        pre_ready, conv_step, silu_done, zs_ready = map(each, ("pre_r", "conv_s", "silu_d", "zs_r"))
        halo_ready = each("halo_r")
        dt_full, raw_ready, neg_ready, e_ready, l1p_ready, dt_ready, a_ready = map(
            each, ("dt_f", "raw_r", "neg_r", "e_r", "l1p_r", "dt_r", "a_r"))
        cum_full, decay_ready, ddt_ready = map(each, ("cum_f", "decay_r", "ddt_r"))
        state_ready = each("state_r")
        y_ready, sq2_ready, lnm_ready, rstd2_ready, o_ready, h_ready = map(
            each, ("y_r", "sq2_r", "lnm_r", "rstd2_r", "o_r", "h_r"))
        steps_ready, diff_full, L_ready, gt_full, gt_free, gm_ready, mt_ready = map(
            sem, ("m_steps_r", "m_diff_f", "m_L_r", "m_gt_f", "m_gt_free", "m_gm_r", "m_mt_r"))
        y_full, ds_full, faded_ready, yo_ready, yt_ready, pyt_full, pyt_free = map(
            sem, ("m_y_f", "m_ds_f", "m_faded_r", "m_yo_r", "m_yt_r", "m_pyt_f", "m_pyt_free"))
        CH = NB * NC

        def bank(name, b):
            n = SLOT[(name, b)]
            return pa[n % 2], pa_full[n % 2], pa_free[n % 2], n // 2

        def heads(x):
            return x.unsqueeze(2).broadcast_to([x.shape[0], NH, DS])

        sem.start(but=(s_const, s_x, s_w))
        block = ctx.enter_context(nc.Block())

        @block.sync
        def _(sp):
            for dst, src in c_dram:
                sp.dma_start(dst, src).then_inc(s_const, 16)
            sp.dma_start(H[:, :, :], x_dram).then_inc(s_x, 16)
            sp.dma_start(X[:, :, :], x_dram).then_inc(s_x, 16)
            with sp.Fori(0, NL) as l:
                for b in range(NB):
                    sp.wait_ge(h_ready[b], START + l * NT)
                for dst, src in ((win[:, :], win_d), (wout[:, :, :], wout_d), (par[:, :], par_d), (row[:, :, :], row_d)):
                    idx = (bass.ds(l, 1),) + (slice(None),) * (len(src.shape) - 1)
                    s = src[idx]
                    pat = "a p n -> (a p) n" if len(src.shape) == 3 else "a p k n -> (a p) k n"
                    sp.dma_start(dst, s.rearrange(pat)).then_inc(s_w, 16)

        @block.gpsimd
        def _(pool):
            for dst, src in later:
                pool.dma_start(dst, src).then_inc(s_later, 16)
            nc.gpsimd.memset(eps[:, :], LN_EPS).then_inc(s_eps, 1)
            pool.wait_ge(s_const, 16 * len(c_dram))
            with pool.Fori(0, NL) as l, pool.Fori(0, NT) as t:
                it = l * NT + t
                for b in range(NB):
                    for c in range(NC):
                        i = b * NC + c
                        pool.wait_ge(a_ready[b], START + it + 1)
                        pool.wait_ge(diff_full, START + it * CH + max(i - 1, 0))
                        nc.gpsimd.tensor_tensor(steps[i % 2][:, :, :], a[b][:, c, :].unsqueeze(2).broadcast_to([P, NH, Q]),
                                                tri[:, :].unsqueeze(1).broadcast_to([P, NH, Q]), ALU.mult).then_inc(steps_ready, 1)

        @block.tensor
        def _(pe):
            mm = nc.tensor.matmul

            def into(name, b, it):
                p, full, free, k = bank(name, b)
                pe.wait_ge(free, START + it * PER_BANK + k)
                return p[:, :], full

            def project(b, it, name, lo, hi):
                p, full = into(name, b, it)
                mm(p, win[:, lo:hi], u[b][:, :], start=True, stop=True).then_inc(full, 1)

            def front(b, l, t, it):
                pe.wait_ge(h_ready[b], START + it)
                p, full = into("mean", b, it)
                mm(p, mean_w[:, :], H[:, b, bass.ds(t * TT, TT)], start=True, stop=True).then_inc(full, 1)
                p, full = into("var", b, it)
                pe.wait_ge(sq_ready[b], START + it + 1)
                mm(p, mean_w[:, :], sq[b][:, :], start=True, stop=True).then_inc(full, 1)
                pe.wait_ge(u_ready[b], START + it + 1)
                pe.wait_ge(s_w, 64 * (l + 1))
                pe.wait_ge(decay_ready[1 - b], START + it + b)
                for c in range(NC):
                    last = mm(p_dt[:, c * NH:(c + 1) * NH], u[b][:, c * Q:(c + 1) * Q], win[:, 2 * DI + 2 * DS:],
                              start=True, stop=True)
                last.then_inc(dt_full[b], 1)
                project(b, it, "x0", DI, DI + P)
                project(b, it, "x1", DI + P, 2 * DI)
                project(b, it, "bc", 2 * DI, 2 * DI + 2 * DS)
                pe.wait_ge(a_ready[b], START + it + 1)
                for k, m in enumerate((tri, low, ones)):
                    last = mm(p_cum[:, k * NC * NH:(k + 1) * NC * NH], m[:, :], a[b][:, :, :].rearrange("p c h -> p (c h)"),
                              start=True, stop=True)
                last.then_inc(cum_full[b], 1)

            def gates(b, it):
                project(b, it, "z0", 0, P)
                project(b, it, "z1", P, DI)

            def chunk_front(b, c, it):
                i, q = b * NC + c, slice(c * Q, (c + 1) * Q)
                pe.wait_ge(gt_free, START + it * CH + i)
                if c == 0:
                    pe.wait_ge(silu_done[b], START + it + 1)
                mm(p_g, bt[b][:, q], ct[b][:, q], start=True, stop=True)
                for k in range(2):
                    nc.tensor.transpose(p_xtok[:, k * P:(k + 1) * P], xs[b][:, k, q], ident[:, :])
                nc.tensor.transpose(p_btok, bt[b][:, q], ident[0:DS, 0:DS]).then_inc(gt_full, 1)
                pe.wait_ge(steps_ready, START + it * CH + i + 1)
                pe.wait_ge(L_ready, START + it * CH + i)
                mm(p_diff[:, :, :], low[:, :], steps[i % 2][:, :, :], start=True, stop=True).then_inc(diff_full, 1)

            def chunk_back(b, c, it):
                i, q = b * NC + c, slice(c * Q, (c + 1) * Q)
                pe.wait_ge(gt_free, START + it * CH + i + 1)
                pe.wait_ge(yt_ready, START + it * CH + i)
                pe.wait_ge(state_ready[b], START + it * NC + l_off[0] + c)
                mm(p_y[:, 1, :, :], ct[b][:, q], state[b][:, :, :], start=True, stop=True)
                pe.wait_ge(mt_ready, START + it * CH + i + 1)
                for h in range(NH):
                    last = mm(p_y[:, 0, h, :], mt[i % 2][:, h, :], xdt[i % 2][:, h, :], start=True, stop=True)
                last.then_inc(y_full, 1)
                mm(p_ds[0:DS, 0:NH * DS], btok[i % 2][:, :], xdec[i % 2][:, :, :], start=True, stop=True).then_inc(ds_full, 1)

            def turn(b, c, it):
                i = b * NC + c
                pe.wait_ge(yt_ready, START + it * CH + i + 1)
                if c % 2 == 0:
                    pe.wait_ge(pyt_free, START + it * CH // 2 + i // 2)
                for k in range(2):
                    last = nc.tensor.transpose(p_yt[:, k, c % 2, :], yt[i % 2][:, k * P:(k + 1) * P], ident[:, :])
                last.then_inc(pyt_full, 1)

            def back(b, it):
                p, full = into("ms", b, it)
                pe.wait_ge(sq2_ready[b], START + it + 1)
                for k in range(2):
                    last = mm(p, rms_w[:, :], sq2[b][:, k, :], start=(k == 0), stop=(k == 1))
                last.then_inc(full, 1)
                p, full = into("out", b, it)
                for k in range(2):
                    last = mm(p, wout[:, k, :], y[b][:, k, :], start=(k == 0), stop=(k == 1))
                last.then_inc(full, 1)

            pe.wait_ge(s_const, 16 * len(c_dram))
            pe.wait_ge(s_x, 32)
            l_off = [0]
            with pe.Fori(0, NL) as l, pe.Fori(0, NT) as t:
                it = l * NT + t
                l_off[0] = l + 1
                for b in range(NB):
                    front(b, l, t, it)
                for b in range(NB):
                    gates(b, it)
                for b in range(NB):
                    chunk_front(b, 0, it)
                    for c in range(NC):
                        if c + 1 < NC:
                            chunk_front(b, c + 1, it)
                        if c:
                            turn(b, c - 1, it)
                        chunk_back(b, c, it)
                    turn(b, NC - 1, it)
                    if b == 0:
                        pe.wait_ge(s_prep, START + 3 * (l + 1))
                    back(b, it)

        @block.scalar
        def _(act):
            f = nc.scalar.activation

            def front(b, it):
                act.wait_ge(xc_ready[b], START + it + 1)
                f(sq[b][:, :], xc[b][:, :], ACT.Square).then_inc(sq_ready[b], 1)
                p, full, free, k = bank("var", b)
                act.wait_ge(full, START + it * PER_BANK + k + 1)
                f(rstd[b][:, :], p[:, :], ACT.Ln, bias=eps[:, :]).then_inc(free, 1)
                act.wait_ge(free, START + it * PER_BANK + k + 1)
                f(rstd[b][:, :], rstd[b][:, :], ACT.Exp, scale=-0.5).then_inc(rstd_ready[b], 1)

            def softplus(b, it):
                act.wait_ge(neg_ready[b], START + it + 1)
                f(l1p[b][:, :, :], neg[b][:, :, :], ACT.Exp).then_inc(e_ready[b], 1)
                act.wait_ge(e_ready[b], START + it + 1)
                f(l1p[b][:, :, :], l1p[b][:, :, :], ACT.Ln, bias=1.0).then_inc(l1p_ready[b], 1)

            def leave(b, it):
                act.wait_ge(halo_ready[b], START + it)
                act.wait_ge(silu_done[b], START + it)
                for k, name in enumerate(("x0", "x1", "bc")):
                    p, full, free, n = bank(name, b)
                    act.wait_ge(full, START + it * PER_BANK + n + 1)
                    f(pre[b][:, k, DC - 1:], p[:, :], ACT.Copy)
                    f(acc[b][:, k, :], p[:, :], ACT.Identity, scale=par[:, C_CW + 4 * k + 3:C_CW + 4 * k + 4],
                      bias=par[:, C_CB + k:C_CB + k + 1]).then_inc(free, 1)

            def silus(b, it):
                act.wait_ge(h_ready[b], START + it)
                for k in range(2):
                    p, full, free, n = bank(f"z{k}", b)
                    act.wait_ge(full, START + it * PER_BANK + n + 1)
                    f(zs[b][:, k, :], p[:, :], ACT.Silu).then_inc(free, 1)
                for k in range(3):
                    act.wait_ge(conv_step[b], START + it * 9 + 7 + k)
                    if k < 2:
                        f(xs[b][:, k, :], acc[b][:, k, :], ACT.Silu)
                    else:
                        f(bt[b][:, :], acc[b][0:DS, k, :], ACT.Silu)
                        f(ct[b][:, :], acc[b][DS:, k, :], ACT.Silu).then_inc(silu_done[b], 1)

            def decays(b, it):
                act.wait_ge(cum_full[b], START + it + 1)
                f(decay[b][:, :, :, :].rearrange("p k c h -> p (k c h)"), p_cum, ACT.Exp).then_inc(decay_ready[b], 1)

            def chunk(b, c, it):
                i = b * NC + c
                act.wait_ge(diff_full, START + it * CH + i + 1)
                act.wait_ge(mt_ready, START + it * CH + max(i - 1, 0))
                f(L[i % 2][:, :, :], p_diff[:, :, :], ACT.Exp).then_inc(L_ready, 1)

            def back(b, it):
                act.wait_ge(y_ready[b], START + it + 1)
                f(sq2[b][:, :, :], y[b][:, :, :], ACT.Square).then_inc(sq2_ready[b], 1)
                p, full, free, k = bank("ms", b)
                act.wait_ge(full, START + it * PER_BANK + k + 1)
                f(rstd[b][:, :], p[:, :], ACT.Ln, bias=eps[:, :]).then_inc(free, 1)
                act.wait_ge(free, START + it * PER_BANK + k + 1)
                f(rstd[b][:, :], rstd[b][:, :], ACT.Exp, scale=-0.5).then_inc(rstd2_ready[b], 1)

            act.wait_ge(s_eps, START + 1)
            with act.Fori(0, NL) as l:
                act.preload_act_table_set("natural_log_exp_and_others")
                act.wait_ge(s_w, 64 * (l + 1))
                f(arow[:, :], row[:, 1, :], ACT.Exp).then_inc(s_aexp, 1)
                with act.Fori(0, NT) as t:
                    it = l * NT + t
                    act.preload_act_table_set("natural_log_exp_and_others")
                    for b in range(NB):
                        front(b, it)
                        softplus(b, it)
                        leave(b, it)
                        decays(b, it)
                    for b in range(NB):
                        silus(b, it)
                    act.preload_act_table_set("natural_log_exp_and_others")
                    for b in range(NB):
                        for c in range(NC):
                            chunk(b, c, it)
                        back(b, it)

        @block.vector
        def _(dve):
            v = nc.vector
            conv = [0]

            def front(b, t, it):
                if b == 0:
                    pass
                dve.wait_ge(h_ready[b], START + it)
                p, full, free, k = bank("mean", b)
                dve.wait_ge(full, START + it * PER_BANK + k + 1)
                v.tensor_tensor(xc[b][:, :], H[:, b, bass.ds(t * TT, TT)], p[:, :], ALU.subtract).then_inc(free, 1)
                dve.wait_ge(free, START + it * PER_BANK + k + 1)
                v.tensor_scalar(u[b][:, :], xc[b][:, :], par[:, C_LNW:C_LNW + 1], None, ALU.mult).then_inc(xc_ready[b], 1)
                dve.wait_ge(rstd_ready[b], START + it + 1)
                dve.wait_ge(xc_ready[b], START + it + 1)
                v.tensor_tensor(u[b][:, :], u[b][:, :], rstd[b][:, :], ALU.mult).then_inc(u1_ready[b], 1)
                dve.wait_ge(u1_ready[b], START + it + 1)
                v.tensor_scalar(u[b][:, :], u[b][:, :], par[:, C_LNB:C_LNB + 1], None, ALU.add).then_inc(u_ready[b], 1)

            def softplus_in(b, it):
                dve.wait_ge(dt_full[b], START + it + 1)
                v.tensor_tensor(raw[b][:, :, :], p_dt.rearrange("p (c h) -> p c h", h=NH),
                                row[:, 0, :].unsqueeze(1).broadcast_to([P, NC, NH]), ALU.add).then_inc(raw_ready[b], 1)
                dve.wait_ge(raw_ready[b], START + it + 1)
                v.scalar_tensor_tensor(neg[b][:, :, :], raw[b][:, :, :], -1.0, raw[b][:, :, :], ALU.mult, ALU.min).then_inc(neg_ready[b], 1)

            def softplus_out(b, it):
                dve.wait_ge(l1p_ready[b], START + it + 1)
                v.scalar_tensor_tensor(dt[b][:, :, :], raw[b][:, :, :], 0.0, l1p[b][:, :, :], ALU.max, ALU.add)\
                    .then_inc(dt_ready[b], 1)
                dve.wait_ge(dt_ready[b], START + it + 1)
                v.tensor_tensor(a[b][:, :, :], dt[b][:, :, :], arow[:, :].unsqueeze(1).broadcast_to([P, NC, NH]), ALU.mult)\
                    .then_inc(a_ready[b], 1)

            def convolve(b, l, it):
                dve.wait_ge(halo_ready[b], START + it)
                dve.wait_ge(state_ready[b], START + it * NC + l + 1)
                for k in range(DC - 1):
                    for j, name in enumerate(("x0", "x1", "bc")):
                        _, _, free, n = bank(name, b)
                        if k == 0:
                            dve.wait_ge(free, START + it * PER_BANK + n + 1)
                        else:
                            dve.wait_ge(conv_step[b], START + it * 9 + (k - 1) * 3 + j + 1)
                        w = par[:, C_CW + 4 * j + k:C_CW + 4 * j + k + 1]
                        v.scalar_tensor_tensor(acc[b][:, j, :], pre[b][:, j, k:k + TT], w, acc[b][:, j, :], ALU.mult, ALU.add)\
                            .then_inc(conv_step[b], 1)
                dve.wait_ge(conv_step[b], START + it * 9 + 9)
                v.tensor_copy(pre[b][:, :, 0:DC - 1], pre[b][:, :, TT:]).then_inc(halo_ready[b], 1)

            def decays(b, it):
                dve.wait_ge(decay_ready[b], START + it + 1)
                v.tensor_tensor(ddt[b][:, :, :], decay[b][:, 1, :, :], dt[b][:, :, :], ALU.mult).then_inc(ddt_ready[b], 1)

            def chunk_front(b, c, it):
                i = b * NC + c
                dve.wait_ge(gt_full, START + it * CH + i + 1)
                dve.wait_ge(ddt_ready[b], START + it + 1)
                dve.wait_ge(ds_full, START + it * CH + max(i - 1, 0))
                k = i % 2
                v.tensor_tensor(gm[k][:, :], p_g, tri[:, :], ALU.mult).then_inc(gm_ready, 1)
                x3 = p_xtok.rearrange("p (h n) -> p h n", h=NH)
                v.tensor_tensor(xdt[k][:, :, :], x3, heads(dt[b][:, c, :]), ALU.mult)
                v.tensor_tensor(xdec[k][:, :, :], x3, heads(ddt[b][:, c, :]), ALU.mult)
                v.tensor_copy(btok[k][:, :], p_btok).then_inc(gt_free, 1)
                dve.wait_ge(gt_free, START + it * CH + i + 1)
                dve.wait_ge(gm_ready, START + it * CH + i + 1)
                dve.wait_ge(L_ready, START + it * CH + i + 1)
                v.tensor_tensor(mt[k][:, :, :], gm[k][:, :].unsqueeze(1).broadcast_to([P, NH, Q]), L[k][:, :, :], ALU.mult)\
                    .then_inc(mt_ready, 1)

            def chunk_back(b, c, l, it):
                i, k = b * NC + c, (b * NC + c) % 2
                dve.wait_ge(state_ready[b], START + it * NC + l + 1 + c)
                v.tensor_tensor(faded[b][:, :, :], state[b][:, :, :], heads(decay[b][0:DS, 2, c, :]), ALU.mult)\
                    .then_inc(faded_ready, 1)
                dve.wait_ge(y_full, START + it * CH + i + 1)
                v.tensor_tensor(yo[k][:, :, :], p_y[:, 1, :, :], heads(decay[b][:, 0, c, :]), ALU.mult).then_inc(yo_ready, 1)
                dve.wait_ge(faded_ready, START + it * CH + i + 1)
                dve.wait_ge(ds_full, START + it * CH + i + 1)
                v.tensor_tensor(state[b][:, :, :], faded[b][:, :, :], p_ds[0:DS, 0:NH * DS].rearrange("p (h n) -> p h n", h=NH), ALU.add)\
                    .then_inc(state_ready[b], 1)
                dve.wait_ge(yo_ready, START + it * CH + i + 1)
                dve.wait_ge(pyt_full, START + it * CH + max(i - 1, 0))
                v.tensor_tensor(yt[k][:, :], yo[k][:, :, :].rearrange("p h n -> p (h n)"),
                                p_y[:, 0, :, :].rearrange("p h n -> p (h n)"), ALU.add).then_inc(yt_ready, 1)

            def skip(b, j, it):
                dve.wait_ge(pyt_full, START + it * CH + b * NC + 2 * j + 2)
                q = slice(j * 2 * Q, (j + 1) * 2 * Q)
                for k in range(2):
                    last = v.scalar_tensor_tensor(y[b][:, k, q], xs[b][:, k, q], par[:, C_D + k:C_D + k + 1],
                                                  p_yt[:, k, :, :].rearrange("p c q -> p (c q)"), ALU.mult, ALU.add)
                last.then_inc(pyt_free, 1)

            def back(b, t, it):
                dve.wait_ge(pyt_free, START + it * CH // 2 + 2 * b + 2)
                v.tensor_tensor(y[b][:, :, :], y[b][:, :, :], zs[b][:, :, :], ALU.mult).then_inc(y_ready[b], 1)
                p, full, free, k = bank("out", b)
                dve.wait_ge(full, START + it * PER_BANK + k + 1)
                dve.wait_ge(rstd2_ready[b], START + it + 1)
                v.tensor_tensor(o[b][:, :], p[:, :], rstd[b][:, :], ALU.mult).then_inc(free, 1)
                dve.wait_ge(free, START + it * PER_BANK + k + 1)
                h = H[:, b, bass.ds(t * TT, TT)]
                v.tensor_tensor(h, h, o[b][:, :], ALU.add).then_inc(h_ready[b], 1)

            with dve.Fori(0, NL) as l:
                dve.wait_ge(s_w, 64 * (l + 1))
                for b in range(NB):
                    dve.wait_ge(halo_ready[b], START + l * NT)
                    v.memset(pre[b][:, :, 0:DC - 1], 0.0)
                    dve.wait_ge(state_ready[b], START + l * (NT * NC + 1))
                    v.memset(state[b][:, :, :], 0.0).then_inc(state_ready[b], 1)
                for k in range(2):
                    v.tensor_scalar(wout[:, k, :], wout[:, k, :], par[:, C_RW + k:C_RW + k + 1], None, ALU.mult).then_inc(s_prep, 1)
                dve.wait_ge(s_aexp, START + l + 1)
                v.tensor_scalar(arow[:, :], arow[:, :], -1.0, None, ALU.mult).then_inc(s_prep, 1)
                with dve.Fori(0, NT) as t:
                    it = l * NT + t
                    dve.wait_ge(s_prep, START + 3 * (l + 1))
                    for b in range(NB):
                        front(b, t, it)
                        softplus_in(b, it)
                        softplus_out(b, it)
                        convolve(b, l, it)
                        decays(b, it)
                    for b in range(NB):
                        chunk_front(b, 0, it)
                        for c in range(NC):
                            if c + 1 < NC:
                                chunk_front(b, c + 1, it)
                            if c == 2:
                                skip(b, 0, it)
                            chunk_back(b, c, l, it)
                        skip(b, 1, it)
                        back(b, t, it)


class Banks:

    def __init__(self, nc, ps, sem, prefix, order, n):
        self.per, self.slot, self.bank = [0] * n, {}, []
        for k in range(n):
            self.bank.append((ps(f"{prefix}_bank{k}", [P, 512]), sem(f"{prefix}_full{k}"), sem(f"{prefix}_free{k}")))
        for i, name in enumerate(order):
            self.slot[name] = (i % n, self.per[i % n])
            self.per[i % n] += 1

    def before(self, name, it):
        k, i = self.slot[name]
        bank, _, free = self.bank[k]
        return bank, free, it * self.per[k] + i

    def full(self, name, it):
        k, i = self.slot[name]
        bank, full, _ = self.bank[k]
        return bank, full, it * self.per[k] + i + 1

    def read(self, name, it):
        k, i = self.slot[name]
        return self.bank[k][2], START + it * self.per[k] + i + 1

    def sem_full(self, name):
        return self.bank[self.slot[name][0]][1]

    def sem_free(self, name):
        return self.bank[self.slot[name][0]][2]


def ffn(nc, X, H, XP, cst, wts):
    tri, low, ones, ident, mean_w, rms_w = cst
    up, down, s_weights, n_weights = wts
    FB = 512 // P
    with ExitStack() as ctx:
        sb, ps, sem = tensors(nc, ctx)
        two = lambda name, shape: [sb(f"f_{name}{b}", shape) for b in range(NB)]
        s, sq, r, xn = two("s", [P, TT]), two("sq", [P, TT]), two("r", [P, TT]), two("xn", [P, TT])
        hid, hsq, o = two("hid", [P, FB, TT]), two("hsq", [P, FB, TT]), two("o", [P, TT])
        asum, thr, nthr = sb("f_asum", [P, 2]), sb("f_thr", [P, 2]), sb("f_nthr", [P, 2])
        mneg = sb("f_mneg", [P, 2, 512])
        eps, tiny, guard = sb("f_eps", [P, 1]), sb("f_tiny", [P, 1]), sb("f_guard", [P, 1])
        STAGES = ["mean", "var", "ms", "up0", "up1", "up2", "up3", "ms2", "down", "mean2", "var2"]
        order = [(n, b) for n in STAGES for b in range(NB)]
        K = Banks(nc, ps, sem, "f", order, 8)
        each = lambda name: [sem(f"f_{name}{b}") for b in range(NB)]
        s_eps, s_asum, s_alpha, s_thr, s_neg, s_tern = map(sem, ("f_eps_r", "f_asum_r", "f_alpha", "f_thr_r", "f_neg_r", "f_tern"))
        s1_ready, sq_ready, rstd_ready, x1_ready, sq1_ready, xn_ready = map(
            each, ("s1", "sqr", "rstd", "x1", "sq1", "xnr"))
        rms_ready, lrms_ready, r_ready = map(each, ("rms", "lrms", "rr"))
        hsq_ready, s2_ready, sq2_ready, rstd2_ready, x2_ready = map(each, ("hsq_r", "s2", "sq2", "rstd2", "x2"))
        sem.start()
        block = ctx.enter_context(nc.Block())

        @block.gpsimd
        def _(pool):
            nc.gpsimd.memset(XP[:, :, :], 0.0)
            nc.gpsimd.memset(eps[:, :], LN_EPS)
            nc.gpsimd.memset(tiny[:, :], 1e-19)
            nc.gpsimd.memset(guard[:, :], 1e-8).then_inc(s_eps, 1)
            with pool.Fori(0, NT) as t:
                for b in range(NB):
                    for j in range(FB):
                        pool.wait_ge(*K.read((f"up{j}", b), t))
                        nc.gpsimd.tensor_tensor(hsq[b][:, j, :], hid[b][:, j, :], hid[b][:, j, :], ALU.mult)\
                            .then_inc(hsq_ready[b], 1)

        @block.tensor
        def _(pe):
            mm = nc.tensor.matmul

            def product(name, b, it, terms):
                bank, free, n = K.before((name, b), it)
                pe.wait_ge(free, START + n)
                for i, (w, x) in enumerate(terms):
                    last = mm(bank[:, :], w, x, start=(i == 0), stop=(i == len(terms) - 1))
                last.then_inc(K.sem_full((name, b)), 1)

            pe.wait_ge(s_weights, n_weights)
            pe.wait_ge(s_asum, START + 2)
            bank = K.bank[7][0]
            mm(bank[:, 0:2], ones[:, :], asum[:, :], start=True, stop=True).then_inc(s_alpha, 1)
            pe.wait_ge(s_thr, START + 1)
            with pe.Fori(0, NT) as t:
                for b in range(NB):
                    pe.wait_ge(s1_ready[b], START + t + 1)
                    product("mean", b, t, [(mean_w[:, :], s[b][:, :])])
                for b in range(NB):
                    pe.wait_ge(sq_ready[b], START + t + 1)
                    product("var", b, t, [(mean_w[:, :], sq[b][:, :])])
                for b in range(NB):
                    pe.wait_ge(sq1_ready[b], START + t + 1)
                    product("ms", b, t, [(mean_w[:, :], sq[b][:, :])])
                for j in range(FB):
                    for b in range(NB):
                        if j == 0:
                            pe.wait_ge(xn_ready[b], START + t + 1)
                            if b == 0:
                                pe.wait_ge(s_tern, START + 2)
                        product(f"up{j}", b, t, [(up[:, j * P:(j + 1) * P], xn[b][:, :])])
                for b in range(NB):
                    pe.wait_ge(hsq_ready[b], START + (t + 1) * FB)
                    product("ms2", b, t, [(rms_w[:, :], hsq[b][:, j, :]) for j in range(FB)])
                for b in range(NB):
                    pe.wait_ge(hsq_ready[b], START + (t + 1) * FB)
                    product("down", b, t, [(down[:, j, :], hid[b][:, j, :]) for j in range(FB)])
                for b in range(NB):
                    pe.wait_ge(s2_ready[b], START + t + 1)
                    product("mean2", b, t, [(mean_w[:, :], s[b][:, :])])
                for b in range(NB):
                    pe.wait_ge(sq2_ready[b], START + t + 1)
                    product("var2", b, t, [(mean_w[:, :], sq[b][:, :])])

        @block.scalar
        def _(act):
            f = nc.scalar.activation

            def rstd(name, b, it, done):
                bank, full, n = K.full((name, b), it)
                act.wait_ge(full, START + n)
                f(r[b][:, :], bank[:, :], ACT.Ln, bias=eps[:, :]).then_inc(K.sem_free((name, b)), 1)
                act.wait_ge(K.sem_free((name, b)), START + n)
                f(r[b][:, :], r[b][:, :], ACT.Exp, scale=-0.5).then_inc(done[b], 1)

            def one_over_rms(name, b, it, scale, k):
                bank, full, n = K.full((name, b), it)
                act.wait_ge(full, START + n)
                f(r[b][:, :], bank[:, :], ACT.Ln, bias=tiny[:, :], scale=scale).then_inc(K.sem_free((name, b)), 1)
                act.wait_ge(K.sem_free((name, b)), START + n)
                f(r[b][:, :], r[b][:, :], ACT.Exp, scale=0.5).then_inc(rms_ready[b], 1)
                act.wait_ge(rms_ready[b], START + 2 * it + k + 1)
                f(r[b][:, :], r[b][:, :], ACT.Ln, bias=guard[:, :]).then_inc(lrms_ready[b], 1)
                act.wait_ge(lrms_ready[b], START + 2 * it + k + 1)
                f(r[b][:, :], r[b][:, :], ACT.Exp, scale=-1.0).then_inc(r_ready[b], 1)

            act.preload_act_table_set("natural_log_exp_and_others")
            act.wait_ge(s_eps, START + 1)
            with act.Fori(0, NT) as t:
                act.preload_act_table_set("natural_log_exp_and_others")
                for b in range(NB):
                    act.wait_ge(*K.read(("mean", b), t))
                    f(sq[b][:, :], s[b][:, :], ACT.Square).then_inc(sq_ready[b], 1)
                for b in range(NB):
                    rstd("var", b, t, rstd_ready)
                for b in range(NB):
                    act.wait_ge(x1_ready[b], START + t + 1)
                    f(sq[b][:, :], X[:, b, bass.ds(t * TT, TT)], ACT.Square).then_inc(sq1_ready[b], 1)
                for b in range(NB):
                    one_over_rms("ms", b, t, 1.0, 0)
                for j in range(FB):
                    for b in range(NB):
                        bank, full, n = K.full((f"up{j}", b), t)
                        if j == 0:
                            act.wait_ge(x2_ready[b], START + t)
                        act.wait_ge(full, START + n)
                        f(hid[b][:, j, :], bank[:, :], ACT.Gelu).then_inc(K.sem_free((f"up{j}", b)), 1)
                act.preload_act_table_set("natural_log_exp_and_others")
                for b in range(NB):
                    one_over_rms("ms2", b, t, 0.5, 1)
                for b in range(NB):
                    act.wait_ge(*K.read(("mean2", b), t))
                    f(sq[b][:, :], s[b][:, :], ACT.Square).then_inc(sq2_ready[b], 1)
                for b in range(NB):
                    rstd("var2", b, t, rstd2_ready)

        @block.vector
        def _(dve):
            v = nc.vector

            def centre(name, b, it):
                bank, full, n = K.full((name, b), it)
                dve.wait_ge(full, START + n)
                v.tensor_tensor(s[b][:, :], s[b][:, :], bank[:, :], ALU.subtract).then_inc(K.sem_free((name, b)), 1)

            dve.wait_ge(s_weights, n_weights)
            for k, w in enumerate((up[:, :], down[:, :, :].rearrange("p k n -> p (k n)"))):
                v.tensor_reduce(asum[:, k:k + 1], w, AX.X, ALU.add, apply_absolute_value=True).then_inc(s_asum, 1)
            dve.wait_ge(s_alpha, START + 1)
            bank = K.bank[7][0]
            v.tensor_scalar(thr[:, :], bank[:, 0:2], 0.5 / (D * 512), None, ALU.mult)
            v.tensor_scalar(nthr[:, :], bank[:, 0:2], -0.5 / (D * 512), None, ALU.mult).then_inc(s_thr, 1)
            dve.wait_ge(s_thr, START + 1)
            for k, w in enumerate((up[:, :], down[:, :, :].rearrange("p k n -> p (k n)"))):
                v.tensor_scalar(mneg[:, k, :], w, nthr[:, k:k + 1], None, ALU.is_lt).then_inc(s_neg, 1)
                dve.wait_ge(s_neg, START + k + 1)
                v.scalar_tensor_tensor(w, w, thr[:, k:k + 1], mneg[:, k, :], ALU.is_gt, ALU.subtract).then_inc(s_tern, 1)
            dve.wait_ge(s_eps, START + 1)
            with dve.Fori(0, NT) as t:
                tile = lambda b: X[:, b, bass.ds(t * TT, TT)]
                for b in range(NB):
                    dve.wait_ge(x2_ready[b], START + t)
                    v.tensor_tensor(s[b][:, :], tile(b), H[:, b, bass.ds(t * TT, TT)], ALU.add).then_inc(s1_ready[b], 1)
                for b in range(NB):
                    centre("mean", b, t)
                for b in range(NB):
                    dve.wait_ge(rstd_ready[b], START + t + 1)
                    v.tensor_tensor(tile(b), s[b][:, :], r[b][:, :], ALU.mult).then_inc(x1_ready[b], 1)
                for b in range(NB):
                    dve.wait_ge(r_ready[b], START + 2 * t + 1)
                    v.tensor_tensor(xn[b][:, :], tile(b), r[b][:, :], ALU.mult).then_inc(xn_ready[b], 1)
                for b in range(NB):
                    bank, full, n = K.full(("down", b), t)
                    dve.wait_ge(full, START + n)
                    dve.wait_ge(r_ready[b], START + 2 * t + 2)
                    v.tensor_tensor(o[b][:, :], bank[:, :], r[b][:, :], ALU.mult).then_inc(K.sem_free(("down", b)), 1)
                    dve.wait_ge(K.sem_free(("down", b)), START + n)
                    v.tensor_tensor(s[b][:, :], o[b][:, :], tile(b), ALU.add).then_inc(s2_ready[b], 1)
                for b in range(NB):
                    centre("mean2", b, t)
                for b in range(NB):
                    dve.wait_ge(rstd2_ready[b], START + t + 1)
                    v.tensor_tensor(XP[:, b, bass.ds(t * TT + 1, TT)], s[b][:, :], r[b][:, :], ALU.mult).then_inc(x2_ready[b], 1)


EPS = math.exp(-1 / 12)
EPS_RKV = (EPS / 2, EPS + 0.3 / 11, EPS)
NF = 8
E_LO, E_HI = float(np.exp(np.float32(-20))), float(np.exp(np.float32(10)))
BIG = 2.0 ** 39


def wkv(nc, X, XP, cst, wts):
    tri, low, ones, ident, mean_w, rms_w = cst
    wr, wk, wv, wo, decay, t_rem, par, bo, s_weights, n_weights = wts
    U_, BK, BR, BV = range(4)
    with ExitStack() as ctx:
        sb, ps, sem = tensors(nc, ctx)
        mix = sb("w_mix", [P, 3, TT])
        tmp = sb("w_tmp", [P, 3, TT])
        t_now = sb("w_t_now", [2, TT])
        ubk, nbr = sb("w_ubk", [P, NF]), sb("w_nbr", [P, NF])
        eps, onec = sb("w_eps", [P, 1]), sb("w_one", [P, 1])
        par2 = lambda name, shape: [sb(f"w_{name}{k}", shape) for k in range(2)]
        V, er, G = par2("V", [P, TT]), par2("er", [P, TT]), par2("G", [P, 4, TT])
        AB, dn, O = par2("AB", [P, 2, TT]), par2("dn", [P, TT]), par2("O", [P, TT])
        CS = sb("w_CS", [P, NF, 2, 1 + TT])
        s, sq, r = sb("w_s", [P, TT]), sb("w_sq", [P, TT]), sb("w_r", [P, TT])
        pk = [ps(f"w_pk{k}", [P, TT]) for k in range(2)]
        pv = [ps(f"w_pv{k}", [P, TT]) for k in range(2)]
        pr = [ps(f"w_pr{k}", [P, TT]) for k in range(2)]
        pacc, pst = ps("w_pacc", [P, TT]), ps("w_pst", [P, TT])
        (s_eps, s_prep, mix1, mix_ready, k_full, k_read, kw_full, kw_read, v_full, v_read, r_full, er_read, clip_ready, er1_ready,
         ev_ready, cs_ready, ab_ready, dn_ready, ln_ready, rd_ready, o_ready, o_used, acc_full, s_ready, mean_full, xc_ready,
         sq_ready, var_full, lv_ready, rstd_ready, x3_ready, halo, clear) = [sem(f"w_s{i}_{n}") for i, n in enumerate(
             "eps prep mix1 mix k_full k_read kw_full kw_read v_full v_read r_full er clip er1 ev cs ab dn ln rd o o_used "
             "acc s mean xc sq var lv rstd x3 halo clear".split())]
        sem.start()
        block = ctx.enter_context(nc.Block())

        @block.gpsimd
        def _(pool):
            nc.gpsimd.memset(eps[:, :], LN_EPS)
            nc.gpsimd.memset(onec[:, :], 1.0).then_inc(s_eps, 1)
            with pool.Fori(0, NB) as b, pool.Fori(0, NT) as t:
                it = b * NT + t
                for f in range(NF):
                    k, n = f % 2, it * NF + f
                    pool.wait_ge(cs_ready, START + n + 1)
                    pool.wait_ge(o_ready, START + it * NF + max(f - 1, 0))
                    nc.gpsimd.tensor_tensor(AB[k][:, :, :], CS[:, f, :, 0:TT], G[k][:, 2:4, :], ALU.add)\
                        .then_inc(ab_ready, 1)
                    pool.wait_ge(ab_ready, START + n + 1)
                    pool.wait_ge(er1_ready, START + n + 1)
                    nc.gpsimd.tensor_tensor(dn[k][:, :], AB[k][:, 1, :], er[k][:, :], ALU.mult).then_inc(dn_ready, 1)

        @block.tensor
        def _(pe):
            mm = nc.tensor.matmul

            def project(f, t, it):
                k, n, fs = f % 2, it * NF + f, slice(f * P, (f + 1) * P)
                prev = it * NF + max(f - 1, 0)
                pe.wait_ge(kw_read, START + prev)
                mm(pk[k][:, :], wk[:, fs], mix[:, 1, :], start=True, stop=True).then_inc(k_full, 1)
                pe.wait_ge(v_read, START + prev)
                mm(pv[k][:, :], wv[:, fs], mix[:, 2, :], start=True, stop=True).then_inc(v_full, 1)
                pe.wait_ge(er_read, START + prev)
                mm(pr[k][:, :], wr[:, fs], mix[:, 0, :], start=True, stop=True).then_inc(r_full, 1)
                pe.wait_ge(k_read, START + n + 1)
                mm(pk[k][:, :], decay[:, fs], t_now[:, :], start=False, stop=True,
                   skip_group_check=True).then_inc(kw_full, 1)

            def collect(f, it):
                pe.wait_ge(o_ready, START + it * NF + f + 1)
                if f == 0:
                    pe.wait_ge(s_ready, START + it)
                mm(pacc[:, :], wo[:, f, :], O[f % 2][:, :], start=(f == 0), stop=(f == NF - 1)).then_inc(o_used, 1)

            pe.wait_ge(s_weights, n_weights)
            pe.wait_ge(s_prep, START + 1)
            with pe.Fori(0, NB) as b, pe.Fori(0, NT) as t:
                it = b * NT + t
                pe.wait_ge(mix_ready, START + it + 1)
                project(0, t, it)
                for f in range(NF):
                    if f + 1 < NF:
                        project(f + 1, t, it)
                    if f:
                        collect(f - 1, it)
                collect(NF - 1, it)
                pe.wait_ge(s_ready, START + it + 1)
                pe.wait_ge(lv_ready, START + it)
                mm(pst[:, :], mean_w[:, :], s[:, :], start=True, stop=True).then_inc(mean_full, 1)
                pe.wait_ge(sq_ready, START + it + 1)
                mm(pst[:, :], mean_w[:, :], sq[:, :], start=True, stop=True).then_inc(var_full, 1)

        @block.scalar
        def _(act):
            a = nc.scalar.activation

            def front(f, it):
                k, n = f % 2, it * NF + f
                act.wait_ge(k_full, START + n + 1)
                act.wait_ge(ab_ready, START + it * NF + max(f - 1, 0))
                a(G[k][:, 3, :], pk[k][:, :], ACT.Exp, bias=ubk[:, f:f + 1]).then_inc(k_read, 1)
                act.wait_ge(v_full, START + n + 1)
                a(V[k][:, :], pv[k][:, :], ACT.Identity, bias=par[:, f, BV:BV + 1]).then_inc(v_read, 1)
                act.wait_ge(kw_full, START + n + 1)
                a(G[k][:, 1, :], pk[k][:, :], ACT.Exp).then_inc(kw_read, 1)
                act.wait_ge(r_full, START + n + 1)
                act.wait_ge(dn_ready, START + it * NF + max(f - 1, 0))
                a(er[k][:, :], pr[k][:, :], ACT.Exp, scale=-1.0, bias=nbr[:, f:f + 1]).then_inc(er_read, 1)

            def back(f, it):
                k, n = f % 2, it * NF + f
                act.wait_ge(dn_ready, START + n + 1)
                a(dn[k][:, :], dn[k][:, :], ACT.Ln).then_inc(ln_ready, 1)
                act.wait_ge(ln_ready, START + n + 1)
                a(dn[k][:, :], dn[k][:, :], ACT.Exp, scale=-1.0).then_inc(rd_ready, 1)

            act.preload_act_table_set("natural_log_exp_and_others")
            act.wait_ge(s_eps, START + 1)
            act.wait_ge(s_prep, START + 1)
            with act.Fori(0, NB) as b, act.Fori(0, NT) as t:
                it = b * NT + t
                for f in range(NF + 1):
                    if f < NF:
                        front(f, it)
                    if f:
                        back(f - 1, it)
                act.wait_ge(xc_ready, START + it + 1)
                a(sq[:, :], s[:, :], ACT.Square).then_inc(sq_ready, 1)
                act.wait_ge(var_full, START + it + 1)
                a(r[:, :], pst[:, :], ACT.Ln, bias=eps[:, :]).then_inc(lv_ready, 1)
                act.wait_ge(lv_ready, START + it + 1)
                a(r[:, :], r[:, :], ACT.Exp, scale=-0.5).then_inc(rstd_ready, 1)

        @block.vector
        def _(dve):
            v = nc.vector

            def front(f, it):
                k, n = f % 2, it * NF + f
                dve.wait_ge(kw_read, START + n + 1)
                v.tensor_scalar(G[k][:, 1::2, :], G[k][:, 1::2, :], E_LO, E_HI, ALU.max, ALU.min).then_inc(clip_ready, 1)
                dve.wait_ge(er_read, START + n + 1)
                v.tensor_scalar(er[k][:, :], er[k][:, :], BIG, 1.0, ALU.min, ALU.add).then_inc(er1_ready, 1)
                dve.wait_ge(clip_ready, START + n + 1)
                dve.wait_ge(v_read, START + n + 1)
                v.tensor_tensor(G[k][:, 0::2, :], G[k][:, 1::2, :], V[k][:, :].unsqueeze(1).broadcast_to([P, 2, TT]), ALU.mult)\
                    .then_inc(ev_ready, 1)
                dve.wait_ge(ab_ready, START + it * NF)
                v.tensor_copy(CS[:, f, :, 0:1], CS[:, f, :, TT:]).then_inc(halo, 1)
                dve.wait_ge(halo, START + n + 1)
                dve.wait_ge(ev_ready, START + n + 1)
                for j in range(2):
                    last = v.tensor_tensor_scan(CS[:, f, j, 1:], onec[:, :].broadcast_to([P, TT]), G[k][:, j, :],
                                                CS[:, f, j, 0:1], ALU.mult, ALU.add)
                last.then_inc(cs_ready, 1)

            def back(f, it):
                k, n = f % 2, it * NF + f
                dve.wait_ge(rd_ready, START + n + 1)
                dve.wait_ge(o_used, START + it * NF + max(f - 1, 0))
                v.tensor_tensor(O[k][:, :], AB[k][:, 0, :], dn[k][:, :], ALU.mult).then_inc(o_ready, 1)

            dve.wait_ge(s_weights, n_weights)
            v.tensor_scalar(decay[0:1, :], decay[0:1, :], 0.0, -1.0, ALU.max, ALU.mult)
            v.tensor_tensor(ubk[:, :], par[:, :, U_], par[:, :, BK], ALU.add)
            v.tensor_scalar(nbr[:, :], par[:, :, BR], -1.0, None, ALU.mult).then_inc(s_prep, 1)
            dve.wait_ge(s_eps, START + 1)
            with dve.Fori(0, NB) as b:
                dve.wait_ge(cs_ready, START + b * NT * NF)
                v.memset(CS[:, :, :, TT:], 0.0).then_inc(clear, 1)
                with dve.Fori(0, NT) as t:
                    it = b * NT + t
                    dve.wait_ge(x3_ready, START + it)
                    tile = lambda o: XP[:, b, bass.ds(t * TT + o, TT)]
                    v.tensor_copy(t_now[:, :], t_rem[:, bass.ds(t * TT, TT)])
                    for j, e in enumerate(EPS_RKV):
                        v.tensor_scalar(tmp[:, j, :], tile(0), e, None, ALU.mult).then_inc(mix1, 1)
                    for j, e in enumerate(EPS_RKV):
                        dve.wait_ge(mix1, START + it * 3 + j + 1)
                        last = v.scalar_tensor_tensor(mix[:, j, :], tile(2), 1.0 - e, tmp[:, j, :], ALU.mult, ALU.add)
                    last.then_inc(mix_ready, 1)
                    dve.wait_ge(clear, START + b + 1)
                    for f in range(NF + 1):
                        if f < NF:
                            front(f, it)
                        if f:
                            back(f - 1, it)
                    dve.wait_ge(o_used, START + (it + 1) * NF)
                    v.scalar_tensor_tensor(s[:, :], pacc[:, :], bo[:, :], tile(1), ALU.add, ALU.add).then_inc(s_ready, 1)
                    dve.wait_ge(mean_full, START + it + 1)
                    v.tensor_tensor(s[:, :], s[:, :], pst[:, :], ALU.subtract).then_inc(xc_ready, 1)
                    dve.wait_ge(rstd_ready, START + it + 1)
                    v.tensor_tensor(X[:, b, bass.ds(t * TT, TT)], s[:, :], r[:, :], ALU.mult).then_inc(x3_ready, 1)


NE, NG, I = 16, 4, 64
NPR = NE * I // P
GE = NE // NG
TOP_K, TOP_G = 4, 2


def moe(nc, X, OUT, cst, wts, out_dram):
    tri, low, ones, ident, mean_w, rms_w = cst
    gw, ebias, gp, up, dp, sel, below, s_weights, n_weights = wts
    with ExitStack() as ctx:
        sb, ps, sem = tensors(nc, ctx)
        eps = sb("e_eps", [P, 1])
        logit, comb_t = sb("e_logit", [NE, TT]), [sb(f"e_comb_t{k}", [NE, TT]) for k in range(2)]
        tok = lambda name, *n: sb(f"e_{name}", [P, NC, *n])
        ex, sc, sfc = tok("ex", NE), tok("sc", NE), tok("sfc", NE)
        mx, mn = tok("mx", NE // 2), tok("mn", NE // 2)
        t1, t2, t3, gs = tok("t1", NG), tok("t2", NG), tok("t3", NG), tok("gs", NG)
        ggt, geq, gcnt, masked = tok("ggt", NG, NG), tok("geq", NG, NG), tok("gcnt", NG), tok("masked", NE)
        egt, eeq, ecnt = tok("egt", NE, NE), tok("eeq", NE, NE), tok("ecnt", NE)
        w, den, rden, comb = tok("w", NE), tok("den"), tok("rden"), tok("comb", NE)
        par2 = lambda name, shape: [sb(f"e_{name}{k}", shape) for k in range(2)]
        sg, gu, act_ = par2("sg", [P, TT]), par2("gu", [P, TT]), par2("act", [P, TT])
        s, sq, r = sb("e_s", [P, TT]), sb("e_sq", [P, TT]), sb("e_r", [P, TT])
        pg = [ps(f"e_pg{k}", [P, TT]) for k in range(2)]
        pu = [ps(f"e_pu{k}", [P, TT]) for k in range(2)]
        pc = [ps(f"e_pc{k}", [P, TT]) for k in range(2)]
        py, pm = ps("e_py", [P, TT]), ps("e_pm", [P, TT])
        (s_eps, chain, lg_full, lg_ready, lt_full, ex_ready, comb_ready, ct_full, ct_ready, g_full, g_read, u_full, c_full,
         u_read, c_read, y_step, s_ready, mean_full, xc_ready, sq_ready, var_full, lv_ready, rstd_ready, out_ready, s_out) = [
             sem(f"e_s{i}_{n}") for i, n in enumerate(
                 "eps chain lg_f lg lt_f ex comb ct_f ct g_f g_r u_f c_f u_r c_r y s mean xc sq var lv rstd out store".split())]
        NTILE = NB * NT
        sem.start(but=(s_out,))
        block = ctx.enter_context(nc.Block())
        flat = lambda x: x[:, :, :].rearrange("p b t -> p (b t)")

        @block.sync
        def _(sp):
            with sp.Fori(0, NTILE) as it:
                sp.wait_ge(out_ready, START + it + 1)
                sp.dma_start(out_dram[:, bass.ds(it * TT, TT)], flat(OUT)[:, bass.ds(it * TT, TT)]).then_inc(s_out, 16)
            sp.wait_ge(s_out, 16 * NTILE)

        @block.gpsimd
        def _(pool):
            nc.gpsimd.memset(eps[:, :], LN_EPS).then_inc(s_eps, 1)

        @block.tensor
        def _(pe):
            mm = nc.tensor.matmul

            def expert(j, it):
                k, n = j % 2, it * NPR + j
                x = flat(X)[:, bass.ds(it * TT, TT)]
                prev = it * NPR + max(j - 1, 0)
                pe.wait_ge(g_read, START + prev)
                mm(pg[k][:, :], gp[:, j * P:(j + 1) * P], x, start=True, stop=True).then_inc(g_full, 1)
                pe.wait_ge(u_read, START + prev)
                mm(pu[k][:, :], up[:, j * P:(j + 1) * P], x, start=True, stop=True).then_inc(u_full, 1)
                if j == 0:
                    pe.wait_ge(ct_ready, START + it + 1)
                pe.wait_ge(c_read, START + prev)
                mm(pc[k][:, :], sel[:, j * P:(j + 1) * P], comb_t[0][:, :], start=True, stop=True).then_inc(c_full, 1)

            def collect(j, it):
                pe.wait_ge(c_read, START + it * NPR + j + 1)
                if j == 0:
                    pe.wait_ge(s_ready, START + it)
                mm(py[:, :], dp[:, j, :], act_[j % 2][:, :], start=(j == 0), stop=(j == NPR - 1)).then_inc(y_step, 1)

            pe.wait_ge(s_weights, n_weights)
            with pe.Fori(0, NTILE) as it:
                pe.wait_ge(lv_ready, START + it)
                mm(pm[0:NE, :], gw[:, :], flat(X)[:, bass.ds(it * TT, TT)], start=True, stop=True).then_inc(lg_full, 1)
                pe.wait_ge(lg_ready, START + it + 1)
                for c in range(NC):
                    last = mm(pm[:, c * NE:(c + 1) * NE], logit[:, c * Q:(c + 1) * Q], ident[0:NE, 0:NE], start=True, stop=True)
                last.then_inc(lt_full, 1)
                pe.wait_ge(comb_ready, START + it + 1)
                for c in range(NC):
                    last = nc.tensor.transpose(pm[0:NE, c * Q:(c + 1) * Q], comb[:, c, :], ident[:, :])
                last.then_inc(ct_full, 1)
                expert(0, it)
                for j in range(NPR):
                    if j + 1 < NPR:
                        expert(j + 1, it)
                    collect(j, it)
                pe.wait_ge(s_ready, START + it + 1)
                mm(pm[:, :], mean_w[:, :], s[:, :], start=True, stop=True).then_inc(mean_full, 1)
                pe.wait_ge(sq_ready, START + it + 1)
                mm(pm[:, :], mean_w[:, :], sq[:, :], start=True, stop=True).then_inc(var_full, 1)

        @block.scalar
        def _(act):
            a = nc.scalar.activation
            act.preload_act_table_set("natural_log_exp_and_others")
            act.wait_ge(s_eps, START + 1)
            with act.Fori(0, NTILE) as it:
                act.preload_act_table_set("natural_log_exp_and_others")
                act.wait_ge(lg_full, START + it + 1)
                a(logit[:, :], pm[0:NE, :], ACT.Copy).then_inc(lg_ready, 1)
                act.wait_ge(lt_full, START + it + 1)
                a(ex[:, :, :].rearrange("p c e -> p (c e)"), pm[:, 0:NC * NE], ACT.Exp, scale=-1.0).then_inc(ex_ready, 1)
                act.wait_ge(ct_full, START + it + 1)
                a(comb_t[0][:, :], pm[0:NE, :], ACT.Copy).then_inc(ct_ready, 1)
                for j in range(NPR):
                    k, n = j % 2, it * NPR + j
                    act.wait_ge(g_full, START + n + 1)
                    act.wait_ge(u_read, START + it * NPR + max(j - 1, 0))
                    a(sg[k][:, :], pg[k][:, :], ACT.Silu).then_inc(g_read, 1)
                act.preload_act_table_set("natural_log_exp_and_others")
                act.wait_ge(xc_ready, START + it + 1)
                a(sq[:, :], s[:, :], ACT.Square).then_inc(sq_ready, 1)
                act.wait_ge(var_full, START + it + 1)
                a(r[:, :], pm[:, :], ACT.Ln, bias=eps[:, :]).then_inc(lv_ready, 1)
                act.wait_ge(lv_ready, START + it + 1)
                a(r[:, :], r[:, :], ACT.Exp, scale=-0.5).then_inc(rstd_ready, 1)

        @block.vector
        def _(dve):
            v = nc.vector
            STEPS = 27

            def route(it):
                n = [0]

                def step(ins):
                    n[0] += 1
                    ins.then_inc(chain, 1)
                    dve.wait_ge(chain, START + it * STEPS + n[0])

                dve.wait_ge(ex_ready, START + it + 1)
                step(v.tensor_scalar(ex[:, :, :], ex[:, :, :], 1.0, None, ALU.add))
                step(v.reciprocal(sc[:, :, :], ex[:, :, :]))
                step(v.tensor_tensor(sfc[:, :, :], sc[:, :, :], ebias[:, :].unsqueeze(1).broadcast_to([P, NC, NE]), ALU.add))
                pairs = sfc[:, :, :].rearrange("p c (n two) -> p c n two", two=2)
                step(v.tensor_tensor(mx[:, :, :], pairs[:, :, :, 0], pairs[:, :, :, 1], ALU.max))
                step(v.tensor_tensor(mn[:, :, :], pairs[:, :, :, 0], pairs[:, :, :, 1], ALU.min))
                hi = mx[:, :, :].rearrange("p c (g two) -> p c g two", two=2)
                lo = mn[:, :, :].rearrange("p c (g two) -> p c g two", two=2)
                step(v.tensor_tensor(t1[:, :, :], hi[:, :, :, 0], hi[:, :, :, 1], ALU.max))
                step(v.tensor_tensor(t2[:, :, :], hi[:, :, :, 0], hi[:, :, :, 1], ALU.min))
                step(v.tensor_tensor(t3[:, :, :], lo[:, :, :, 0], lo[:, :, :, 1], ALU.max))
                step(v.tensor_tensor(t2[:, :, :], t2[:, :, :], t3[:, :, :], ALU.max))
                step(v.tensor_tensor(gs[:, :, :], t1[:, :, :], t2[:, :, :], ALU.add))

                def rank(x, m, gt, eq, cnt):
                    other = x.unsqueeze(2).broadcast_to([P, NC, m, m])
                    own = x.unsqueeze(3).broadcast_to([P, NC, m, m])
                    step(v.tensor_tensor(eq[:, :, :, :], other, own, ALU.is_equal))
                    step(v.tensor_tensor(gt[:, :, :, :], other, own, ALU.is_gt))
                    step(v.tensor_tensor(eq[:, :, :, :], eq[:, :, :, :], below[:, 0:m, 0:m].unsqueeze(1).broadcast_to([P, NC, m, m]), ALU.mult))
                    step(v.tensor_tensor(gt[:, :, :, :], gt[:, :, :, :], eq[:, :, :, :], ALU.add))
                    step(v.tensor_reduce(cnt[:, :, :], gt[:, :, :, :], AX.X, ALU.add))

                rank(gs[:, :, :], NG, ggt, geq, gcnt)
                step(v.tensor_scalar(gcnt[:, :, :], gcnt[:, :, :], TOP_G - 0.5, None, ALU.is_lt))
                step(v.tensor_tensor(masked[:, :, :].rearrange("p c (g e) -> p c g e", g=NG), sfc[:, :, :].rearrange("p c (g e) -> p c g e", g=NG),
                                     gcnt[:, :, :].unsqueeze(3).broadcast_to([P, NC, NG, GE]), ALU.mult))
                rank(masked[:, :, :], NE, egt, eeq, ecnt)
                step(v.tensor_scalar(ecnt[:, :, :], ecnt[:, :, :], TOP_K - 0.5, None, ALU.is_lt))
                step(v.tensor_tensor(w[:, :, :], sc[:, :, :], ecnt[:, :, :], ALU.mult))
                step(v.tensor_reduce(den[:, :], w[:, :, :], AX.X, ALU.add))
                step(v.tensor_scalar(den[:, :], den[:, :], 1e-20, None, ALU.add))
                step(v.reciprocal(rden[:, :], den[:, :]))
                assert n[0] == STEPS, n[0]
                dve.wait_ge(ct_full, START + it)
                v.tensor_tensor(comb[:, :, :], w[:, :, :], rden[:, :].unsqueeze(2).broadcast_to([P, NC, NE]), ALU.mult).then_inc(comb_ready, 1)

            dve.wait_ge(s_weights, n_weights)
            with dve.Fori(0, NTILE) as it:
                route(it)
                for j in range(NPR):
                    k, n = j % 2, it * NPR + j
                    dve.wait_ge(g_read, START + n + 1)
                    dve.wait_ge(u_full, START + n + 1)
                    v.tensor_tensor(gu[k][:, :], sg[k][:, :], pu[k][:, :], ALU.mult).then_inc(u_read, 1)
                    dve.wait_ge(u_read, START + n + 1)
                    dve.wait_ge(c_full, START + n + 1)
                    dve.wait_ge(y_step, START + it * NPR + max(j - 1, 0))
                    v.tensor_tensor(act_[k][:, :], gu[k][:, :], pc[k][:, :], ALU.mult).then_inc(c_read, 1)
                dve.wait_ge(y_step, START + (it + 1) * NPR)
                v.tensor_tensor(s[:, :], py[:, :], flat(X)[:, bass.ds(it * TT, TT)], ALU.add).then_inc(s_ready, 1)
                dve.wait_ge(mean_full, START + it + 1)
                v.tensor_tensor(s[:, :], s[:, :], pm[:, :], ALU.subtract).then_inc(xc_ready, 1)
                dve.wait_ge(rstd_ready, START + it + 1)
                v.tensor_tensor(flat(OUT)[:, bass.ds(it * TT, TT)], s[:, :], r[:, :], ALU.mult).then_inc(out_ready, 1)


def constants():
    i = np.arange(P)
    le, gt = i[:, None] <= i[None, :], i[:, None] > i[None, :]
    parts = [le, gt, np.ones((P, P)), np.eye(P), np.full((P, P), 1 / D), np.full((P, P), 1 / DI)]
    return np.stack(parts, 1).astype(np.float32)


def program(nc, d):
    with ExitStack() as ctx:
        sb = lambda name, shape: ctx.enter_context(nc.sbuf_tensor(name, shape, F32))
        X, H, XP = sb("X", [P, NB, T]), sb("H", [P, NB, T]), sb("XP", [P, NB, T + 2])
        C = sb("C", [P, 6, P])
        cst = tuple(C[:, k, :] for k in range(6))
        names = ["f_up", "f_down", "wr", "wk", "wv", "wo", "decay", "t_rem", "w_par", "bo", "gw", "ebias", "gp", "eup", "dp", "sel", "below"]
        W = {n: sb("W_" + n, list(d[n].shape)) for n in names}
        s_weights = ctx.enter_context(nc.semaphore("s_weights"))
        n_weights = 16 * len(names)
        full = lambda x: x[tuple(slice(None) for _ in x.shape)]

        mamba(nc, X, H, cst, d["x"], d["win"], d["wout"], d["par"], d["row"], [(C[:, :, :], d["cst"])],
              [(full(W[n]), d[n]) for n in names], s_weights)
        ffn(nc, X, H, XP, cst, (W["f_up"], W["f_down"], s_weights, n_weights))
        wkv(nc, X, XP, cst, tuple(W[n] for n in ("wr", "wk", "wv", "wo", "decay", "t_rem", "w_par", "bo")) + (s_weights, n_weights))
        moe(nc, X, H, cst, tuple(W[n] for n in ("gw", "ebias", "gp", "eup", "dp", "sel", "below")) + (s_weights, n_weights), d["out"])


def kernel(**inputs):
    from concourse import bacc
    from concourse.bass_utils import run_bass_kernel_spmd

    z = {k: np.asarray(v) for k, v in inputs.items()}
    f = np.ascontiguousarray
    feat = lambda x: f(x.reshape(-1, P).T)
    blocks = lambda w: f(w.T.reshape(-1, P, w.shape[0]).transpose(1, 0, 2))
    per = lambda x: x.reshape(NL, -1, P).transpose(0, 2, 1)
    arrays = {
        "x": feat(z["L0_attn_x"]).reshape(P, NB, T),
        "win": f(z["L0_attn_in_proj_w"].transpose(0, 2, 1)),
        "wout": f(z["L0_attn_out_proj_w"].transpose(0, 2, 1).reshape(NL, 2, P, D).transpose(0, 2, 1, 3)),
        "par": f(np.concatenate([
            per(z["L0_attn_ln_w"]), per(z["L0_attn_ln_b"]),
            z["L0_attn_conv_w"].reshape(NL, 3, P, DC).transpose(0, 2, 1, 3).reshape(NL, P, 3 * DC),
            per(z["L0_attn_conv_b"]), per(np.repeat(z["L0_attn_D"], DS, axis=1)), per(z["L0_attn_rms_w"])], 2)),
        "row": f(np.broadcast_to(np.stack([z["L0_attn_dt_bias"], z["L0_attn_A_log"]], 1)[:, None], (NL, P, 2, NH))),
        "cst": constants(),
        "f_up": f(z["L0_ffn_w_up"].T), "f_down": blocks(z["L0_ffn_w_down"]),
        "wr": f(z["L1_attn_Wr"].T), "wk": f(z["L1_attn_Wk"].T), "wv": f(z["L1_attn_Wv"].T), "wo": blocks(z["L1_attn_Wo"]),
        "decay": f(np.stack([z["L1_attn_time_decay"], z["L1_attn_bk"]])),
        "t_rem": np.stack([T - 1 - np.arange(T), np.ones(T)]).astype(np.float32),
        "w_par": f(np.stack([z["L1_attn_U"], z["L1_attn_bk"], z["L1_attn_br"], z["L1_attn_bv"]], -1).reshape(NF, P, 4).transpose(1, 0, 2)),
        "bo": f(z["L1_attn_bo"][:, None]),
        "gw": f(z["L1_ffn_gate_weight"].T), "ebias": f(np.broadcast_to(z["L1_ffn_e_bias"], (P, NE))),
        "gp": f(z["L1_ffn_gate_proj"].reshape(NE * I, D).T), "eup": f(z["L1_ffn_up_proj"].reshape(NE * I, D).T),
        "dp": f(z["L1_ffn_down_proj"].transpose(0, 2, 1).reshape(NPR, P, D).transpose(1, 0, 2)),
        "sel": f(np.repeat(np.eye(NE), I, axis=1).astype(np.float32)),
        "below": f(np.broadcast_to(np.arange(NE)[:, None] > np.arange(NE)[None, :], (P, NE, NE)).astype(np.float32)),
    }
    nc = bacc.Bacc("TRN2", target_bir_lowering=False, num_devices=1)
    d = {n: nc.dram_tensor(f"in_{n}", a.shape, mybir.dt.from_np(a.dtype), kind="ExternalInput").ap() for n, a in arrays.items()}
    d["out"] = nc.dram_tensor("out_y", (P, NB * T), F32, kind="ExternalOutput").ap()
    program(nc, d)
    r = run_bass_kernel_spmd(nc, [{f"in_{n}": a for n, a in arrays.items()}], core_ids=[0])
    y = np.asarray(r.results[0]["out_y"])
    return f(y.T.reshape(NB, T, D))
```

```python
import math
from contextlib import ExitStack

import numpy as np
import concourse.bass as bass
from concourse import mybir

F32 = mybir.dt.float32
F32R = mybir.dt.float32r
ACT = mybir.ActivationFunctionType
ALU = mybir.AluOpType
AX = mybir.AxisListType

P = 128
D = 128
NB = 2
T = 1024
TT = 512
NT = T // TT
NL = 2
DI = 256
DS = 64
NH = DI // DS
Q = 128
NC = TT // Q
DC = 4
LN_EPS = 1e-5
START = 1
N_IT = NL * NT
C_LNW, C_LNB, C_CW, C_CB, C_D, C_RW, N_PAR = 0, 1, 2, 14, 17, 19, 21


def tensors(nc, ctx):
    sems = []

    def give_back():
        nc.clear_and_free_semaphores(sems)
        nc.all_engine_barrier()

    ctx.callback(give_back)

    def sb(name, shape, dt=F32):
        return ctx.enter_context(nc.sbuf_tensor(name, shape, dt))

    def ps(name, shape, dt=F32):
        return ctx.enter_context(nc.psum_tensor(name, shape, dt))

    def sem(name):
        sems.append(nc.alloc_semaphore(name=name))
        return sems[-1]

    def start(but=()):
        engines = (nc.vector, nc.scalar, nc.tensor, nc.gpsimd, nc.sync)
        for i, s in enumerate(x for x in sems if not any(x is y for y in but)):
            engines[i % len(engines)].sem_inc(s, START)
        nc.all_engine_barrier()
    sem.start = start
    return sb, ps, sem


def lag(n, k):
    return max(n - k, 0) if isinstance(n, int) else n - k


def mamba(nc, XH, cst, x_dram, win_d, wout_d, par_d, row_d, again_d, c_dram, later=(), s_later=None):
    with ExitStack() as ctx:
        sb, ps, sem = tensors(nc, ctx)
        tri, low, ones, ident, mean_w, rms_w = cst
        low_r = sb("m_low_r", [P, P], F32R)
        win = sb("m_win", [P, 2 * DI + 2 * DS + NH])
        wout_in, wout = sb("m_wout_in", [P, 2, D]), sb("m_wout", [P, 2, D])
        par = sb("m_par", [P, N_IT, N_PAR])
        row = sb("m_row", [P, 2, N_IT, NH])
        arow = sb("m_arow", [P, N_IT, NH])
        again = sb("m_again", [P, N_IT + 1])
        eps = sb("m_eps", [P, 1])
        xc, sq, rstd, u = sb("m_xc", [P, TT]), sb("m_sq", [P, TT]), sb("m_rstd", [P, TT]), sb("m_u", [P, TT])
        acc = sb("m_acc", [P, 3, TT])
        raw, neg, l1p = sb("m_raw", [P, NC, NH]), sb("m_neg", [P, NC, NH]), sb("m_l1p", [P, NC, NH])
        two = lambda name, shape, dt=F32: [sb(f"m_{name}{b}", shape, dt) for b in range(NB)]
        pre = two("pre", [P, 3, DC - 1 + TT])
        xs, bt, ct, zs = two("xs", [P, 2, TT]), two("bt", [DS, TT]), two("ct", [DS, TT]), two("zs", [P, 2, TT])
        dt, a, decay, ddt = two("dt", [P, NC, NH]), two("a", [P, NC, NH]), two("decay", [P, 3, NC, NH]), two("ddt", [P, NC, NH])
        a_hi, a_lo = two("a_hi", [P, NC, NH], F32R), two("a_lo", [P, NC, NH], F32R)
        state, y = two("state", [DS, NH, DS]), two("y", [P, 2, TT])
        sq2, rstd2, o = sb("m_sq2", [P, 2, TT]), sb("m_rstd2", [P, TT]), sb("m_o", [P, TT])
        par2 = lambda name, shape, dt=F32: [sb(f"m_{name}{k}", shape, dt) for k in range(2)]
        st_hi, st_lo = par2("st_hi", [P, NH, Q], F32R), par2("st_lo", [P, NH, Q], F32R)
        L, gm, mt = par2("L", [P, NH, Q]), par2("gm", [P, Q]), par2("mt", [P, NH, Q])
        xdt, xdec, btok = par2("xdt", [P, NH, DS]), par2("xdec", [P, NH, DS]), par2("btok", [P, DS])
        yo, yt = par2("yo", [P, NH, DS]), par2("yt", [P, NH * DS])
        faded = sb("m_faded", [DS, NH, DS])

        bank = [ps(f"m_bank{k}", [P, TT]) for k in range(3)]
        p_diff = ps("m_pdiff", [P, NH, Q])
        p_gt = ps("m_pgt", [P, 512])
        p_y = ps("m_py", [P, 2, NH, DS])
        p_ds = ps("m_pds", [DS, NH * DS])
        p_yt = ps("m_pyt", [P, 2, 2, Q])
        p_g = p_gt[:, 0:Q]
        p_xtok = p_gt[:, Q:Q + NH * DS]
        p_btok = p_gt[:, Q + NH * DS:Q + NH * DS + DS]
        BANK = dict(mean=0, var=1, dt=2, x1=0, bc=1, x0=2, sums=0, z0=2, ms=0, out=1, z1=0)
        place = {n: bank[k][:, :] for n, k in BANK.items()}
        p_dt, p_sums = bank[BANK["dt"]][:, 0:NC * NH], bank[BANK["sums"]][:, 0:3 * NC * NH]
        PARTS = (("x1", DI + P, 1), ("bc", 2 * DI, 2), ("x0", DI, 0))

        s_const, s_x, s_par, s_win, s_wout, s_eps, s_arow, s_prep, s_low = (sem("m_s_" + n) for n in (
            "const", "x", "par", "win", "wout", "eps", "arow", "prep", "low"))
        (mean_full, xc_ready, sq_ready, var_full, lnv_ready, rstd_ready, u1_ready, u_ready, dt_full, raw_ready, neg_ready,
         e_ready, l1p_ready, dt_ready, a_ready, ahi_ready, alo_ready, cum_full, decay_ready, ddt_ready, x_full, z0_full, z1_full,
         z0_read, z1_read, halo_ready, silu_done, y_ready, sq2_ready, ms_full, ms_read, rstd2_ready, out_full, o_ready,
         h_ready) = (sem("m_" + n) for n in (
            "mean_f xc_r sq_r var_f lnv_r rstd_r u1_r u_r dt_f raw_r neg_r e_r l1p_r dt_r a_r ahi_r alo_r cum_f decay_r "
            "ddt_r x_f z0_f z1_f z0_read z1_read halo_r silu_d y_r sq2_r ms_f ms_read rstd2_r out_f o_r h_r").split())
        x_read, conv_step = sem("m_x_read"), sem("m_conv_s")
        (steps_ready, diff_full, L_ready, gt_full, gt_free, gm_ready, mt_ready, y_full, ds_full, faded_ready, yo_ready,
         yt_ready, pyt_full) = (sem("m_" + n) for n in (
            "steps_r diff_f L_r gt_f gt_free gm_r mt_r y_f ds_f faded_r yo_r yt_r pyt_f").split())
        pyt_free = sem("m_pyt_free")
        state_ready = sem("m_state_r")
        n_const, n_x, N_PARS = 16 * len(c_dram), 16 * NB, 16 * 3

        def heads(x):
            return x.unsqueeze(2).broadcast_to([x.shape[0], NH, DS])

        def flat(x):
            return x.rearrange("p a n -> p (a n)")

        def pars(it, col):
            return flat(par[:, bass.ds(it, 1), col:col + 1])

        def tile_in(b, it):
            return XH[:, b, bass.ds(it * TT, TT)]

        def tile_out(b, it):
            return XH[:, b, bass.ds((it + NT) * TT, TT)]

        def tiles(engine, body, finish):
            def step(it, first, last):
                for b in range(NB):
                    nxt = (b + 1, it) if b + 1 < NB else None if last else (0, it + 1)
                    prv = (b - 1, it) if b else None if first else (NB - 1, it - 1)
                    body(it * NB + b, (b, it), nxt, prv)
            step(0, True, False)
            with engine.Fori(1, N_IT - 1) as it:
                step(it, False, False)
            step(N_IT - 1, False, True)
            finish(N_IT * NB, (NB - 1, N_IT - 1))

        sem.start(but=(s_const, s_x, s_par, s_win, s_wout))
        block = ctx.enter_context(nc.Block())

        @block.sync
        def _(sp):
            for b in range(NB):
                sp.dma_start(XH[:, b, 0:T], x_dram[:, b, :]).then_inc(s_x, 16)
                if b == 0:
                    for dst, src in c_dram:
                        sp.dma_start(dst, src).then_inc(s_const, 16)
                    for dst, src in ((par[:, :, :], par_d), (row[:, :, :, :], row_d), (again[:, :], again_d)):
                        sp.dma_start(dst, src).then_inc(s_par, 16)
                    sp.dma_start(win[:, :], win_d[0]).then_inc(s_win, 16)
                    sp.dma_start(wout_in[:, :, :], wout_d[0]).then_inc(s_wout, 16)
            for dst, src in later:
                sp.dma_start(dst, src).then_inc(s_later, 16)
            with sp.Fori(1, N_IT) as it:
                sp.wait_ge(z1_full, START + NB * it)
                sp.dma_start(win[:, :], win_d[bass.ds(it, 1)].rearrange("a p n -> (a p) n")).then_inc(s_win, 16)
                sp.wait_ge(s_prep, START + it)
                sp.dma_start(wout_in[:, :, :], wout_d[bass.ds(it, 1)].rearrange("a p k n -> (a p) k n")).then_inc(s_wout, 16)

        @block.gpsimd
        def _(pool):
            mul = lambda out, x, w: nc.gpsimd.tensor_tensor(out, x, w, ALU.mult)

            def halves(m, b):
                pool.wait_ge(ahi_ready, START + m + 1)
                nc.gpsimd.tensor_tensor(a_lo[b][:, :, :], a[b][:, :, :], a_hi[b][:, :, :].bitcast(F32), ALU.subtract)\
                    .then_inc(alo_ready, 1)
                pool.wait_ge(alo_ready, START + m + 1)

            def steps(g, b, c):
                pool.wait_ge(diff_full, START + lag(g, 1))
                t3 = tri[:, :].unsqueeze(1).broadcast_to([P, NH, Q])
                for x, out in ((a_hi, st_hi), (a_lo, st_lo)):
                    last = mul(out[c % 2][:, :, :], x[b][:, c, :].bitcast(F32).unsqueeze(2).broadcast_to([P, NH, Q]), t3)
                last.then_inc(steps_ready, 1)

            def masked(g, k):
                pool.wait_ge(gm_ready, START + g + 1)
                pool.wait_ge(L_ready, START + g + 1)
                pool.wait_ge(y_full, START + lag(g, 1))
                mul(mt[k][:, :, :], gm[k][:, :].unsqueeze(1).broadcast_to([P, NH, Q]), L[k][:, :, :]).then_inc(mt_ready, 1)

            def fade(g, m, b, c):
                pool.wait_ge(state_ready, START + m * (NC + 1) + 1 + c)
                mul(faded[:, :, :], state[b][:, :, :], heads(decay[b][0:DS, 2, c, :])).then_inc(faded_ready, 1)

            def residual(m, b, it):
                pool.wait_ge(o_ready, START + m + 1)
                nc.gpsimd.tensor_tensor(tile_out(b, it), tile_in(b, it), o[:, :], ALU.add).then_inc(h_ready, 1)

            nc.gpsimd.memset(eps[:, :], LN_EPS).then_inc(s_eps, 1)
            pool.wait_ge(s_const, n_const)
            pool.wait_ge(s_x, n_x)
            halves(0, 0)
            steps(0, 0, 0)
            steps(1, 0, 1)
            masked(0, 0)

            def body(m, now, nxt, prv):
                b, g = now[0], m * NC
                for c in range(NC):
                    fade(g + c, m, b, c)
                    if c == 0:
                        steps(g + 2, b, 2)
                    if c < NC - 1:
                        masked(g + c + 1, (c + 1) % 2)
                    if 0 < c < NC - 2:
                        steps(g + c + 2, b, c + 2)
                    elif c and nxt:
                        if c == NC - 2:
                            halves(m + 1, nxt[0])
                        steps(g + c + 2, nxt[0], c + 2 - NC)
                    if c == NC - 1:
                        if nxt:
                            masked(g + NC, 0)
                        if prv:
                            residual(m - 1, *prv)

            def finish(m, prv):
                residual(m - 1, *prv)
            tiles(pool, body, finish)

        @block.tensor
        def _(pe):
            mm = nc.tensor.matmul

            def mean(m, b, it):
                pe.wait_ge(z1_read, START + m)
                pe.wait_ge(h_ready, START + lag(m, NB * NT - 1))
                mm(place["mean"], mean_w[:, :], tile_in(b, it), start=True, stop=True).then_inc(mean_full, 1)

            def var(m):
                pe.wait_ge(o_ready, START + lag(m, 2))
                pe.wait_ge(sq_ready, START + m + 1)
                mm(place["var"], mean_w[:, :], sq[:, :], start=True, stop=True).then_inc(var_full, 1)

            def project(name, lo, full):
                mm(place[name], win[:, lo:lo + P], u[:, :], start=True, stop=True).then_inc(full, 1)

            def project_dt(m, b, it):
                pe.wait_ge(u_ready, START + m + 1)
                if b == 0:
                    pe.wait_ge(s_win, 16 * (it + 1))
                pe.wait_ge(z0_read, START + m)
                for c in range(NC):
                    last = mm(p_dt[:, c * NH:(c + 1) * NH], u[:, c * Q:(c + 1) * Q], win[:, 2 * DI + 2 * DS:],
                              start=True, stop=True)
                last.then_inc(dt_full, 1)

            def project_x(m, i):
                if i == 2:
                    pe.wait_ge(raw_ready, START + m + 1)
                project(*PARTS[i][0:2], x_full)

            def project_z0(m):
                pe.wait_ge(x_read, START + 3 * m + 3)
                project("z0", 0, z0_full)

            def project_z1(m):
                pe.wait_ge(decay_ready, START + m + 1)
                pe.wait_ge(ms_read, START + lag(m, 1))
                project("z1", P, z1_full)

            def sums(m, b):
                pe.wait_ge(a_ready, START + m + 1)
                pe.wait_ge(x_read, START + 3 * m + 1)
                for k, w in enumerate((tri, low, ones)):
                    last = mm(p_sums[:, k * NC * NH:(k + 1) * NC * NH], w[:, :], a[b][:, :, :].rearrange("p c h -> p (c h)"),
                              start=True, stop=True)
                last.then_inc(cum_full, 1)

            def differences(g, c):
                pe.wait_ge(steps_ready, START + g + 1)
                pe.wait_ge(L_ready, START + g)
                mm(p_diff[:, :, :], low_r[:, :], st_hi[c % 2][:, :, :], start=True, stop=False)
                mm(p_diff[:, :, :], low_r[:, :], st_lo[c % 2][:, :, :], start=False, stop=True).then_inc(diff_full, 1)

            def chunk_front(g, m, b, c):
                q = slice(c * Q, (c + 1) * Q)
                pe.wait_ge(gt_free, START + g)
                if c == 0:
                    pe.wait_ge(silu_done, START + m + 1)
                mm(p_g, bt[b][:, q], ct[b][:, q], start=True, stop=True)
                for k in range(2):
                    nc.tensor.transpose(p_xtok[:, k * P:(k + 1) * P], xs[b][:, k, q], ident[:, :])
                nc.tensor.transpose(p_btok, bt[b][:, q], ident[0:DS, 0:DS]).then_inc(gt_full, 1)

            def chunk_back(g, m, b, c):
                q = slice(c * Q, (c + 1) * Q)
                pe.wait_ge(yt_ready, START + g)
                pe.wait_ge(state_ready, START + m * (NC + 1) + 1 + c)
                mm(p_y[:, 1, :, :], ct[b][:, q], state[b][:, :, :], start=True, stop=True)
                pe.wait_ge(gt_free, START + g + 1)
                pe.wait_ge(mt_ready, START + g + 1)
                for h in range(NH):
                    last = mm(p_y[:, 0, h, :], mt[c % 2][:, h, :], xdt[c % 2][:, h, :], start=True, stop=True)
                last.then_inc(y_full, 1)
                mm(p_ds[:, :], btok[c % 2][:, :], xdec[c % 2][:, :, :], start=True, stop=True).then_inc(ds_full, 1)

            def turn(g, pair, c):
                pe.wait_ge(yt_ready, START + g + 1)
                if c % 2 == 0:
                    pe.wait_ge(pyt_free, START + pair)
                for k in range(2):
                    last = nc.tensor.transpose(p_yt[:, k, c % 2, :], yt[c % 2][:, k * P:(k + 1) * P], ident[:, :])
                last.then_inc(pyt_full, 1)

            def mean_square(m, b, bank_left):
                pe.wait_ge(*bank_left)
                pe.wait_ge(sq2_ready, START + m + 1)
                for k in range(2):
                    last = mm(place["ms"], rms_w[:, :], sq2[:, k, :], start=(k == 0), stop=(k == 1))
                last.then_inc(ms_full, 1)

            def project_out(m, b, it, bank_left):
                pe.wait_ge(*bank_left)
                if b == 0:
                    pe.wait_ge(s_prep, START + it + 1)
                for k in range(2):
                    last = mm(place["out"], wout[:, k, :], y[b][:, k, :], start=(k == 0), stop=(k == 1))
                last.then_inc(out_full, 1)

            pe.wait_ge(s_const, n_const)
            pe.wait_ge(s_x, n_x)
            pe.wait_ge(s_low, START + 1)
            mean(0, 0, 0)
            var(0)
            project_dt(0, 0, 0)
            for i in range(3):
                project_x(0, i)
            sums(0, 0)
            project_z0(0)
            project_z1(0)
            differences(0, 0)
            chunk_front(0, 0, 0, 0)

            def body(m, now, nxt, prv):
                b, g = now[0], m * NC
                if nxt:
                    mean(m + 1, *nxt)
                differences(g + 1, 1)
                chunk_front(g + 1, m, b, 1)
                chunk_back(g, m, b, 0)
                if prv:
                    turn(g - 1, m * 2 - 1, NC - 1)
                if nxt:
                    var(m + 1)
                differences(g + 2, 2)
                chunk_front(g + 2, m, b, 2)
                chunk_back(g + 1, m, b, 1)
                turn(g, m * 2, 0)
                if nxt:
                    project_dt(m + 1, *nxt)
                    project_x(m + 1, 0)
                differences(g + 3, 3)
                chunk_front(g + 3, m, b, 3)
                if nxt:
                    project_x(m + 1, 1)
                    project_x(m + 1, 2)
                chunk_back(g + 2, m, b, 2)
                turn(g + 1, m * 2, 1)
                if nxt:
                    sums(m + 1, nxt[0])
                    project_z0(m + 1)
                if prv:
                    mean_square(m - 1, prv[0], (decay_ready, START + m + 2) if nxt else (z1_read, START + m + 1))
                if nxt:
                    differences(g + 4, 0)
                chunk_back(g + 3, m, b, 3)
                turn(g + 2, m * 2 + 1, 2)
                if prv:
                    project_out(m - 1, *prv, (x_read, START + 3 * m + (5 if nxt else 3)))
                if nxt:
                    project_z1(m + 1)
                    chunk_front(g + 4, m + 1, nxt[0], 0)

            def finish(m, prv):
                turn(m * NC - 1, m * 2 - 1, NC - 1)
                mean_square(m - 1, prv[0], (ms_read, START + m - 1))
                project_out(m - 1, *prv, (o_ready, START + m - 1))
            tiles(pe, body, finish)

        @block.scalar
        def _(act):
            f = nc.scalar.activation

            def square(m):
                act.wait_ge(xc_ready, START + m + 1)
                f(sq[:, :], xc[:, :], ACT.Square).then_inc(sq_ready, 1)

            def norm(m):
                act.wait_ge(var_full, START + m + 1)
                f(rstd[:, :], place["var"], ACT.Ln, bias=eps[:, :]).then_inc(lnv_ready, 1)
                act.wait_ge(lnv_ready, START + m + 1)
                f(rstd[:, :], rstd[:, :], ACT.Exp, scale=-0.5).then_inc(rstd_ready, 1)

            def softplus(m):
                act.wait_ge(neg_ready, START + m + 1)
                f(l1p[:, :, :], neg[:, :, :], ACT.Exp).then_inc(e_ready, 1)
                act.wait_ge(e_ready, START + m + 1)
                f(l1p[:, :, :], l1p[:, :, :], ACT.Ln, bias=1.0).then_inc(l1p_ready, 1)

            def leave(m, b, it, i):
                if i == 0:
                    act.wait_ge(halo_ready, START + lag(m, 1))
                name, _, j = PARTS[i]
                act.wait_ge(x_full, START + 3 * m + i + 1)
                f(pre[b][:, j, DC - 1:], place[name], ACT.Copy)
                f(acc[:, j, :], place[name], ACT.Identity, scale=pars(it, C_CW + 4 * j + 3), bias=pars(it, C_CB + j))\
                    .then_inc(x_read, 1)

            def silus(m, b):
                act.wait_ge(y_ready, START + lag(m, 1))
                act.wait_ge(z0_full, START + m + 1)
                f(zs[b][:, 0, :], place["z0"], ACT.Silu).then_inc(z0_read, 1)
                act.wait_ge(conv_step, START + m * 9 + 7)
                f(xs[b][:, 1, :], acc[:, 1, :], ACT.Silu)
                act.wait_ge(conv_step, START + m * 9 + 8)
                f(bt[b][:, :], acc[0:DS, 2, :], ACT.Silu)
                f(ct[b][:, :], acc[DS:, 2, :], ACT.Silu)
                act.wait_ge(conv_step, START + m * 9 + 9)
                f(xs[b][:, 0, :], acc[:, 0, :], ACT.Silu).then_inc(silu_done, 1)
                act.wait_ge(z1_full, START + m + 1)
                f(zs[b][:, 1, :], place["z1"], ACT.Silu).then_inc(z1_read, 1)

            def decays(m, b):
                act.wait_ge(cum_full, START + m + 1)
                f(decay[b][:, :, :, :].rearrange("p k c h -> p (k c h)"), p_sums, ACT.Exp).then_inc(decay_ready, 1)

            def between(g, k):
                act.wait_ge(diff_full, START + g + 1)
                act.wait_ge(mt_ready, START + lag(g, 1))
                f(L[k][:, :, :], p_diff[:, :, :], ACT.Exp).then_inc(L_ready, 1)

            def square2(m, b):
                act.wait_ge(y_ready, START + m + 1)
                f(sq2[:, :, :], y[b][:, :, :], ACT.Square).then_inc(sq2_ready, 1)

            def norm2(m):
                act.wait_ge(ms_full, START + m + 1)
                act.wait_ge(o_ready, START + m)
                f(rstd2[:, :], place["ms"], ACT.Ln, bias=eps[:, :]).then_inc(ms_read, 1)
                act.wait_ge(ms_read, START + m + 1)
                f(rstd2[:, :], rstd2[:, :], ACT.Exp, scale=-0.5).then_inc(rstd2_ready, 1)

            def silu_block(m, b):
                act.preload_act_table_set("silu_and_others")
                silus(m, b)
                act.preload_act_table_set("natural_log_exp_and_others")

            act.preload_act_table_set("natural_log_exp_and_others")
            act.wait_ge(s_eps, START + 1)
            act.wait_ge(s_par, N_PARS)
            f(arow[:, :, :], row[:, 1, :, :], ACT.Exp).then_inc(s_arow, 1)
            square(0)
            norm(0)
            softplus(0)
            for j in range(3):
                leave(0, 0, 0, j)
            decays(0, 0)
            between(0, 0)
            silu_block(0, 0)

            def body(m, now, nxt, prv):
                g = m * NC
                if nxt:
                    square(m + 1)
                between(g + 1, 1)
                if nxt:
                    norm(m + 1)
                between(g + 2, 0)
                if prv:
                    square2(m - 1, prv[0])
                if nxt:
                    softplus(m + 1)
                    leave(m + 1, *nxt, 0)
                    leave(m + 1, *nxt, 1)
                between(g + 3, 1)
                if nxt:
                    leave(m + 1, *nxt, 2)
                    decays(m + 1, nxt[0])
                if prv:
                    norm2(m - 1)
                if nxt:
                    between(g + 4, 0)
                    silu_block(m + 1, nxt[0])

            def finish(m, prv):
                square2(m - 1, prv[0])
                norm2(m - 1)
            tiles(act, body, finish)

        @block.vector
        def _(dve):
            v = nc.vector

            def centre(m, b, it):
                dve.wait_ge(mean_full, START + m + 1)
                dve.wait_ge(sq_ready, START + m)
                v.tensor_tensor(xc[:, :], tile_in(b, it), place["mean"], ALU.subtract).then_inc(xc_ready, 1)

            def scale(m, it):
                dve.wait_ge(rstd_ready, START + m + 1)
                dve.wait_ge(xc_ready, START + m + 1)
                dve.wait_ge(z1_full, START + m)
                v.tensor_tensor(u[:, :], xc[:, :], rstd[:, :], ALU.mult).then_inc(u1_ready, 1)
                dve.wait_ge(u1_ready, START + m + 1)
                v.tensor_scalar(u[:, :], u[:, :], pars(it, C_LNW), pars(it, C_LNB), ALU.mult, ALU.add).then_inc(u_ready, 1)

            def softplus_in(m, it):
                dve.wait_ge(dt_full, START + m + 1)
                v.tensor_tensor(raw[:, :, :], p_dt.rearrange("p (c h) -> p c h", h=NH),
                                row[:, 0, bass.ds(it, 1), :].broadcast_to([P, NC, NH]), ALU.add).then_inc(raw_ready, 1)
                dve.wait_ge(raw_ready, START + m + 1)
                v.scalar_tensor_tensor(neg[:, :, :], raw[:, :, :], -1.0, raw[:, :, :], ALU.mult, ALU.min).then_inc(neg_ready, 1)

            def softplus_out(m, b, it):
                dve.wait_ge(l1p_ready, START + m + 1)
                v.scalar_tensor_tensor(dt[b][:, :, :], raw[:, :, :], 0.0, l1p[:, :, :], ALU.max, ALU.add).then_inc(dt_ready, 1)
                dve.wait_ge(dt_ready, START + m + 1)
                for out, ready in ((a, a_ready), (a_hi, ahi_ready)):
                    v.tensor_tensor(out[b][:, :, :], dt[b][:, :, :], arow[:, bass.ds(it, 1), :].broadcast_to([P, NC, NH]), ALU.mult)\
                        .then_inc(ready, 1)

            def convolve(m, b, it, k, i):
                j = PARTS[i][2]
                if k == 0:
                    dve.wait_ge(x_read, START + 3 * m + i + 1)
                    dve.wait_ge(halo_ready, START + lag(m, 1))
                else:
                    dve.wait_ge(conv_step, START + m * 9 + (k - 1) * 3 + i + 1)
                v.scalar_tensor_tensor(acc[:, j, :], pre[b][:, j, k:k + TT], pars(it, C_CW + 4 * j + k), acc[:, j, :],
                                       ALU.mult, ALU.add).then_inc(conv_step, 1)

            def halo(m, b, it):
                dve.wait_ge(conv_step, START + m * 9 + 9)
                v.tensor_scalar(pre[b][:, :, 0:DC - 1], pre[b][:, :, TT:], again[:, bass.ds(it + 1, 1)], None, ALU.mult)\
                    .then_inc(halo_ready, 1)

            def decays(m, b):
                dve.wait_ge(decay_ready, START + m + 1)
                v.tensor_tensor(ddt[b][:, :, :], decay[b][:, 1, :, :], dt[b][:, :, :], ALU.mult).then_inc(ddt_ready, 1)

            def clear_state(m, b, it):
                v.tensor_scalar(state[b][:, :, :], state[b][:, :, :], again[0:DS, bass.ds(it, 1)], None, ALU.mult)\
                    .then_inc(state_ready, 1)

            def chunk_front(g, m, b, c):
                k = c % 2
                dve.wait_ge(gt_full, START + g + 1)
                dve.wait_ge(ddt_ready, START + m + 1)
                dve.wait_ge(ds_full, START + lag(g, 1))
                v.tensor_tensor(gm[k][:, :], p_g, tri[:, :], ALU.mult).then_inc(gm_ready, 1)
                x3 = p_xtok.rearrange("p (h n) -> p h n", h=NH)
                v.tensor_tensor(xdt[k][:, :, :], x3, heads(dt[b][:, c, :]), ALU.mult)
                v.tensor_tensor(xdec[k][:, :, :], x3, heads(ddt[b][:, c, :]), ALU.mult)
                v.tensor_copy(btok[k][:, :], p_btok).then_inc(gt_free, 1)

            def chunk_back(g, b, c):
                k = c % 2
                dve.wait_ge(y_full, START + g + 1)
                v.tensor_tensor(yo[k][:, :, :], p_y[:, 1, :, :], heads(decay[b][:, 0, c, :]), ALU.mult).then_inc(yo_ready, 1)
                dve.wait_ge(faded_ready, START + g + 1)
                dve.wait_ge(ds_full, START + g + 1)
                v.tensor_tensor(state[b][:, :, :], faded[:, :, :], p_ds[:, :].rearrange("p (h n) -> p h n", h=NH), ALU.add)\
                    .then_inc(state_ready, 1)
                dve.wait_ge(yo_ready, START + g + 1)
                dve.wait_ge(pyt_full, START + lag(g, 1))
                v.tensor_tensor(yt[k][:, :], yo[k][:, :, :].rearrange("p h n -> p (h n)"),
                                p_y[:, 0, :, :].rearrange("p h n -> p (h n)"), ALU.add).then_inc(yt_ready, 1)

            def skip(pair, b, it, j):
                dve.wait_ge(pyt_full, START + pair * 2 + 2)
                q = slice(j * 2 * Q, (j + 1) * 2 * Q)
                for k in range(2):
                    last = v.scalar_tensor_tensor(y[b][:, k, q], xs[b][:, k, q], pars(it, C_D + k),
                                                  p_yt[:, k, :, :].rearrange("p c q -> p (c q)"), ALU.mult, ALU.add)
                last.then_inc(pyt_free, 1)

            def gate(m, b):
                dve.wait_ge(pyt_free, START + m * 2 + 2)
                v.tensor_tensor(y[b][:, :, :], y[b][:, :, :], zs[b][:, :, :], ALU.mult).then_inc(y_ready, 1)

            def prepare_out(it):
                dve.wait_ge(out_full, START + it * NB)
                dve.wait_ge(s_wout, 16 * (it + 1))
                for k in range(2):
                    last = v.tensor_scalar(wout[:, k, :], wout_in[:, k, :], pars(it, C_RW + k), None, ALU.mult)
                last.then_inc(s_prep, 1)

            def normed(m):
                dve.wait_ge(out_full, START + m + 1)
                dve.wait_ge(rstd2_ready, START + m + 1)
                dve.wait_ge(h_ready, START + m)
                v.tensor_tensor(o[:, :], place["out"], rstd2[:, :], ALU.mult).then_inc(o_ready, 1)

            for b in range(NB):
                v.memset(pre[b][:, :, 0:DC - 1], 0.0)
                v.memset(state[b][:, :, :], 0.0)
            dve.wait_ge(s_const, n_const)
            v.tensor_copy(low_r[:, :], low[:, :]).then_inc(s_low, 1)
            dve.wait_ge(s_x, n_x)
            centre(0, 0, 0)
            dve.wait_ge(s_par, N_PARS)
            scale(0, 0)
            softplus_in(0, 0)
            dve.wait_ge(s_arow, START + 1)
            v.tensor_scalar(arow[:, :, :], arow[:, :, :], -1.0, None, ALU.mult).then_inc(s_arow, 1)
            dve.wait_ge(s_arow, START + 2)
            softplus_out(0, 0, 0)
            for k in range(DC - 1):
                for j in range(3):
                    convolve(0, 0, 0, k, j)
            halo(0, 0, 0)
            decays(0, 0)
            clear_state(0, 0, 0)
            chunk_front(0, 0, 0, 0)

            def body(m, now, nxt, prv):
                b, it = now
                g = m * NC
                if nxt:
                    centre(m + 1, *nxt)
                chunk_front(g + 1, m, b, 1)
                chunk_back(g, b, 0)
                if prv:
                    skip(m * 2 - 1, *prv, 1)
                if nxt:
                    scale(m + 1, nxt[1])
                if prv:
                    gate(m - 1, prv[0])
                chunk_front(g + 2, m, b, 2)
                chunk_back(g + 1, b, 1)
                if nxt:
                    softplus_in(m + 1, nxt[1])
                    convolve(m + 1, *nxt, 0, 0)
                if nxt:
                    softplus_out(m + 1, *nxt)
                chunk_front(g + 3, m, b, 3)
                if nxt:
                    convolve(m + 1, *nxt, 0, 1)
                    convolve(m + 1, *nxt, 0, 2)
                chunk_back(g + 2, b, 2)
                skip(m * 2, b, it, 0)
                if nxt:
                    for k in range(1, DC - 1):
                        for j in range(3):
                            convolve(m + 1, *nxt, k, j)
                    halo(m + 1, *nxt)
                    decays(m + 1, nxt[0])
                chunk_back(g + 3, b, 3)
                if prv:
                    normed(m - 1)
                if b == 0:
                    prepare_out(it)
                if nxt:
                    clear_state(m + 1, *nxt)
                    chunk_front(g + 4, m + 1, nxt[0], 0)

            def finish(m, prv):
                skip(m * 2 - 1, *prv, 1)
                gate(m - 1, prv[0])
                normed(m - 1)
            tiles(dve, body, finish)


class Banks:

    def __init__(self, nc, ps, sem, prefix, order, n):
        self.per, self.slot, self.bank = [0] * n, {}, []
        for k in range(n):
            self.bank.append((ps(f"{prefix}_bank{k}", [P, 512]), sem(f"{prefix}_full{k}"), sem(f"{prefix}_free{k}")))
        for i, name in enumerate(order):
            self.slot[name] = (i % n, self.per[i % n])
            self.per[i % n] += 1

    def before(self, name, it):
        k, i = self.slot[name]
        bank, _, free = self.bank[k]
        return bank, free, it * self.per[k] + i

    def full(self, name, it):
        k, i = self.slot[name]
        bank, full, _ = self.bank[k]
        return bank, full, it * self.per[k] + i + 1

    def read(self, name, it):
        k, i = self.slot[name]
        return self.bank[k][2], START + it * self.per[k] + i + 1

    def sem_full(self, name):
        return self.bank[self.slot[name][0]][1]

    def sem_free(self, name):
        return self.bank[self.slot[name][0]][2]


def ffn(nc, X, H, XP, cst, wts):
    tri, low, ones, ident, mean_w, rms_w = cst
    up, down, split, s_weights, n_weights = wts
    FB = 512 // P
    with ExitStack() as ctx:
        sb, ps, sem = tensors(nc, ctx)
        two = lambda name, shape: [sb(f"f_{name}{b}", shape) for b in range(NB)]
        s, sq, r, xn = two("s", [P, TT]), two("sq", [P, TT]), two("r", [P, TT]), two("xn", [P, TT])
        hid, hsq, o = two("hid", [P, FB, TT]), two("hsq", [P, FB, TT]), two("o", [P, TT])
        asum, thr, nthr = sb("f_asum", [P, 2]), sb("f_thr", [P, 2]), sb("f_nthr", [P, 2])
        mneg = sb("f_mneg", [P, 2, 512])
        eps, tiny, guard = sb("f_eps", [P, 1]), sb("f_tiny", [P, 1]), sb("f_guard", [P, 1])
        STAGES = ["mean", "var", "ms", "up0", "up1", "up2", "up3", "ms2", "down", "mean2", "var2"]
        order = [(n, b) for n in STAGES for b in range(NB)]
        K = Banks(nc, ps, sem, "f", order, 8)
        each = lambda name: [sem(f"f_{name}{b}") for b in range(NB)]
        s_eps, s_asum, s_alpha, s_thr, s_neg, s_tern = map(sem, ("f_eps_r", "f_asum_r", "f_alpha", "f_thr_r", "f_neg_r", "f_tern"))
        s_high = sem("f_high")
        s1_ready, sq_ready, rstd_ready, x1_ready, sq1_ready, xn_ready = map(
            each, ("s1", "sqr", "rstd", "x1", "sq1", "xnr"))
        rms_ready, lrms_ready, r_ready = map(each, ("rms", "lrms", "rr"))
        hsq_ready, s2_ready, sq2_ready, rstd2_ready, x2_ready = map(each, ("hsq_r", "s2", "sq2", "rstd2", "x2"))
        sem.start()
        block = ctx.enter_context(nc.Block())

        @block.gpsimd
        def _(pool):
            nc.gpsimd.memset(XP[:, :, :], 0.0)
            nc.gpsimd.memset(eps[:, :], LN_EPS)
            nc.gpsimd.memset(tiny[:, :], 1e-19)
            nc.gpsimd.memset(guard[:, :], 1e-8).then_inc(s_eps, 1)
            pool.wait_ge(s_weights, n_weights)
            for k, (w, hi, lo) in enumerate(split):
                nc.gpsimd.tensor_copy(hi, w).then_inc(s_high, 1)
                pool.wait_ge(s_high, START + k + 1)
                nc.gpsimd.tensor_tensor(lo, w, hi.bitcast(F32), ALU.subtract)
            with pool.Fori(0, NT) as t:
                for b in range(NB):
                    for j in range(FB):
                        pool.wait_ge(*K.read((f"up{j}", b), t))
                        nc.gpsimd.tensor_tensor(hsq[b][:, j, :], hid[b][:, j, :], hid[b][:, j, :], ALU.mult)\
                            .then_inc(hsq_ready[b], 1)

        @block.tensor
        def _(pe):
            mm = nc.tensor.matmul

            def product(name, b, it, terms):
                bank, free, n = K.before((name, b), it)
                pe.wait_ge(free, START + n)
                for i, (w, x) in enumerate(terms):
                    last = mm(bank[:, :], w, x, start=(i == 0), stop=(i == len(terms) - 1))
                last.then_inc(K.sem_full((name, b)), 1)

            pe.wait_ge(s_weights, n_weights)
            pe.wait_ge(s_asum, START + 2)
            bank = K.bank[7][0]
            mm(bank[:, 0:2], ones[:, :], asum[:, :], start=True, stop=True).then_inc(s_alpha, 1)
            pe.wait_ge(s_thr, START + 1)
            with pe.Fori(0, NT) as t:
                for b in range(NB):
                    pe.wait_ge(s1_ready[b], START + t + 1)
                    product("mean", b, t, [(mean_w[:, :], s[b][:, :])])
                for b in range(NB):
                    pe.wait_ge(sq_ready[b], START + t + 1)
                    product("var", b, t, [(mean_w[:, :], sq[b][:, :])])
                for b in range(NB):
                    pe.wait_ge(sq1_ready[b], START + t + 1)
                    product("ms", b, t, [(mean_w[:, :], sq[b][:, :])])
                for j in range(FB):
                    for b in range(NB):
                        if j == 0:
                            pe.wait_ge(xn_ready[b], START + t + 1)
                            if b == 0:
                                pe.wait_ge(s_tern, START + 2)
                        product(f"up{j}", b, t, [(up[:, j * P:(j + 1) * P], xn[b][:, :])])
                for b in range(NB):
                    pe.wait_ge(hsq_ready[b], START + (t + 1) * FB)
                    product("ms2", b, t, [(rms_w[:, :], hsq[b][:, j, :]) for j in range(FB)])
                for b in range(NB):
                    pe.wait_ge(hsq_ready[b], START + (t + 1) * FB)
                    product("down", b, t, [(down[:, j, :], hid[b][:, j, :]) for j in range(FB)])
                for b in range(NB):
                    pe.wait_ge(s2_ready[b], START + t + 1)
                    product("mean2", b, t, [(mean_w[:, :], s[b][:, :])])
                for b in range(NB):
                    pe.wait_ge(sq2_ready[b], START + t + 1)
                    product("var2", b, t, [(mean_w[:, :], sq[b][:, :])])

        @block.scalar
        def _(act):
            f = nc.scalar.activation

            def rstd(name, b, it, done):
                bank, full, n = K.full((name, b), it)
                act.wait_ge(full, START + n)
                f(r[b][:, :], bank[:, :], ACT.Ln, bias=eps[:, :]).then_inc(K.sem_free((name, b)), 1)
                act.wait_ge(K.sem_free((name, b)), START + n)
                f(r[b][:, :], r[b][:, :], ACT.Exp, scale=-0.5).then_inc(done[b], 1)

            def one_over_rms(name, b, it, scale, k):
                bank, full, n = K.full((name, b), it)
                act.wait_ge(full, START + n)
                f(r[b][:, :], bank[:, :], ACT.Ln, bias=tiny[:, :], scale=scale).then_inc(K.sem_free((name, b)), 1)
                act.wait_ge(K.sem_free((name, b)), START + n)
                f(r[b][:, :], r[b][:, :], ACT.Exp, scale=0.5).then_inc(rms_ready[b], 1)
                act.wait_ge(rms_ready[b], START + 2 * it + k + 1)
                f(r[b][:, :], r[b][:, :], ACT.Ln, bias=guard[:, :]).then_inc(lrms_ready[b], 1)
                act.wait_ge(lrms_ready[b], START + 2 * it + k + 1)
                f(r[b][:, :], r[b][:, :], ACT.Exp, scale=-1.0).then_inc(r_ready[b], 1)

            act.preload_act_table_set("natural_log_exp_and_others")
            act.wait_ge(s_eps, START + 1)
            with act.Fori(0, NT) as t:
                act.preload_act_table_set("natural_log_exp_and_others")
                for b in range(NB):
                    act.wait_ge(*K.read(("mean", b), t))
                    f(sq[b][:, :], s[b][:, :], ACT.Square).then_inc(sq_ready[b], 1)
                for b in range(NB):
                    rstd("var", b, t, rstd_ready)
                for b in range(NB):
                    act.wait_ge(x1_ready[b], START + t + 1)
                    f(sq[b][:, :], X[:, b, bass.ds(t * TT, TT)], ACT.Square).then_inc(sq1_ready[b], 1)
                for b in range(NB):
                    one_over_rms("ms", b, t, 1.0, 0)
                for j in range(FB):
                    for b in range(NB):
                        bank, full, n = K.full((f"up{j}", b), t)
                        if j == 0:
                            act.wait_ge(x2_ready[b], START + t)
                        act.wait_ge(full, START + n)
                        f(hid[b][:, j, :], bank[:, :], ACT.Gelu).then_inc(K.sem_free((f"up{j}", b)), 1)
                act.preload_act_table_set("natural_log_exp_and_others")
                for b in range(NB):
                    one_over_rms("ms2", b, t, 0.5, 1)
                for b in range(NB):
                    act.wait_ge(*K.read(("mean2", b), t))
                    f(sq[b][:, :], s[b][:, :], ACT.Square).then_inc(sq2_ready[b], 1)
                for b in range(NB):
                    rstd("var2", b, t, rstd2_ready)

        @block.vector
        def _(dve):
            v = nc.vector

            def centre(name, b, it):
                bank, full, n = K.full((name, b), it)
                dve.wait_ge(full, START + n)
                v.tensor_tensor(s[b][:, :], s[b][:, :], bank[:, :], ALU.subtract).then_inc(K.sem_free((name, b)), 1)

            dve.wait_ge(s_weights, n_weights)
            for k, w in enumerate((up[:, :], down[:, :, :].rearrange("p k n -> p (k n)"))):
                v.tensor_reduce(asum[:, k:k + 1], w, AX.X, ALU.add, apply_absolute_value=True).then_inc(s_asum, 1)
            dve.wait_ge(s_alpha, START + 1)
            bank = K.bank[7][0]
            v.tensor_scalar(thr[:, :], bank[:, 0:2], 0.5 / (D * 512), None, ALU.mult)
            v.tensor_scalar(nthr[:, :], bank[:, 0:2], -0.5 / (D * 512), None, ALU.mult).then_inc(s_thr, 1)
            dve.wait_ge(s_thr, START + 1)
            for k, w in enumerate((up[:, :], down[:, :, :].rearrange("p k n -> p (k n)"))):
                v.tensor_scalar(mneg[:, k, :], w, nthr[:, k:k + 1], None, ALU.is_lt).then_inc(s_neg, 1)
                dve.wait_ge(s_neg, START + k + 1)
                v.scalar_tensor_tensor(w, w, thr[:, k:k + 1], mneg[:, k, :], ALU.is_gt, ALU.subtract).then_inc(s_tern, 1)
            dve.wait_ge(s_eps, START + 1)
            with dve.Fori(0, NT) as t:
                tile = lambda b: X[:, b, bass.ds(t * TT, TT)]
                for b in range(NB):
                    dve.wait_ge(x2_ready[b], START + t)
                    v.tensor_tensor(s[b][:, :], tile(b), H[:, b, bass.ds(t * TT, TT)], ALU.add).then_inc(s1_ready[b], 1)
                for b in range(NB):
                    centre("mean", b, t)
                for b in range(NB):
                    dve.wait_ge(rstd_ready[b], START + t + 1)
                    v.tensor_tensor(tile(b), s[b][:, :], r[b][:, :], ALU.mult).then_inc(x1_ready[b], 1)
                for b in range(NB):
                    dve.wait_ge(r_ready[b], START + 2 * t + 1)
                    v.tensor_tensor(xn[b][:, :], tile(b), r[b][:, :], ALU.mult).then_inc(xn_ready[b], 1)
                for b in range(NB):
                    bank, full, n = K.full(("down", b), t)
                    dve.wait_ge(full, START + n)
                    dve.wait_ge(r_ready[b], START + 2 * t + 2)
                    v.tensor_tensor(o[b][:, :], bank[:, :], r[b][:, :], ALU.mult).then_inc(K.sem_free(("down", b)), 1)
                    dve.wait_ge(K.sem_free(("down", b)), START + n)
                    v.tensor_tensor(s[b][:, :], o[b][:, :], tile(b), ALU.add).then_inc(s2_ready[b], 1)
                for b in range(NB):
                    centre("mean2", b, t)
                for b in range(NB):
                    dve.wait_ge(rstd2_ready[b], START + t + 1)
                    v.tensor_tensor(XP[:, bass.ds(b * NT + t, 1), 1:TT + 1].rearrange("p a n -> p (a n)"), s[b][:, :], r[b][:, :], ALU.mult)\
                        .then_inc(x2_ready[b], 1)
            for b in range(NB):
                dve.wait_ge(x2_ready[b], START + NT)
                for t in range(1, NT):
                    before, behind = XP[:, b * NT + t - 1, :], XP[:, b * NT + t, :]
                    v.tensor_copy(before[:, TT + 1:], behind[:, 1:2])
                    v.tensor_copy(behind[:, 0:1], before[:, TT:TT + 1])


EPS = math.exp(-1 / 12)
EPS_RKV = (EPS / 2, EPS + 0.3 / 11, EPS)
NF = 8
E_LO, E_HI = float(np.exp(np.float32(-20))), float(np.exp(np.float32(10)))
BIG = 2.0 ** 39
NTILE = NB * NT
TP = TT + 2


def wkv(nc, X, XP, SCR, cst, wts):
    tri, low, ones, ident, mean_w, rms_w = cst
    wr, wk, wv, wo, decay, t_rem, par, bo, keep, behind, s_weights, n_weights = wts
    U_, BK, BR, BV, DECAY = range(5)
    with ExitStack() as ctx:
        sb, ps, sem = tensors(nc, ctx)
        mix_kv = sb("w_mix_kv", [P, NTILE, 2, TT])
        t_in = sb("w_t_in", [2, TT], F32R)
        later = sb("w_later", [P, NF, NTILE])
        neg_w = sb("w_neg_w", [P, NF])
        dec_hi, dec_lo = sb("w_dec_hi", [2, NF * P], F32R), sb("w_dec_lo", [2, NF * P], F32R)
        ubk, nbr = sb("w_ubk", [P, NF]), sb("w_nbr", [P, NF])
        eps, onec = sb("w_eps", [P, 1]), sb("w_one", [P, 1])
        RING = 4
        ring = lambda name, shape: [sb(f"w_{name}{k}", shape) for k in range(RING)]
        V, er, G = ring("V", [P, TT]), ring("er", [P, TT]), ring("G", [P, 4, TT])
        AB, O = ring("AB", [P, 2, TT]), ring("O", [P, TT])
        CS = ring("CS", [P, 2, 1 + TT])
        carry = sb("w_carry", [P, NF, 2])
        s, sq, r = (SCR[:, :, :].rearrange("p b t -> p (b t)")[:, k * TT:(k + 1) * TT] for k in range(3))
        pk = [ps(f"w_pk{k}", [P, TT]) for k in range(2)]
        pv = [ps(f"w_pv{k}", [P, TT]) for k in range(2)]
        pr = [ps(f"w_pr{k}", [P, TT]) for k in range(2)]
        pacc, pst = ps("w_pacc", [P, TT]), ps("w_pst", [P, TT])
        (s_eps, s_prep, mix1, mix_ready, k_full, k_read, kw_full, kw_read, v_full, v_read, r_full, er_read, clip_ready, er1_ready,
         ev_ready, cs_ready, ab_ready, dn_ready, ln_ready, rd_ready, o_ready, o_used, s_ready, mean_full, xc_ready,
         sq_ready, var_full, lv_ready, rstd_ready, x3_ready, halo, carry_ready, dec_ready) = [sem(f"w_s{i}_{n}") for i, n in enumerate(
             "eps prep mix1 mix k_full k_read kw_full kw_read v_full v_read r_full er clip er1 ev cs ab dn ln rd o o_used "
             "s mean xc sq var lv rstd x3 halo carry dec".split())]
        sem.start()
        block = ctx.enter_context(nc.Block())
        xp = XP[:, :, :]
        xf = X[:, :, :].rearrange("p b t -> p (b t)")

        def tiles(engine, body):
            body(0, True, False)
            with engine.Fori(1, NTILE - 1) as i:
                body(i, False, False)
            body(NTILE - 1, False, True)

        def mix(i, j):
            if j == 0:
                return xf[:, bass.ds(i * TT, TT)]
            return mix_kv[:, bass.ds(i, 1), j - 1, :].rearrange("p a t -> p (a t)")

        @block.gpsimd
        def _(pool):
            nc.gpsimd.memset(eps[:, :], LN_EPS)
            nc.gpsimd.memset(onec[:, :], 1.0).then_inc(s_eps, 1)

            def body(i, first, last):
                for f in range(NF):
                    k, n = f % RING, i * NF + f
                    pool.wait_ge(cs_ready, START + n + 1)
                    if not (first and f < RING):
                        pool.wait_ge(o_ready, START + n - RING + 1)
                    nc.gpsimd.tensor_tensor(AB[k][:, :, :], CS[k][:, :, 0:TT], G[k][:, 2:4, :], ALU.add).then_inc(ab_ready, 1)
                    pool.wait_ge(ab_ready, START + n + 1)
                    pool.wait_ge(er1_ready, START + n + 1)
                    nc.gpsimd.tensor_tensor(er[k][:, :], AB[k][:, 1, :], er[k][:, :], ALU.mult).then_inc(dn_ready, 1)
            tiles(pool, body)

        @block.tensor
        def _(pe):
            mm = nc.tensor.matmul

            def project(f, n, first, x):
                k, fs = f % 2, slice(f * P, (f + 1) * P)
                old = not (first and f < 2)
                if old:
                    pe.wait_ge(kw_read, START + n - 1)
                mm(pk[k][:, :], wk[:, fs], x(1), start=True, stop=True).then_inc(k_full, 1)
                if old:
                    pe.wait_ge(v_read, START + n - 1)
                mm(pv[k][:, :], wv[:, fs], x(2), start=True, stop=True).then_inc(v_full, 1)
                if old:
                    pe.wait_ge(er_read, START + n - 1)
                mm(pr[k][:, :], wr[:, fs], x(0), start=True, stop=True).then_inc(r_full, 1)
                pe.wait_ge(k_read, START + n + 1)
                mm(pk[k][:, :], dec_hi[:, fs], t_in[:, :], start=False, stop=True, skip_group_check=True)
                mm(pk[k][:, :], dec_lo[:, fs], t_in[:, :], start=False, stop=True, skip_group_check=True).then_inc(kw_full, 1)

            def collect(f, n, tile):
                pe.wait_ge(o_ready, START + n + 1)
                if f == 0 and tile is not None:
                    pe.wait_ge(s_ready, START + tile)
                mm(pacc[:, :], wo[:, f, :], O[f % RING][:, :], start=(f == 0), stop=(f == NF - 1)).then_inc(o_used, 1)

            def mix_of(i):
                return lambda j: mix(i, j)

            def mean(i):
                pe.wait_ge(s_ready, START + i + 1)
                mm(pst[:, :], mean_w[:, :], s[:, :], start=True, stop=True).then_inc(mean_full, 1)

            def var(i):
                pe.wait_ge(sq_ready, START + i + 1)
                mm(pst[:, :], mean_w[:, :], sq[:, :], start=True, stop=True).then_inc(var_full, 1)

            pe.wait_ge(s_weights, n_weights)
            pe.wait_ge(s_prep, START + 1)
            pe.wait_ge(mix_ready, START + 1)
            project(0, 0, True, mix_of(0))

            def body(i, first, last):
                for f in range(NF):
                    n = i * NF + f
                    if f < NF - 1:
                        project(f + 1, n + 1, first, mix_of(i))
                    elif not last:
                        pe.wait_ge(mix_ready, START + i + 2)
                        project(0, n + 1, False, mix_of(i + 1))
                    if f >= 4:
                        for k in (0, 1) if f == 4 else (f - 3,):
                            collect(k, i * NF + k, None if first else i)
                    elif f < 3 and not first:
                        collect(f - 3 + NF, n - 3, None)
                    if not first:
                        if f == 4:
                            mean(i - 1)
                        if f == 6:
                            var(i - 1)
            tiles(pe, body)
            for f in range(NF - 3, NF):
                collect(f, (NTILE - 1) * NF + f, None)
            mean(NTILE - 1)
            var(NTILE - 1)

        @block.scalar
        def _(act):
            a = nc.scalar.activation

            def front(f, n, i, first):
                k, b = f % RING, f % 2
                old = not (first and f < RING)
                act.wait_ge(k_full, START + n + 1)
                if old:
                    act.wait_ge(ab_ready, START + n - RING + 1)
                a(G[k][:, 3, :], pk[b][:, :], ACT.Exp, bias=ubk[:, f:f + 1]).then_inc(k_read, 1)
                act.wait_ge(v_full, START + n + 1)
                a(V[k][:, :], pv[b][:, :], ACT.Identity, bias=par[:, f, BV:BV + 1]).then_inc(v_read, 1)
                act.wait_ge(r_full, START + n + 1)
                if old:
                    act.wait_ge(o_ready, START + n - RING + 1)
                a(er[k][:, :], pr[b][:, :], ACT.Exp, scale=-1.0, bias=nbr[:, f:f + 1]).then_inc(er_read, 1)
                act.wait_ge(kw_full, START + n + 1)
                a(G[k][:, 1, :], pk[b][:, :], ACT.Exp, bias=later[:, f, bass.ds(i, 1)]).then_inc(kw_read, 1)

            def back(f, n):
                k = f % RING
                act.wait_ge(dn_ready, START + n + 1)
                a(er[k][:, :], er[k][:, :], ACT.Ln).then_inc(ln_ready, 1)
                act.wait_ge(ln_ready, START + n + 1)
                a(er[k][:, :], er[k][:, :], ACT.Exp, scale=-1.0).then_inc(rd_ready, 1)

            def before(i):
                for j, e in enumerate(EPS_RKV):
                    a(mix(i, j), xp[:, bass.ds(i, 1), 0:TT].rearrange("p a t -> p (a t)"), ACT.Copy, scale=e).then_inc(mix1, 1)

            def square(i):
                act.wait_ge(xc_ready, START + i + 1)
                a(sq[:, :], s[:, :], ACT.Square).then_inc(sq_ready, 1)

            def rstd(i):
                act.wait_ge(var_full, START + i + 1)
                a(r[:, :], pst[:, :], ACT.Ln, bias=eps[:, :]).then_inc(lv_ready, 1)
                act.wait_ge(lv_ready, START + i + 1)
                a(r[:, :], r[:, :], ACT.Exp, scale=-0.5).then_inc(rstd_ready, 1)

            act.preload_act_table_set("natural_log_exp_and_others")
            before(0)
            act.wait_ge(s_eps, START + 1)
            act.wait_ge(s_prep, START + 1)

            def body(i, first, last):
                for f in range(NF):
                    n = i * NF + f
                    front(f, n, i, first)
                    if f >= 2:
                        back(f - 2, n - 2)
                    elif not first:
                        back(f - 2 + NF, n - 2)
                    if f == 3 and not last:
                        before(i + 1)
                    if not first:
                        if f == 5:
                            square(i - 1)
                        if f == 7:
                            rstd(i - 1)
            tiles(act, body)
            for f in range(NF - 2, NF):
                back(f, (NTILE - 1) * NF + f)
            square(NTILE - 1)
            rstd(NTILE - 1)

        @block.vector
        def _(dve):
            v = nc.vector

            def blend(i):
                for j, e in enumerate(EPS_RKV):
                    dve.wait_ge(mix1, START + i * 3 + j + 1)
                    last = v.scalar_tensor_tensor(mix(i, j),
                                                  xp[:, bass.ds(i, 1), 2:].rearrange("p a t -> p (a t)"), 1.0 - e,
                                                  mix(i, j), ALU.mult, ALU.add)
                last.then_inc(mix_ready, 1)

            def front(f, n, i, first):
                k = f % RING
                dve.wait_ge(kw_read, START + n + 1)
                v.tensor_scalar(G[k][:, 1::2, :], G[k][:, 1::2, :], E_LO, E_HI, ALU.max, ALU.min).then_inc(clip_ready, 1)
                dve.wait_ge(er_read, START + n + 1)
                v.tensor_scalar(er[k][:, :], er[k][:, :], BIG, 1.0, ALU.min, ALU.add).then_inc(er1_ready, 1)
                if not first:
                    dve.wait_ge(carry_ready, START + n - NF + 1)
                if not (first and f < RING):
                    dve.wait_ge(ab_ready, START + n - RING + 1)
                v.tensor_tensor(CS[k][:, :, 0], carry[:, f, :], keep[:, bass.ds(i, 1)].broadcast_to([P, 2]), ALU.mult).then_inc(halo, 1)
                dve.wait_ge(clip_ready, START + n + 1)
                dve.wait_ge(v_read, START + n + 1)
                v.tensor_tensor(G[k][:, 0::2, :], G[k][:, 1::2, :], V[k][:, :].unsqueeze(1).broadcast_to([P, 2, TT]), ALU.mult)\
                    .then_inc(ev_ready, 1)
                dve.wait_ge(halo, START + n + 1)
                for j in (1, 0):
                    if j == 0:
                        dve.wait_ge(ev_ready, START + n + 1)
                    last = v.tensor_tensor_scan(CS[k][:, j, 1:], onec[:, :].broadcast_to([P, TT]), G[k][:, j, :],
                                                CS[k][:, j, 0:1], ALU.mult, ALU.add)
                last.then_inc(cs_ready, 1)

            def back(f, n, first):
                k = f % RING
                dve.wait_ge(cs_ready, START + n + 1)
                v.tensor_copy(carry[:, f, :], CS[k][:, :, TT]).then_inc(carry_ready, 1)
                dve.wait_ge(rd_ready, START + n + 1)
                if not (first and f < RING):
                    dve.wait_ge(o_used, START + n - RING + 1)
                v.tensor_tensor(O[k][:, :], AB[k][:, 0, :], er[k][:, :], ALU.mult).then_inc(o_ready, 1)

            def total(i):
                dve.wait_ge(o_used, START + (i + 1) * NF)
                dve.wait_ge(x3_ready, START + i)
                v.scalar_tensor_tensor(s[:, :], pacc[:, :], bo[:, :], xp[:, bass.ds(i, 1), 1:TT + 1].rearrange("p a t -> p (a t)"),
                                       ALU.add, ALU.add).then_inc(s_ready, 1)

            def centre(i):
                dve.wait_ge(mean_full, START + i + 1)
                v.tensor_tensor(s[:, :], s[:, :], pst[:, :], ALU.subtract).then_inc(xc_ready, 1)

            def scale(i):
                dve.wait_ge(rstd_ready, START + i + 1)
                v.tensor_tensor(xf[:, bass.ds(i * TT, TT)], s[:, :], r[:, :], ALU.mult).then_inc(x3_ready, 1)

            dve.wait_ge(s_weights, n_weights)
            v.tensor_scalar(decay[0:1, :], decay[0:1, :], 0.0, -1.0, ALU.max, ALU.mult).then_inc(dec_ready, 1)
            v.tensor_tensor(ubk[:, :], par[:, :, U_], par[:, :, BK], ALU.add)
            v.tensor_scalar(nbr[:, :], par[:, :, BR], -1.0, None, ALU.mult)
            v.memset(carry[:, :, :], 0.0)
            v.tensor_copy(t_in[:, :], t_rem[:, :])
            v.tensor_scalar(neg_w[:, :], par[:, :, DECAY], 0.0, -1.0, ALU.max, ALU.mult).then_inc(dec_ready, 1)
            dve.wait_ge(dec_ready, START + 2)
            v.tensor_tensor(later[:, :, :], neg_w[:, :].unsqueeze(2).broadcast_to([P, NF, NTILE]),
                            behind[:, :].unsqueeze(1).broadcast_to([P, NF, NTILE]), ALU.mult)
            v.tensor_copy(dec_hi[:, :], decay[:, :]).then_inc(dec_ready, 1)
            dve.wait_ge(dec_ready, START + 3)
            v.tensor_tensor(dec_lo[:, :], decay[:, :], dec_hi[:, :].bitcast(F32), ALU.subtract).then_inc(s_prep, 1)
            dve.wait_ge(s_prep, START + 1)
            dve.wait_ge(s_eps, START + 1)

            def body(i, first, last):
                for f in range(NF):
                    n = i * NF + f
                    front(f, n, i, first)
                    if f >= 2:
                        back(f - 2, n - 2, first)
                    elif not first:
                        back(f - 2 + NF, n - 2, False)
                    if not first:
                        if f == 2:
                            total(i - 1)
                        if f == 4:
                            centre(i - 1)
                        if f == 7:
                            scale(i - 1)
                    if f == 5 and not last:
                        blend(i + 1)
            blend(0)
            tiles(dve, body)
            for f in range(NF - 2, NF):
                back(f, (NTILE - 1) * NF + f, False)
            total(NTILE - 1)
            centre(NTILE - 1)
            scale(NTILE - 1)


NE, NG, I = 16, 4, 64
NPR = NE * I // P
GE = NE // NG
TOP_K, TOP_G = 4, 2
LO = 64


def moe(nc, X, OUT, cst, wts, out_dram):
    tri, low, ones, ident, mean_w, rms_w = cst
    gw, ebias, (gp_hi, gp_lo), (up_hi, up_lo), (dp_hi, dp_lo), sel, inner, below, s_weights, n_weights = wts
    with ExitStack() as ctx:
        sb, ps, sem = tensors(nc, ctx)
        eps = sb("e_eps", [P, 1])
        x_hi, x_lo = sb("e_x_hi", [P, NTILE * TT], F32R), sb("e_x_lo", [P, NTILE * TT], F32R)
        sel2 = sb("e_sel2", [P, NE * I], F32R)
        logit = [sb(f"e_logit{k}", [NE, TT]) for k in range(2)]
        comb_f, comb_t = sb("e_comb_f", [NE, TT]), sb("e_comb_t", [P, NTILE * TT], F32R)
        tok = lambda name, *n: sb(f"e_{name}", [P, NTILE * NC, *n])
        ex, sc, sfc = tok("ex", NE), tok("sc", NE), tok("sfc", NE)
        mx, mn = tok("mx", NE // 2), tok("mn", NE // 2)
        t1, t2, t3, gs = tok("t1", NG), tok("t2", NG), tok("t3", NG), tok("gs", NG)
        ggt, geq, gcnt, masked = tok("ggt", NG, NG), tok("geq", NG, NG), tok("gcnt", NG), tok("masked", NE)
        top8, above, n_above, equal, count, chosen = (tok("top8", 8), tok("above", NE), tok("n_above"), tok("equal", NE),
                                                      tok("count", NE), tok("chosen", NE))
        comb_now = sb("e_comb_now", [P, NC, NE])
        w, den, rden, comb = tok("w", NE), tok("den"), tok("rden"), tok("comb", NE)
        RING = 4
        ring = lambda name, dt=F32: [sb(f"e_{name}{k}", [P, TT], dt) for k in range(RING)]
        sg, gu, av, av_hi, av_lo = ring("sg"), ring("gu"), ring("av"), ring("av_hi", F32R), ring("av_lo", F32R)
        s, sq, r = sb("e_s", [P, TT]), sb("e_sq", [P, TT]), sb("e_r", [P, TT])
        pg = [ps(f"e_pg{k}", [P, TT]) for k in range(2)]
        pu = [ps(f"e_pu{k}", [P, TT]) for k in range(2)]
        pc, py, pm, pl = ps("e_pc", [P, TT]), ps("e_py", [P, TT]), ps("e_pm", [P, TT]), ps("e_pl", [P, TT])
        (s_eps, x_hi_ready, x_lo_ready, sel_ready, comb0, chain, lg_full, lg_ready, lt_full, ex_ready, all_ready, comb_ready, ct_full,
         cf_ready, chi_ready, ct_ready, g_full, g_read, u_full, c_full, gu_ready, av_ready, hi_ready, lo_ready, y_step, s_ready,
         mean_full, xc_ready, sq_ready, var_full, lv_ready, rstd_ready, out_ready, s_out) = [
             sem(f"e_s{i}_{n}") for i, n in enumerate(
                 "eps x_hi x_lo sel comb0 chain lg_f lg lt_f ex all comb ct_f cf chi ct g_f g_r u_f c_f gu av hi lo y s mean xc sq "
                 "var lv rstd out store".split())]
        sem.start(but=(s_out,))
        block = ctx.enter_context(nc.Block())
        xf, of = X[:, :, :].rearrange("p b t -> p (b t)"), OUT[:, :, :].rearrange("p b t -> p (b t)")

        def tiles(engine, body):
            body(0, True, False)
            with engine.Fori(1, NTILE - 1) as i:
                body(i, False, False)
            body(NTILE - 1, False, True)

        @block.sync
        def _(sp):
            with sp.Fori(0, NTILE) as i:
                sp.wait_ge(out_ready, START + i + 1)
                sp.dma_start(out_dram[:, bass.ds(i * TT, TT)], of[:, bass.ds(i * TT, TT)]).then_inc(s_out, 16)
            sp.wait_ge(s_out, 16 * NTILE)

        @block.gpsimd
        def _(pool):
            nc.gpsimd.memset(eps[:, :], LN_EPS).then_inc(s_eps, 1)
            with pool.Fori(0, NTILE) as i:
                t = bass.ds(i * TT, TT)
                pool.wait_ge(x_hi_ready, START + i + 1)
                nc.gpsimd.tensor_tensor(x_lo[:, t], xf[:, t], x_hi[:, t].bitcast(F32), ALU.subtract).then_inc(x_lo_ready, 1)

            def body(i, first, last):
                for j in range(NPR):
                    k, n = j % RING, i * NPR + j
                    pool.wait_ge(hi_ready, START + n + 1)
                    if not (first and j < RING):
                        pool.wait_ge(y_step, START + n - RING + 1)
                    nc.gpsimd.tensor_tensor(av_lo[k][:, :], av[k][:, :], av_hi[k][:, :].bitcast(F32), ALU.subtract)\
                        .then_inc(lo_ready, 1)
            tiles(pool, body)

        @block.tensor
        def _(pe):
            mm = nc.tensor.matmul

            def three(out, w_hi, w_lo, v_hi, v_lo, start, stop):
                mm(out, w_hi, v_hi, start=start, stop=False)
                mm(out, w_hi, v_lo, start=False, stop=False)
                return mm(out, w_lo, v_hi, start=False, stop=stop)

            def expert(j, n, i, first):
                k, js, x = j % 2, slice(j * P, (j + 1) * P), bass.ds(i * TT, TT)
                old = not (first and j < 2)
                if j == 0:
                    pe.wait_ge(x_lo_ready, START + i + 1)
                if old:
                    pe.wait_ge(g_read, START + n - 1)
                three(pg[k][:, :], gp_hi[:, js], gp_lo[:, js], x_hi[:, x], x_lo[:, x], True, True).then_inc(g_full, 1)
                if old:
                    pe.wait_ge(gu_ready, START + n - 1)
                three(pu[k][:, :], up_hi[:, js], up_lo[:, js], x_hi[:, x], x_lo[:, x], True, True).then_inc(u_full, 1)

            def weights(j, n, i, first):
                if j == 0:
                    pe.wait_ge(ct_ready, START + i + 1)
                if not (first and j < 1):
                    pe.wait_ge(av_ready, START + n)
                mm(pc[:, :], sel2[:, j * P:(j + 1) * P], comb_t[:, bass.ds(i * TT, TT)], start=True, stop=True).then_inc(c_full, 1)

            def collect(j, n, i):
                pe.wait_ge(lo_ready, START + n + 1)
                if j == 0 and i is not None:
                    pe.wait_ge(s_ready, START + i)
                k = j % RING
                three(py[:, :], dp_hi[:, j, :], dp_lo[:, j, :], av_hi[k][:, :], av_lo[k][:, :], j == 0, j == NPR - 1)\
                    .then_inc(y_step, 1)

            def logits(i):
                mm((pl, py)[i % 2][0:NE, :], gw[:, :], xf[:, i * TT:(i + 1) * TT], start=True, stop=True).then_inc(lg_full, 1)

            def to_tokens(i):
                pe.wait_ge(lg_ready, START + i + 1)
                for c in range(NC):
                    last = mm((pl, py)[i % 2][:, c * NE:(c + 1) * NE], logit[i % 2][:, c * Q:(c + 1) * Q], ident[0:NE, 0:NE],
                              start=True, stop=True)
                last.then_inc(lt_full, 1)

            def to_experts(i):
                pe.wait_ge(comb_ready, START + i + 1)
                for c in range(NC):
                    last = nc.tensor.transpose(pl[0:NE, c * Q:(c + 1) * Q], comb_now[:, c, :], ident[:, :])
                last.then_inc(ct_full, 1)

            def mean(i):
                pe.wait_ge(s_ready, START + i + 1)
                mm(pm[:, :], mean_w[:, :], s[:, :], start=True, stop=True).then_inc(mean_full, 1)

            def var(i):
                pe.wait_ge(sq_ready, START + i + 1)
                mm(pm[:, :], mean_w[:, :], sq[:, :], start=True, stop=True).then_inc(var_full, 1)

            pe.wait_ge(s_weights, n_weights)
            for i in range(NTILE):
                if i >= 2:
                    pe.wait_ge(ex_ready, START + i - 1)
                logits(i)
                if i % 2:
                    to_tokens(i - 1)
                    to_tokens(i)
            expert(0, 0, 0, True)
            expert(1, 1, 0, True)
            pe.wait_ge(ex_ready, START + NTILE)
            to_experts(0)
            pe.wait_ge(sel_ready, START + 1)

            def body(i, first, last):
                for j in range(NPR):
                    n = i * NPR + j
                    weights(j, n, i, first)
                    if j < NPR - 2:
                        expert(j + 2, n + 2, i, first)
                    elif not last:
                        expert(j + 2 - NPR, n + 2, i + 1, False)
                    if j >= 2:
                        collect(j - 2, n - 2, None if first else i)
                    elif not first:
                        collect(j - 2 + NPR, n - 2, None)
                    if not first and j == 2:
                        mean(i - 1)
                    if not first and j == 4:
                        var(i - 1)
                    if not last and j == (NPR - 1 if first else 4):
                        pe.wait_ge(cf_ready, START + i + 1)
                        to_experts(i + 1)
            tiles(pe, body)
            for j in range(NPR - 2, NPR):
                collect(j, (NTILE - 1) * NPR + j, None)
            mean(NTILE - 1)
            var(NTILE - 1)

        @block.scalar
        def _(act):
            a = nc.scalar.activation

            def silu(j, n, first):
                k = j % RING
                act.wait_ge(g_full, START + n + 1)
                if not (first and j < RING):
                    act.wait_ge(gu_ready, START + n - RING + 1)
                a(sg[k][:, :], pg[j % 2][:, :], ACT.Silu).then_inc(g_read, 1)

            def high(j, n, first):
                k = j % RING
                act.wait_ge(av_ready, START + n + 1)
                if not (first and j < RING):
                    act.wait_ge(y_step, START + n - RING + 1)
                a(av_hi[k][:, :], av[k][:, :], ACT.Copy).then_inc(hi_ready, 1)

            def take_logits(i):
                act.wait_ge(lg_full, START + i + 1)
                if i >= 2:
                    act.wait_ge(lt_full, START + i - 1)
                a(logit[i % 2][:, :], (pl, py)[i % 2][0:NE, :], ACT.Copy).then_inc(lg_ready, 1)

            def exp_logits(i):
                act.wait_ge(lt_full, START + i + 1)
                a(ex[:, i * NC:(i + 1) * NC, :].rearrange("p c e -> p (c e)"), (pl, py)[i % 2][:, 0:NC * NE], ACT.Exp, scale=-1.0)\
                    .then_inc(ex_ready, 1)

            def take_weights(i):
                act.wait_ge(ct_full, START + i + 1)
                act.wait_ge(ct_ready, START + i)
                a(comb_f[:, :], pl[0:NE, :], ACT.Copy).then_inc(cf_ready, 1)
                act.wait_ge(cf_ready, START + i + 1)
                a(comb_t[0:NE, bass.ds(i * TT, TT)], comb_f[:, :], ACT.Copy).then_inc(chi_ready, 1)

            def square(i):
                act.wait_ge(xc_ready, START + i + 1)
                a(sq[:, :], s[:, :], ACT.Square).then_inc(sq_ready, 1)

            def rstd(i):
                act.wait_ge(var_full, START + i + 1)
                a(r[:, :], pm[:, :], ACT.Ln, bias=eps[:, :]).then_inc(lv_ready, 1)
                act.wait_ge(lv_ready, START + i + 1)
                a(r[:, :], r[:, :], ACT.Exp, scale=-0.5).then_inc(rstd_ready, 1)

            act.preload_act_table_set("natural_log_exp_and_others")
            act.wait_ge(s_eps, START + 1)
            for i in range(0, NTILE, 2):
                take_logits(i)
                take_logits(i + 1)
                if i == 0:
                    a(x_hi[:, 0:TT], xf[:, 0:TT], ACT.Copy).then_inc(x_hi_ready, 1)
                exp_logits(i)
                exp_logits(i + 1)
            with act.Fori(1, NTILE) as i:
                t = bass.ds(i * TT, TT)
                a(x_hi[:, t], xf[:, t], ACT.Copy).then_inc(x_hi_ready, 1)
            act.wait_ge(s_weights, n_weights)
            act.wait_ge(comb0, START + 2)
            a(sel2[0:NE, :], sel[:, :], ACT.Copy)
            a(sel2[LO:LO + NE, :], sel[:, :], ACT.Copy).then_inc(sel_ready, 1)
            act.preload_act_table_set("silu_and_others")
            silu(0, 0, True)
            silu(1, 1, True)
            take_weights(0)

            def body(i, first, last):
                for j in range(NPR):
                    n = i * NPR + j
                    if j < NPR - 2:
                        silu(j + 2, n + 2, first)
                    elif not last:
                        silu(j + 2 - NPR, n + 2, False)
                    high(j, n, first)
                    if not first and j == 3:
                        square(i - 1)
                    if not first and j == 5:
                        act.preload_act_table_set("natural_log_exp_and_others")
                        rstd(i - 1)
                        act.preload_act_table_set("silu_and_others")
                    if not last and j == (NPR - 1 if first else 4):
                        take_weights(i + 1)
            tiles(act, body)
            act.preload_act_table_set("natural_log_exp_and_others")
            square(NTILE - 1)
            rstd(NTILE - 1)

        @block.vector
        def _(dve):
            v = nc.vector
            STEPS = 29
            every = (ex, sc, sfc, mx, mn, t1, t2, t3, gs, gcnt, masked, top8, above, equal, count, chosen, w, comb, n_above, den, rden, ggt, geq)

            def route(group, lo, hi):
                n, k, chunks = [0], (hi - lo) * NC, slice(lo * NC, hi * NC)
                ex, sc, sfc, mx, mn, t1, t2, t3, gs, gcnt, masked, top8, above, equal, count, chosen, w, comb = (
                    x[:, chunks, :] for x in every[:18])
                n_above, den, rden = (x[:, chunks] for x in every[18:21])
                ggt, geq = (x[:, chunks, :, :] for x in every[21:])

                def step(ins):
                    n[0] += 1
                    ins.then_inc(chain, 1)
                    dve.wait_ge(chain, START + group * STEPS + n[0])

                dve.wait_ge(ex_ready, START + hi)
                step(v.tensor_scalar(ex, ex, 1.0, None, ALU.add))
                yield
                step(v.reciprocal(sc, ex))
                yield
                step(v.tensor_tensor(sfc, sc, ebias[:, :].unsqueeze(1).broadcast_to([P, k, NE]), ALU.add))
                yield
                pairs = sfc.rearrange("p c (n two) -> p c n two", two=2)
                step(v.tensor_tensor(mx, pairs[:, :, :, 0], pairs[:, :, :, 1], ALU.max))
                yield
                step(v.tensor_tensor(mn, pairs[:, :, :, 0], pairs[:, :, :, 1], ALU.min))
                yield
                hi = mx.rearrange("p c (g two) -> p c g two", two=2)
                lo = mn.rearrange("p c (g two) -> p c g two", two=2)
                step(v.tensor_tensor(t1, hi[:, :, :, 0], hi[:, :, :, 1], ALU.max))
                yield
                step(v.tensor_tensor(t2, hi[:, :, :, 0], hi[:, :, :, 1], ALU.min))
                yield
                step(v.tensor_tensor(t3, lo[:, :, :, 0], lo[:, :, :, 1], ALU.max))
                yield
                step(v.tensor_tensor(t2, t2, t3, ALU.max))
                yield
                step(v.tensor_tensor(gs, t1, t2, ALU.add))
                yield
                other = gs.unsqueeze(2).broadcast_to([P, k, NG, NG])
                own = gs.unsqueeze(3).broadcast_to([P, k, NG, NG])
                before = below[:, :, :].unsqueeze(1).broadcast_to([P, k, NG, NG])
                step(v.tensor_tensor(geq, other, own, ALU.is_equal))
                yield
                step(v.tensor_tensor(ggt, other, own, ALU.is_gt))
                yield
                step(v.tensor_tensor(geq, geq, before, ALU.mult))
                yield
                step(v.tensor_tensor(ggt, ggt, geq, ALU.add))
                yield
                step(v.tensor_reduce(gcnt, ggt, AX.X, ALU.add))
                yield
                step(v.tensor_scalar(gcnt, gcnt, TOP_G - 0.5, None, ALU.is_lt))
                yield
                step(v.tensor_tensor(masked.rearrange("p c (g e) -> p c g e", g=NG), sfc.rearrange("p c (g e) -> p c g e", g=NG),
                                     gcnt.unsqueeze(3).broadcast_to([P, k, NG, GE]), ALU.mult))
                yield
                v.memset(n_above, 0.0)
                for c in range(k):
                    last = v.max(top8[:, c, :], masked[:, c, :])
                step(last)
                yield
                kth = top8[:, :, TOP_K - 1:TOP_K].broadcast_to([P, k, NE])
                step(v.tensor_tensor(above, masked, kth, ALU.is_gt))
                yield
                step(v.tensor_reduce(n_above, above, AX.X, ALU.add))
                yield
                step(v.tensor_tensor(equal, masked, kth, ALU.is_equal))
                yield
                flat = lambda x: x.rearrange("p c e -> p (c e)")
                step(v.tensor_tensor_scan(flat(count), inner[:, 0:k * NE], flat(equal), 0.0, ALU.mult, ALU.add))
                yield
                step(v.tensor_tensor(count, count, n_above.unsqueeze(2).broadcast_to([P, k, NE]), ALU.add))
                yield
                step(v.scalar_tensor_tensor(chosen, count, TOP_K + 0.5, equal, ALU.is_lt, ALU.mult))
                yield
                step(v.tensor_tensor(chosen, chosen, above, ALU.add))
                yield
                step(v.tensor_tensor(w, sc, chosen, ALU.mult))
                yield
                step(v.tensor_reduce(den, w, AX.X, ALU.add))
                yield
                step(v.tensor_scalar(den, den, 1e-20, None, ALU.add))
                yield
                step(v.reciprocal(rden, den))
                yield
                v.tensor_tensor(comb, w, rden.unsqueeze(2).broadcast_to([P, k, NE]), ALU.mult).then_inc(all_ready, 1)
                assert n[0] == STEPS, n[0]

            def choose(i, first):
                dve.wait_ge(all_ready, START + (1 if first else 2))
                dve.wait_ge(ct_full, START + i)
                v.tensor_copy(comb_now[:, :, :], comb[:, bass.ds(i * NC, NC), :]).then_inc(comb_ready, 1)

            def low_weights(i):
                dve.wait_ge(chi_ready, START + i + 1)
                t = bass.ds(i * TT, TT)
                v.tensor_tensor(comb_t[LO:LO + NE, t], comb_f[:, :], comb_t[0:NE, t].bitcast(F32), ALU.subtract).then_inc(ct_ready, 1)

            def gate(j, n, first):
                k = j % RING
                dve.wait_ge(g_read, START + n + 1)
                dve.wait_ge(u_full, START + n + 1)
                v.tensor_tensor(gu[k][:, :], sg[k][:, :], pu[j % 2][:, :], ALU.mult).then_inc(gu_ready, 1)

            def weigh(j, n, first):
                k = j % RING
                dve.wait_ge(gu_ready, START + n + 1)
                dve.wait_ge(c_full, START + n + 1)
                if not (first and j < RING):
                    dve.wait_ge(lo_ready, START + n - RING + 1)
                v.tensor_tensor(av[k][:, :], gu[k][:, :], pc[:, :], ALU.mult).then_inc(av_ready, 1)

            def total(i):
                dve.wait_ge(y_step, START + (i + 1) * NPR)
                v.tensor_tensor(s[:, :], py[:, :], xf[:, bass.ds(i * TT, TT)], ALU.add).then_inc(s_ready, 1)

            def centre(i):
                dve.wait_ge(mean_full, START + i + 1)
                v.tensor_tensor(s[:, :], s[:, :], pm[:, :], ALU.subtract).then_inc(xc_ready, 1)

            def scale(i):
                dve.wait_ge(rstd_ready, START + i + 1)
                v.tensor_tensor(of[:, bass.ds(i * TT, TT)], s[:, :], r[:, :], ALU.mult).then_inc(out_ready, 1)

            v.memset(comb_t[:, :].bitcast(F32), 0.0).then_inc(comb0, 1)
            v.memset(sel2[:, :].bitcast(F32), 0.0).then_inc(comb0, 1)
            dve.wait_ge(s_weights, n_weights)
            for _ in route(0, 0, 1):
                pass
            choose(0, True)
            gate(0, 0, True)
            low_weights(0)

            def body(i, first, last):
                steps = route(1, 1, NTILE) if first else iter(())
                for j in range(NPR):
                    n = i * NPR + j
                    weigh(j, n, first)
                    for _ in range(2):
                        next(steps, None)
                    if j < NPR - 1:
                        gate(j + 1, n + 1, first)
                    elif not last:
                        gate(0, n + 1, False)
                    if j < NPR - 1:
                        for _ in range(3):
                            next(steps, None)
                    if not first:
                        if j == 1:
                            total(i - 1)
                        if j == 2:
                            centre(i - 1)
                        if j == 6:
                            scale(i - 1)
                    if not last and j == (NPR - 1 if first else 3):
                        for _ in steps:
                            pass
                        choose(i + 1, False)
                    if not last and j == (NPR - 1 if first else 5):
                        low_weights(i + 1)
            tiles(dve, body)
            total(NTILE - 1)
            centre(NTILE - 1)
            scale(NTILE - 1)


def constants():
    i = np.arange(P)
    le, gt = i[:, None] <= i[None, :], i[:, None] > i[None, :]
    parts = [le, gt, np.ones((P, P)), np.eye(P), np.full((P, P), 1 / D), np.full((P, P), 1 / DI)]
    return np.stack(parts, 1).astype(np.float32)


def program(nc, d):
    with ExitStack() as ctx:
        def sb(name, shape, dt=F32, scope=ctx):
            return scope.enter_context(nc.sbuf_tensor(name, shape, dt))

        full = lambda x: x[tuple(slice(None) for _ in x.shape)]
        XP = sb("XP", [P, NTILE, TP])
        C = sb("C", [P, 6, P])
        cst = tuple(C[:, k, :] for k in range(6))
        late = ["wr", "wk", "wv", "wo", "decay", "t_rem", "w_par", "bo", "keep", "behind", "gw", "ebias", "sel", "inner", "below"]
        split = ["gp", "eup", "dp"]
        W = {n: sb("W_" + n, list(d[n].shape)) for n in late}
        halves = {n: (sb(f"W_{n}_hi", list(d[n].shape), F32R), sb(f"W_{n}_lo", list(d[n].shape), F32R)) for n in split}
        s_weights = ctx.enter_context(nc.semaphore("s_weights"))

        with ExitStack() as early:
            XH = sb("XH", [P, NB, (1 + NL) * T], scope=early)
            for n in ["f_up", "f_down"] + split:
                W[n] = sb("W_" + n, list(d[n].shape), scope=early)
            n_weights = 16 * len(W)
            mamba(nc, XH, cst, d["x"], d["win"], d["wout"], d["par"], d["row"], d["again"], [(C[:, :, :], d["cst"])],
                  [(full(w), d[n]) for n, w in W.items()], s_weights)
            ffn(nc, XH[:, :, 0:T], XH[:, :, NL * T:], XP, cst, (W["f_up"], W["f_down"], [(full(W[n]), *map(full, halves[n])) for n in split], s_weights, n_weights))
        X, H = sb("X", [P, NB, T]), sb("H", [P, NB, T])
        wkv(nc, X, XP, H, cst, tuple(W[n] for n in ("wr", "wk", "wv", "wo", "decay", "t_rem", "w_par", "bo", "keep", "behind"))
            + (s_weights, n_weights))
        moe(nc, X, H, cst, (W["gw"], W["ebias"], *(halves[n] for n in split), W["sel"], W["inner"], W["below"], s_weights, n_weights),
            d["out"])


def kernel(**inputs):
    from concourse import bacc
    from concourse.bass_utils import run_bass_kernel_spmd

    z = {k: np.asarray(v) for k, v in inputs.items()}
    f = np.ascontiguousarray
    feat = lambda x: f(x.reshape(-1, P).T)
    blocks = lambda w: f(w.T.reshape(-1, P, w.shape[0]).transpose(1, 0, 2))
    its = lambda x: np.repeat(x, NT, axis=0)
    per = lambda x: x.reshape(NL, -1, P).transpose(0, 2, 1)
    arrays = {
        "x": feat(z["L0_attn_x"]).reshape(P, NB, T),
        "win": its(f(z["L0_attn_in_proj_w"].transpose(0, 2, 1))),
        "wout": its(f(z["L0_attn_out_proj_w"].transpose(0, 2, 1).reshape(NL, 2, P, D).transpose(0, 2, 1, 3))),
        "par": f(its(np.concatenate([
            per(z["L0_attn_ln_w"]), per(z["L0_attn_ln_b"]),
            z["L0_attn_conv_w"].reshape(NL, 3, P, DC).transpose(0, 2, 1, 3).reshape(NL, P, 3 * DC),
            per(z["L0_attn_conv_b"]), per(np.repeat(z["L0_attn_D"], DS, axis=1)), per(z["L0_attn_rms_w"])], 2)).transpose(1, 0, 2)),
        "row": f(np.broadcast_to(its(np.stack([z["L0_attn_dt_bias"], z["L0_attn_A_log"]], 1)).transpose(1, 0, 2), (P, 2, N_IT, NH))),
        "again": f(np.broadcast_to(np.arange(N_IT + 1) % NT > 0, (P, N_IT + 1)).astype(np.float32)),
        "cst": constants(),
        "f_up": f(z["L0_ffn_w_up"].T), "f_down": blocks(z["L0_ffn_w_down"]),
        "wr": f(z["L1_attn_Wr"].T), "wk": f(z["L1_attn_Wk"].T), "wv": f(z["L1_attn_Wv"].T), "wo": blocks(z["L1_attn_Wo"]),
        "decay": f(np.stack([z["L1_attn_time_decay"], z["L1_attn_bk"]])),
        "t_rem": np.stack([TT - 1 - np.arange(TT), np.ones(TT)]).astype(np.float32),
        "w_par": f(np.stack([z["L1_attn_U"], z["L1_attn_bk"], z["L1_attn_br"], z["L1_attn_bv"],
                             z["L1_attn_time_decay"]], -1).reshape(NF, P, 5).transpose(1, 0, 2)),
        "bo": f(z["L1_attn_bo"][:, None]),
        "keep": f(np.broadcast_to(np.arange(NTILE) % NT > 0, (P, NTILE)).astype(np.float32)),
        "behind": f(np.broadcast_to(T - TT * (np.arange(NTILE) % NT + 1), (P, NTILE)).astype(np.float32)),
        "gw": f(z["L1_ffn_gate_weight"].T), "ebias": f(np.broadcast_to(z["L1_ffn_e_bias"], (P, NE))),
        "gp": f(z["L1_ffn_gate_proj"].reshape(NE * I, D).T), "eup": f(z["L1_ffn_up_proj"].reshape(NE * I, D).T),
        "dp": f(z["L1_ffn_down_proj"].transpose(0, 2, 1).reshape(NPR, P, D).transpose(1, 0, 2)),
        "sel": f(np.repeat(np.eye(NE), I, axis=1).astype(np.float32)),
        "inner": f(np.broadcast_to(np.arange(NTILE * NC * NE) % NE > 0, (P, NTILE * NC * NE)).astype(np.float32)),
        "below": f(np.broadcast_to(np.arange(NG)[:, None] > np.arange(NG)[None, :], (P, NG, NG)).astype(np.float32)),
    }
    nc = bacc.Bacc("TRN2", target_bir_lowering=False, num_devices=1)
    d = {n: nc.dram_tensor(f"in_{n}", a.shape, mybir.dt.from_np(a.dtype), kind="ExternalInput").ap() for n, a in arrays.items()}
    d["out"] = nc.dram_tensor("out_y", (P, NB * T), F32, kind="ExternalOutput").ap()
    program(nc, d)
    r = run_bass_kernel_spmd(nc, [{f"in_{n}": a for n, a in arrays.items()}], core_ids=[0])
    y = np.asarray(r.results[0]["out_y"])
    return f(y.T.reshape(NB, T, D))
```

```python
import math
from contextlib import ExitStack

import numpy as np
import concourse.bass as bass
from concourse import mybir

F32 = mybir.dt.float32
F32R = mybir.dt.float32r
ACT = mybir.ActivationFunctionType
ALU = mybir.AluOpType
AX = mybir.AxisListType

P = 128
D = 128
NB = 2
T = 1024
TT = 512
NT = T // TT
NL = 2
DI = 256
DS = 64
NH = DI // DS
Q = 128
NC = TT // Q
DC = 4
LN_EPS = 1e-5
START = 1
N_IT = NL * NT
C_LNW, C_LNB, C_CW, C_CB, C_D, C_RW, N_PAR = 0, 1, 2, 14, 17, 19, 21


def tensors(nc, ctx):
    sems = []

    def give_back():
        nc.clear_and_free_semaphores(sems)
        nc.all_engine_barrier()

    ctx.callback(give_back)

    def sb(name, shape, dt=F32):
        return ctx.enter_context(nc.sbuf_tensor(name, shape, dt))

    def ps(name, shape, dt=F32):
        return ctx.enter_context(nc.psum_tensor(name, shape, dt))

    def sem(name):
        sems.append(nc.alloc_semaphore(name=name))
        return sems[-1]

    def start(but=()):
        engines = (nc.vector, nc.scalar, nc.tensor, nc.gpsimd, nc.sync)
        for i, s in enumerate(x for x in sems if not any(x is y for y in but)):
            engines[i % len(engines)].sem_inc(s, START)
        nc.all_engine_barrier()
    sem.start = start
    return sb, ps, sem


def lag(n, k):
    return max(n - k, 0) if isinstance(n, int) else n - k


def mamba(nc, XH, cst, x_dram, win_d, wout_d, par_d, row_d, again_d, c_dram, later=(), s_later=None):
    with ExitStack() as ctx:
        sb, ps, sem = tensors(nc, ctx)
        tri, low, ones, ident, mean_w, rms_w = cst
        low_r = sb("m_low_r", [P, P], F32R)
        win = sb("m_win", [P, 2 * DI + 2 * DS + NH])
        wout_in, wout = sb("m_wout_in", [P, 2, D]), sb("m_wout", [P, 2, D])
        par = sb("m_par", [P, N_IT, N_PAR])
        row = sb("m_row", [P, 2, N_IT, NH])
        arow = sb("m_arow", [P, N_IT, NH])
        again = sb("m_again", [P, N_IT + 1])
        eps = sb("m_eps", [P, 1])
        xc, sq, rstd, u = sb("m_xc", [P, TT]), sb("m_sq", [P, TT]), sb("m_rstd", [P, TT]), sb("m_u", [P, TT])
        acc = sb("m_acc", [P, 3, TT])
        raw, neg, l1p = sb("m_raw", [P, NC, NH]), sb("m_neg", [P, NC, NH]), sb("m_l1p", [P, NC, NH])
        two = lambda name, shape, dt=F32: [sb(f"m_{name}{b}", shape, dt) for b in range(NB)]
        pre = two("pre", [P, 3, DC - 1 + TT])
        xs, bt, ct, zs = two("xs", [P, 2, TT]), two("bt", [DS, TT]), two("ct", [DS, TT]), two("zs", [P, 2, TT])
        dt, a, decay, ddt = two("dt", [P, NC, NH]), two("a", [P, NC, NH]), two("decay", [P, 3, NC, NH]), two("ddt", [P, NC, NH])
        a_hi, a_lo = two("a_hi", [P, NC, NH], F32R), two("a_lo", [P, NC, NH], F32R)
        state, y = two("state", [DS, NH, DS]), two("y", [P, 2, TT])
        sq2, rstd2, o = sb("m_sq2", [P, 2, TT]), sb("m_rstd2", [P, TT]), sb("m_o", [P, TT])
        par2 = lambda name, shape, dt=F32: [sb(f"m_{name}{k}", shape, dt) for k in range(2)]
        st_hi, st_lo = par2("st_hi", [P, NH, Q], F32R), par2("st_lo", [P, NH, Q], F32R)
        L, gm, mt = par2("L", [P, NH, Q]), par2("gm", [P, Q]), par2("mt", [P, NH, Q])
        xdt, xdec, btok = par2("xdt", [P, NH, DS]), par2("xdec", [P, NH, DS]), par2("btok", [P, DS])
        yo, yt = par2("yo", [P, NH, DS]), par2("yt", [P, NH * DS])
        faded = sb("m_faded", [DS, NH, DS])

        bank = [ps(f"m_bank{k}", [P, TT]) for k in range(3)]
        p_diff = ps("m_pdiff", [P, NH, Q])
        p_gt = ps("m_pgt", [P, 512])
        p_y = ps("m_py", [P, 2, NH, DS])
        p_ds = ps("m_pds", [DS, NH * DS])
        p_yt = ps("m_pyt", [P, 2, 2, Q])
        p_g = p_gt[:, 0:Q]
        p_xtok = p_gt[:, Q:Q + NH * DS]
        p_btok = p_gt[:, Q + NH * DS:Q + NH * DS + DS]
        BANK = dict(mean=0, var=1, dt=2, x1=0, bc=1, x0=2, sums=0, z0=2, ms=0, out=1, z1=0)
        place = {n: bank[k][:, :] for n, k in BANK.items()}
        p_dt, p_sums = bank[BANK["dt"]][:, 0:NC * NH], bank[BANK["sums"]][:, 0:3 * NC * NH]
        PARTS = (("x1", DI + P, 1), ("bc", 2 * DI, 2), ("x0", DI, 0))

        s_const, s_x0, s_x, s_par, s_win, s_wout, s_eps, s_arow, s_prep, s_low = (sem("m_s_" + n) for n in (
            "const", "x0", "x", "par", "win", "wout", "eps", "arow", "prep", "low"))
        (mean_full, xc_ready, sq_ready, var_full, lnv_ready, rstd_ready, u1_ready, u_ready, dt_full, raw_ready, neg_ready,
         e_ready, l1p_ready, dt_ready, a_ready, ahi_ready, alo_ready, cum_full, decay_ready, ddt_ready, x_full, z0_full, z1_full,
         z0_read, z1_read, halo_ready, silu_done, y_ready, sq2_ready, ms_full, ms_read, rstd2_ready, out_full, o_ready,
         h_ready) = (sem("m_" + n) for n in (
            "mean_f xc_r sq_r var_f lnv_r rstd_r u1_r u_r dt_f raw_r neg_r e_r l1p_r dt_r a_r ahi_r alo_r cum_f decay_r "
            "ddt_r x_f z0_f z1_f z0_read z1_read halo_r silu_d y_r sq2_r ms_f ms_read rstd2_r out_f o_r h_r").split())
        x_read, conv_step = sem("m_x_read"), sem("m_conv_s")
        (steps_ready, diff_full, L_ready, gt_full, gt_free, gm_ready, mt_ready, y_full, ds_full, faded_ready, yo_ready,
         yt_ready, pyt_full) = (sem("m_" + n) for n in (
            "steps_r diff_f L_r gt_f gt_free gm_r mt_r y_f ds_f faded_r yo_r yt_r pyt_f").split())
        pyt_free = sem("m_pyt_free")
        state_ready = sem("m_state_r")
        n_const, n_x, N_PARS = 16 * len(c_dram), 16 * NB, 16 * 3

        def heads(x):
            return x.unsqueeze(2).broadcast_to([x.shape[0], NH, DS])

        def flat(x):
            return x.rearrange("p a n -> p (a n)")

        def pars(it, col):
            return flat(par[:, bass.ds(it, 1), col:col + 1])

        def tile_in(b, it):
            return XH[:, b, bass.ds(it * TT, TT)]

        def tile_out(b, it):
            return XH[:, b, bass.ds((it + NT) * TT, TT)]

        def tiles(engine, body, finish):
            def step(it, first, last):
                for b in range(NB):
                    nxt = (b + 1, it) if b + 1 < NB else None if last else (0, it + 1)
                    prv = (b - 1, it) if b else None if first else (NB - 1, it - 1)
                    body(it * NB + b, (b, it), nxt, prv)
            step(0, True, False)
            with engine.Fori(1, N_IT - 1) as it:
                step(it, False, False)
            step(N_IT - 1, False, True)
            finish(N_IT * NB, (NB - 1, N_IT - 1))

        sem.start(but=(s_const, s_x0, s_x, s_par, s_win, s_wout))
        block = ctx.enter_context(nc.Block())

        @block.sync
        def _(sp):
            sp.dma_start(XH[:, 0, 0:TT], x_dram[:, 0, 0:TT]).then_inc(s_x0, 16)
            for dst, src in c_dram:
                sp.dma_start(dst, src).then_inc(s_const, 16)
            for dst, src in ((par[:, :, :], par_d), (row[:, :, :, :], row_d), (again[:, :], again_d)):
                sp.dma_start(dst, src).then_inc(s_par, 16)
            sp.dma_start(win[:, :], win_d[0]).then_inc(s_win, 16)
            sp.dma_start(XH[:, 0, TT:T], x_dram[:, 0, TT:]).then_inc(s_x, 16)
            for b in range(1, NB):
                sp.dma_start(XH[:, b, 0:T], x_dram[:, b, :]).then_inc(s_x, 16)
            sp.dma_start(wout_in[:, :, :], wout_d[0]).then_inc(s_wout, 16)
            for dst, src in later:
                sp.dma_start(dst, src).then_inc(s_later, 16)
            with sp.Fori(1, N_IT) as it:
                sp.wait_ge(z1_full, START + NB * it)
                sp.dma_start(win[:, :], win_d[bass.ds(it, 1)].rearrange("a p n -> (a p) n")).then_inc(s_win, 16)
                sp.wait_ge(s_prep, START + it)
                sp.dma_start(wout_in[:, :, :], wout_d[bass.ds(it, 1)].rearrange("a p k n -> (a p) k n")).then_inc(s_wout, 16)

        @block.gpsimd
        def _(pool):
            mul = lambda out, x, w: nc.gpsimd.tensor_tensor(out, x, w, ALU.mult)

            def halves(m, b):
                pool.wait_ge(ahi_ready, START + m + 1)
                nc.gpsimd.tensor_tensor(a_lo[b][:, :, :], a[b][:, :, :], a_hi[b][:, :, :].bitcast(F32), ALU.subtract)\
                    .then_inc(alo_ready, 1)
                pool.wait_ge(alo_ready, START + m + 1)

            def steps(g, b, c):
                pool.wait_ge(diff_full, START + lag(g, 1))
                t3 = tri[:, :].unsqueeze(1).broadcast_to([P, NH, Q])
                for x, out in ((a_hi, st_hi), (a_lo, st_lo)):
                    last = mul(out[c % 2][:, :, :], x[b][:, c, :].bitcast(F32).unsqueeze(2).broadcast_to([P, NH, Q]), t3)
                last.then_inc(steps_ready, 1)

            def masked(g, k):
                pool.wait_ge(gm_ready, START + g + 1)
                pool.wait_ge(L_ready, START + g + 1)
                pool.wait_ge(y_full, START + lag(g, 1))
                mul(mt[k][:, :, :], gm[k][:, :].unsqueeze(1).broadcast_to([P, NH, Q]), L[k][:, :, :]).then_inc(mt_ready, 1)

            def fade(m, b, c):
                pool.wait_ge(state_ready, START + m * (NC + 1) + 1 + c)
                mul(faded[:, :, :], state[b][:, :, :], heads(decay[b][0:DS, 2, c, :])).then_inc(faded_ready, 1)

            def residual(m, b, it):
                pool.wait_ge(o_ready, START + m + 1)
                nc.gpsimd.tensor_tensor(tile_out(b, it), tile_in(b, it), o[:, :], ALU.add).then_inc(h_ready, 1)

            nc.gpsimd.memset(eps[:, :], LN_EPS).then_inc(s_eps, 1)
            pool.wait_ge(s_const, n_const)
            pool.wait_ge(s_x0, 16)
            halves(0, 0)
            steps(0, 0, 0)
            steps(1, 0, 1)
            masked(0, 0)

            def body(m, now, nxt, prv):
                b, g = now[0], m * NC
                for c in range(NC):
                    fade(m, b, c)
                    if c < NC - 2:
                        steps(g + c + 2, b, c + 2)
                    if c < NC - 1:
                        masked(g + c + 1, (c + 1) % 2)
                    if c >= NC - 2 and nxt:
                        if c == NC - 2:
                            halves(m + 1, nxt[0])
                        steps(g + c + 2, nxt[0], c + 2 - NC)
                    if c == NC - 1:
                        if nxt:
                            masked(g + NC, 0)
                        if prv:
                            residual(m - 1, *prv)

            def finish(m, prv):
                residual(m - 1, *prv)
            pool.wait_ge(s_x, n_x)
            tiles(pool, body, finish)

        @block.tensor
        def _(pe):
            mm = nc.tensor.matmul

            def mean(m, b, it):
                pe.wait_ge(z1_read, START + m)
                pe.wait_ge(h_ready, START + lag(m, NB * NT - 1))
                mm(place["mean"], mean_w[:, :], tile_in(b, it), start=True, stop=True).then_inc(mean_full, 1)

            def var(m):
                pe.wait_ge(o_ready, START + lag(m, 2))
                pe.wait_ge(sq_ready, START + m + 1)
                mm(place["var"], mean_w[:, :], sq[:, :], start=True, stop=True).then_inc(var_full, 1)

            def project(name, lo, full):
                mm(place[name], win[:, lo:lo + P], u[:, :], start=True, stop=True).then_inc(full, 1)

            def project_dt(m, b, it):
                pe.wait_ge(u_ready, START + m + 1)
                if b == 0:
                    pe.wait_ge(s_win, 16 * (it + 1))
                pe.wait_ge(z0_read, START + m)
                for c in range(NC):
                    last = mm(p_dt[:, c * NH:(c + 1) * NH], u[:, c * Q:(c + 1) * Q], win[:, 2 * DI + 2 * DS:],
                              start=True, stop=True)
                last.then_inc(dt_full, 1)

            def project_x(m, i):
                if i == 2:
                    pe.wait_ge(raw_ready, START + m + 1)
                project(*PARTS[i][0:2], x_full)

            def project_z0(m):
                pe.wait_ge(x_read, START + 3 * m + 3)
                project("z0", 0, z0_full)

            def project_z1(m):
                pe.wait_ge(decay_ready, START + m + 1)
                pe.wait_ge(ms_read, START + lag(m, 1))
                project("z1", P, z1_full)

            def sums(m, b):
                pe.wait_ge(a_ready, START + m + 1)
                pe.wait_ge(x_read, START + 3 * m + 1)
                for k, w in enumerate((tri, low, ones)):
                    last = mm(p_sums[:, k * NC * NH:(k + 1) * NC * NH], w[:, :], a[b][:, :, :].rearrange("p c h -> p (c h)"),
                              start=True, stop=True)
                last.then_inc(cum_full, 1)

            def differences(g, c):
                pe.wait_ge(steps_ready, START + g + 1)
                pe.wait_ge(L_ready, START + g)
                mm(p_diff[:, :, :], low_r[:, :], st_hi[c % 2][:, :, :], start=True, stop=False)
                mm(p_diff[:, :, :], low_r[:, :], st_lo[c % 2][:, :, :], start=False, stop=True).then_inc(diff_full, 1)

            def chunk_front(g, m, b, c):
                q = slice(c * Q, (c + 1) * Q)
                pe.wait_ge(gt_free, START + g)
                if c == 0:
                    pe.wait_ge(silu_done, START + m + 1)
                mm(p_g, bt[b][:, q], ct[b][:, q], start=True, stop=True)
                for k in range(2):
                    nc.tensor.transpose(p_xtok[:, k * P:(k + 1) * P], xs[b][:, k, q], ident[:, :])
                nc.tensor.transpose(p_btok, bt[b][:, q], ident[0:DS, 0:DS]).then_inc(gt_full, 1)

            def chunk_back(g, m, b, c):
                q = slice(c * Q, (c + 1) * Q)
                pe.wait_ge(yt_ready, START + g)
                pe.wait_ge(state_ready, START + m * (NC + 1) + 1 + c)
                mm(p_y[:, 1, :, :], ct[b][:, q], state[b][:, :, :], start=True, stop=True)
                pe.wait_ge(gt_free, START + g + 1)
                pe.wait_ge(mt_ready, START + g + 1)
                for h in range(NH):
                    last = mm(p_y[:, 0, h, :], mt[c % 2][:, h, :], xdt[c % 2][:, h, :], start=True, stop=True)
                last.then_inc(y_full, 1)
                mm(p_ds[:, :], btok[c % 2][:, :], xdec[c % 2][:, :, :], start=True, stop=True).then_inc(ds_full, 1)

            def turn(g, pair, c):
                pe.wait_ge(yt_ready, START + g + 1)
                if c % 2 == 0:
                    pe.wait_ge(pyt_free, START + pair)
                for k in range(2):
                    last = nc.tensor.transpose(p_yt[:, k, c % 2, :], yt[c % 2][:, k * P:(k + 1) * P], ident[:, :])
                last.then_inc(pyt_full, 1)

            def mean_square(m, bank_left):
                pe.wait_ge(*bank_left)
                pe.wait_ge(sq2_ready, START + m + 1)
                for k in range(2):
                    last = mm(place["ms"], rms_w[:, :], sq2[:, k, :], start=(k == 0), stop=(k == 1))
                last.then_inc(ms_full, 1)

            def project_out(m, b, it, bank_left):
                pe.wait_ge(*bank_left)
                if b == 0:
                    pe.wait_ge(s_prep, START + it + 1)
                for k in range(2):
                    last = mm(place["out"], wout[:, k, :], y[b][:, k, :], start=(k == 0), stop=(k == 1))
                last.then_inc(out_full, 1)

            pe.wait_ge(s_const, n_const)
            pe.wait_ge(s_x0, 16)
            pe.wait_ge(s_low, START + 1)
            mean(0, 0, 0)
            var(0)
            project_dt(0, 0, 0)
            for i in range(3):
                project_x(0, i)
            sums(0, 0)
            project_z0(0)
            project_z1(0)
            differences(0, 0)
            chunk_front(0, 0, 0, 0)

            def body(m, now, nxt, prv):
                b, g = now[0], m * NC
                if nxt:
                    mean(m + 1, *nxt)
                differences(g + 1, 1)
                chunk_front(g + 1, m, b, 1)
                chunk_back(g, m, b, 0)
                if prv:
                    turn(g - 1, m * 2 - 1, NC - 1)
                if nxt:
                    var(m + 1)
                differences(g + 2, 2)
                chunk_front(g + 2, m, b, 2)
                chunk_back(g + 1, m, b, 1)
                turn(g, m * 2, 0)
                if nxt:
                    project_dt(m + 1, *nxt)
                    project_x(m + 1, 0)
                differences(g + 3, 3)
                chunk_front(g + 3, m, b, 3)
                if nxt:
                    project_x(m + 1, 1)
                    project_x(m + 1, 2)
                chunk_back(g + 2, m, b, 2)
                turn(g + 1, m * 2, 1)
                if nxt:
                    sums(m + 1, nxt[0])
                    project_z0(m + 1)
                if prv:
                    mean_square(m - 1, (decay_ready, START + m + 2) if nxt else (z1_read, START + m + 1))
                if nxt:
                    differences(g + 4, 0)
                chunk_back(g + 3, m, b, 3)
                turn(g + 2, m * 2 + 1, 2)
                if prv:
                    project_out(m - 1, *prv, (x_read, START + 3 * m + (5 if nxt else 3)))
                if nxt:
                    project_z1(m + 1)
                    chunk_front(g + 4, m + 1, nxt[0], 0)

            def finish(m, prv):
                turn(m * NC - 1, m * 2 - 1, NC - 1)
                mean_square(m - 1, (ms_read, START + m - 1))
                project_out(m - 1, *prv, (o_ready, START + m - 1))
            pe.wait_ge(s_x, n_x)
            tiles(pe, body, finish)

        @block.scalar
        def _(act):
            f = nc.scalar.activation

            def square(m):
                act.wait_ge(xc_ready, START + m + 1)
                f(sq[:, :], xc[:, :], ACT.Square).then_inc(sq_ready, 1)

            def norm(m):
                act.wait_ge(var_full, START + m + 1)
                f(rstd[:, :], place["var"], ACT.Ln, bias=eps[:, :]).then_inc(lnv_ready, 1)
                act.wait_ge(lnv_ready, START + m + 1)
                f(rstd[:, :], rstd[:, :], ACT.Exp, scale=-0.5).then_inc(rstd_ready, 1)

            def affine(m, it):
                act.wait_ge(u1_ready, START + m + 1)
                f(u[:, :], u[:, :], ACT.Identity, scale=pars(it, C_LNW), bias=pars(it, C_LNB)).then_inc(u_ready, 1)

            def softplus(m):
                act.wait_ge(neg_ready, START + m + 1)
                f(l1p[:, :, :], neg[:, :, :], ACT.Exp).then_inc(e_ready, 1)
                act.wait_ge(e_ready, START + m + 1)
                f(l1p[:, :, :], l1p[:, :, :], ACT.Ln, bias=1.0).then_inc(l1p_ready, 1)

            def leave(m, b, it, i):
                if i == 0:
                    act.wait_ge(halo_ready, START + lag(m, 1))
                name, _, j = PARTS[i]
                act.wait_ge(x_full, START + 3 * m + i + 1)
                f(pre[b][:, j, DC - 1:], place[name], ACT.Copy)
                f(acc[:, j, :], place[name], ACT.Identity, scale=pars(it, C_CW + 4 * j + 3), bias=pars(it, C_CB + j))\
                    .then_inc(x_read, 1)

            def silus(m, b):
                act.wait_ge(y_ready, START + lag(m, 1))
                act.wait_ge(z0_full, START + m + 1)
                f(zs[b][:, 0, :], place["z0"], ACT.Silu).then_inc(z0_read, 1)
                act.wait_ge(conv_step, START + m * 9 + 7)
                f(xs[b][:, 1, :], acc[:, 1, :], ACT.Silu)
                act.wait_ge(conv_step, START + m * 9 + 8)
                f(bt[b][:, :], acc[0:DS, 2, :], ACT.Silu)
                f(ct[b][:, :], acc[DS:, 2, :], ACT.Silu)
                act.wait_ge(conv_step, START + m * 9 + 9)
                f(xs[b][:, 0, :], acc[:, 0, :], ACT.Silu).then_inc(silu_done, 1)
                act.wait_ge(z1_full, START + m + 1)
                f(zs[b][:, 1, :], place["z1"], ACT.Silu).then_inc(z1_read, 1)

            def decays(m, b):
                act.wait_ge(cum_full, START + m + 1)
                f(decay[b][:, :, :, :].rearrange("p k c h -> p (k c h)"), p_sums, ACT.Exp).then_inc(decay_ready, 1)

            def between(g, k):
                act.wait_ge(diff_full, START + g + 1)
                act.wait_ge(mt_ready, START + lag(g, 1))
                f(L[k][:, :, :], p_diff[:, :, :], ACT.Exp).then_inc(L_ready, 1)

            def square2(m, b):
                act.wait_ge(y_ready, START + m + 1)
                f(sq2[:, :, :], y[b][:, :, :], ACT.Square).then_inc(sq2_ready, 1)

            def norm2(m):
                act.wait_ge(ms_full, START + m + 1)
                act.wait_ge(o_ready, START + m)
                f(rstd2[:, :], place["ms"], ACT.Ln, bias=eps[:, :]).then_inc(ms_read, 1)
                act.wait_ge(ms_read, START + m + 1)
                f(rstd2[:, :], rstd2[:, :], ACT.Exp, scale=-0.5).then_inc(rstd2_ready, 1)

            def silu_block(m, b):
                act.preload_act_table_set("silu_and_others")
                silus(m, b)
                act.preload_act_table_set("natural_log_exp_and_others")

            act.preload_act_table_set("natural_log_exp_and_others")
            act.wait_ge(s_eps, START + 1)
            act.wait_ge(s_par, N_PARS)
            f(arow[:, :, :], row[:, 1, :, :], ACT.Exp).then_inc(s_arow, 1)
            square(0)
            norm(0)
            affine(0, 0)
            softplus(0)
            for j in range(3):
                leave(0, 0, 0, j)
            decays(0, 0)
            between(0, 0)
            silu_block(0, 0)

            def body(m, now, nxt, prv):
                g = m * NC
                if nxt:
                    square(m + 1)
                between(g + 1, 1)
                if nxt:
                    norm(m + 1)
                    affine(m + 1, nxt[1])
                between(g + 2, 0)
                if prv:
                    square2(m - 1, prv[0])
                if nxt:
                    softplus(m + 1)
                    leave(m + 1, *nxt, 0)
                between(g + 3, 1)
                if nxt:
                    leave(m + 1, *nxt, 1)
                    leave(m + 1, *nxt, 2)
                    decays(m + 1, nxt[0])
                if prv:
                    norm2(m - 1)
                if nxt:
                    between(g + 4, 0)
                    silu_block(m + 1, nxt[0])

            def finish(m, prv):
                square2(m - 1, prv[0])
                norm2(m - 1)
            tiles(act, body, finish)

        @block.vector
        def _(dve):
            v = nc.vector

            def centre(m, b, it):
                dve.wait_ge(mean_full, START + m + 1)
                dve.wait_ge(sq_ready, START + m)
                v.tensor_tensor(xc[:, :], tile_in(b, it), place["mean"], ALU.subtract).then_inc(xc_ready, 1)

            def scale(m):
                dve.wait_ge(rstd_ready, START + m + 1)
                dve.wait_ge(xc_ready, START + m + 1)
                dve.wait_ge(z1_full, START + m)
                v.tensor_tensor(u[:, :], xc[:, :], rstd[:, :], ALU.mult).then_inc(u1_ready, 1)

            def softplus_in(m, it):
                dve.wait_ge(dt_full, START + m + 1)
                v.tensor_tensor(raw[:, :, :], p_dt.rearrange("p (c h) -> p c h", h=NH),
                                row[:, 0, bass.ds(it, 1), :].broadcast_to([P, NC, NH]), ALU.add).then_inc(raw_ready, 1)
                dve.wait_ge(raw_ready, START + m + 1)
                v.scalar_tensor_tensor(neg[:, :, :], raw[:, :, :], -1.0, raw[:, :, :], ALU.mult, ALU.min).then_inc(neg_ready, 1)

            def softplus_out(m, b, it):
                dve.wait_ge(l1p_ready, START + m + 1)
                v.scalar_tensor_tensor(dt[b][:, :, :], raw[:, :, :], 0.0, l1p[:, :, :], ALU.max, ALU.add).then_inc(dt_ready, 1)
                dve.wait_ge(dt_ready, START + m + 1)
                for out, ready in ((a, a_ready), (a_hi, ahi_ready)):
                    v.tensor_tensor(out[b][:, :, :], dt[b][:, :, :], arow[:, bass.ds(it, 1), :].broadcast_to([P, NC, NH]), ALU.mult)\
                        .then_inc(ready, 1)

            def convolve(m, b, it, k, i):
                j = PARTS[i][2]
                if k == 0:
                    dve.wait_ge(x_read, START + 3 * m + i + 1)
                    dve.wait_ge(halo_ready, START + lag(m, 1))
                else:
                    dve.wait_ge(conv_step, START + m * 9 + (k - 1) * 3 + i + 1)
                v.scalar_tensor_tensor(acc[:, j, :], pre[b][:, j, k:k + TT], pars(it, C_CW + 4 * j + k), acc[:, j, :],
                                       ALU.mult, ALU.add).then_inc(conv_step, 1)

            def halo(m, b, it):
                dve.wait_ge(conv_step, START + m * 9 + 9)
                v.tensor_scalar(pre[b][:, :, 0:DC - 1], pre[b][:, :, TT:], again[:, bass.ds(it + 1, 1)], None, ALU.mult)\
                    .then_inc(halo_ready, 1)

            def decays(m, b):
                dve.wait_ge(decay_ready, START + m + 1)
                v.tensor_tensor(ddt[b][:, :, :], decay[b][:, 1, :, :], dt[b][:, :, :], ALU.mult).then_inc(ddt_ready, 1)

            def clear_state(b, it):
                v.tensor_scalar(state[b][:, :, :], state[b][:, :, :], again[0:DS, bass.ds(it, 1)], None, ALU.mult)\
                    .then_inc(state_ready, 1)

            def chunk_front(g, m, b, c):
                k = c % 2
                dve.wait_ge(gt_full, START + g + 1)
                dve.wait_ge(ddt_ready, START + m + 1)
                dve.wait_ge(ds_full, START + lag(g, 1))
                v.tensor_tensor(gm[k][:, :], p_g, tri[:, :], ALU.mult).then_inc(gm_ready, 1)
                x3 = p_xtok.rearrange("p (h n) -> p h n", h=NH)
                v.tensor_tensor(xdt[k][:, :, :], x3, heads(dt[b][:, c, :]), ALU.mult)
                v.tensor_tensor(xdec[k][:, :, :], x3, heads(ddt[b][:, c, :]), ALU.mult)
                v.tensor_copy(btok[k][:, :], p_btok).then_inc(gt_free, 1)

            def chunk_back(g, b, c):
                k = c % 2
                dve.wait_ge(y_full, START + g + 1)
                v.tensor_tensor(yo[k][:, :, :], p_y[:, 1, :, :], heads(decay[b][:, 0, c, :]), ALU.mult).then_inc(yo_ready, 1)
                dve.wait_ge(faded_ready, START + g + 1)
                dve.wait_ge(ds_full, START + g + 1)
                v.tensor_tensor(state[b][:, :, :], faded[:, :, :], p_ds[:, :].rearrange("p (h n) -> p h n", h=NH), ALU.add)\
                    .then_inc(state_ready, 1)
                dve.wait_ge(yo_ready, START + g + 1)
                dve.wait_ge(pyt_full, START + lag(g, 1))
                v.tensor_tensor(yt[k][:, :], yo[k][:, :, :].rearrange("p h n -> p (h n)"),
                                p_y[:, 0, :, :].rearrange("p h n -> p (h n)"), ALU.add).then_inc(yt_ready, 1)

            def skip(pair, b, it, j):
                dve.wait_ge(pyt_full, START + pair * 2 + 2)
                q = slice(j * 2 * Q, (j + 1) * 2 * Q)
                for k in range(2):
                    last = v.scalar_tensor_tensor(y[b][:, k, q], xs[b][:, k, q], pars(it, C_D + k),
                                                  p_yt[:, k, :, :].rearrange("p c q -> p (c q)"), ALU.mult, ALU.add)
                last.then_inc(pyt_free, 1)

            def gate(m, b):
                dve.wait_ge(pyt_free, START + m * 2 + 2)
                v.tensor_tensor(y[b][:, :, :], y[b][:, :, :], zs[b][:, :, :], ALU.mult).then_inc(y_ready, 1)

            def prepare_out(it):
                dve.wait_ge(out_full, START + it * NB)
                dve.wait_ge(s_wout, 16 * (it + 1))
                for k in range(2):
                    last = v.tensor_scalar(wout[:, k, :], wout_in[:, k, :], pars(it, C_RW + k), None, ALU.mult)
                last.then_inc(s_prep, 1)

            def normed(m):
                dve.wait_ge(out_full, START + m + 1)
                dve.wait_ge(rstd2_ready, START + m + 1)
                dve.wait_ge(h_ready, START + m)
                v.tensor_tensor(o[:, :], place["out"], rstd2[:, :], ALU.mult).then_inc(o_ready, 1)

            for b in range(NB):
                v.memset(pre[b][:, :, 0:DC - 1], 0.0)
                v.memset(state[b][:, :, :], 0.0)
            dve.wait_ge(s_const, n_const)
            v.tensor_copy(low_r[:, :], low[:, :]).then_inc(s_low, 1)
            dve.wait_ge(s_x0, 16)
            centre(0, 0, 0)
            dve.wait_ge(s_par, N_PARS)
            scale(0)
            softplus_in(0, 0)
            dve.wait_ge(s_arow, START + 1)
            v.tensor_scalar(arow[:, :, :], arow[:, :, :], -1.0, None, ALU.mult).then_inc(s_arow, 1)
            dve.wait_ge(s_arow, START + 2)
            softplus_out(0, 0, 0)
            for k in range(DC - 1):
                for j in range(3):
                    convolve(0, 0, 0, k, j)
            halo(0, 0, 0)
            decays(0, 0)
            clear_state(0, 0)
            chunk_front(0, 0, 0, 0)

            def body(m, now, nxt, prv):
                b, it = now
                g = m * NC
                if nxt:
                    centre(m + 1, *nxt)
                chunk_front(g + 1, m, b, 1)
                chunk_back(g, b, 0)
                if prv:
                    skip(m * 2 - 1, *prv, 1)
                if nxt:
                    scale(m + 1)
                chunk_front(g + 2, m, b, 2)
                if prv:
                    gate(m - 1, prv[0])
                chunk_back(g + 1, b, 1)
                if nxt:
                    softplus_in(m + 1, nxt[1])
                if nxt:
                    softplus_out(m + 1, *nxt)
                chunk_front(g + 3, m, b, 3)
                if nxt:
                    convolve(m + 1, *nxt, 0, 0)
                chunk_back(g + 2, b, 2)
                if nxt:
                    convolve(m + 1, *nxt, 0, 1)
                    convolve(m + 1, *nxt, 0, 2)
                skip(m * 2, b, it, 0)
                if nxt:
                    for k in range(1, DC - 1):
                        for j in range(3):
                            convolve(m + 1, *nxt, k, j)
                    halo(m + 1, *nxt)
                    decays(m + 1, nxt[0])
                chunk_back(g + 3, b, 3)
                if prv:
                    normed(m - 1)
                if b == 0:
                    prepare_out(it)
                if nxt:
                    clear_state(*nxt)
                    chunk_front(g + 4, m + 1, nxt[0], 0)

            def finish(m, prv):
                skip(m * 2 - 1, *prv, 1)
                gate(m - 1, prv[0])
                normed(m - 1)
            dve.wait_ge(s_x, n_x)
            tiles(dve, body, finish)


FB = 512 // P
NTILE = NB * NT


def ffn(nc, X, H, XP, cst, wts):
    _, _, ones, _, mean_w, rms_w = cst
    up, down, split, s_weights, n_weights = wts
    with ExitStack() as ctx:
        sb, ps, sem = tensors(nc, ctx)
        tile = lambda name, dt=F32: sb(f"f_{name}", [P, TT], dt)
        x1 = sb("f_x1", [P, NTILE, TT])
        sq, r = sb("f_sq", [P, NTILE, TT]), sb("f_r", [P, NTILE, TT])
        xn_hi, xn_lo = sb("f_xn_hi", [P, NTILE, TT], F32R), sb("f_xn_lo", [P, NTILE, TT], F32R)
        hid, hsq = sb("f_hid", [P, FB, TT]), sb("f_hsq", [P, FB, TT])
        hid_hi, hid_lo = sb("f_hid_hi", [P, FB, TT], F32R), sb("f_hid_lo", [P, FB, TT], F32R)
        o, sq2, r2, rstd2 = tile("o"), tile("sq2"), tile("r2"), tile("rstd2")
        up_t, down_t = sb("f_up_t", [P, FB * P], F32R), sb("f_down_t", [P, FB * P], F32R)
        asum, thr, nthr = sb("f_asum", [P, 2]), sb("f_thr", [P, 2]), sb("f_nthr", [P, 2])
        mneg = sb("f_mneg", [P, 2, FB * P])
        eps, tiny, guard = sb("f_eps", [P, 1]), sb("f_tiny", [P, 1]), sb("f_guard", [P, 1])
        p_back, p_down, p_ms = ps("f_pback", [P, TT]), ps("f_pdown", [P, TT]), ps("f_pms", [P, TT])
        p_up = [ps(f"f_pup{j}", [P, TT]) for j in range(FB)]
        p_front = p_up
        (s_eps, asum_ready, alpha_full, thr_ready, neg_ready, tern_ready, high_ready, sum_ready,
         mean_full, xc_ready, sq_ready, var_full, lv_ready, rstd_ready, x1_ready, lnv_ready, ratio_ready, root_ready,
         lroot_ready, r_ready, xn_ready,
         xnhi_ready, xnlo_ready, up_full, hid_ready, hsq_ready, hsq2_ready, hsum_ready, hi_ready, lo_ready,
         ms2_full, r2_step, r2_ready, down_full, o_ready,
         s2_ready, mean2_full, xc2_ready, sq2_ready, var2_full, lv2_ready, rstd2_ready, x2_ready) = (sem("f_" + n) for n in (
            "eps_r asum_r alpha_f thr_r neg_r tern_r high_r sum_r mean_f xc_r sq_r var_f lv_r rstd_r x1_r lnv_r ratio_r root_r lroot_r r_r xn_r "
            "xnhi_r xnlo_r up_f hid_r hsq_r hsq2_r hsum_r hi_r lo_r ms2_f r2_step r2_r down_f o_r s2_r mean2_f xc2_r sq2_r var2_f lv2_r rstd2_r "
            "x2_r").split())
        sem.start()
        block = ctx.enter_context(nc.Block())

        def of(x, i):
            return x[:, bass.ds(i, 1), :].rearrange("p a t -> p (a t)")

        def tiles(engine, body):
            body(0, True, False)
            with engine.Fori(1, NTILE - 1) as i:
                body(i, False, False)
            body(NTILE - 1, False, True)

        @block.gpsimd
        def _(pool):
            mul = lambda out, a, b: nc.gpsimd.tensor_tensor(out, a, b, ALU.mult)
            nc.gpsimd.memset(eps[:, :], LN_EPS)
            nc.gpsimd.memset(tiny[:, :], 1e-19)
            nc.gpsimd.memset(guard[:, :], 1e-8).then_inc(s_eps, 1)
            nc.gpsimd.memset(XP[:, :, 0:1], 0.0)
            nc.gpsimd.memset(XP[:, :, TT + 1:], 0.0)

            pool.wait_ge(s_weights, n_weights)
            for k, (w, hi, lo) in enumerate(split):
                nc.gpsimd.tensor_copy(hi, w).then_inc(high_ready, 1)
                pool.wait_ge(high_ready, START + k + 1)
                nc.gpsimd.tensor_tensor(lo, w, hi.bitcast(F32), ALU.subtract)

            pool.wait_ge(xn_ready, START + NTILE)

            def body(i, first, last):
                for j in range(FB // 2):
                    pool.wait_ge(hid_ready, START + i * FB + j + 1)
                    mul(hsq[:, j, :], hid[:, j, :], hid[:, j, :]).then_inc(hsq_ready, 1)
            tiles(pool, body)

        @block.tensor
        def _(pe):
            mm = nc.tensor.matmul

            def project_up(i, first):
                pe.wait_ge(xnlo_ready, START + i + 1)
                for j in range(FB):
                    if not first:
                        pe.wait_ge(hid_ready, START + (i - 1) * FB + j + 1)
                    w = up_t[:, j * P:(j + 1) * P]
                    mm(p_up[j][:, :], w, of(xn_hi, i), start=True, stop=False)
                    mm(p_up[j][:, :], w, of(xn_lo, i), start=False, stop=True).then_inc(up_full, 1)

            def mean_square2(i):
                pe.wait_ge(r2_ready, START + i)
                pe.wait_ge(hsum_ready, START + 2 * i + 2)
                mm(p_ms[:, :], rms_w[:, :], hsq[:, 0, :], start=True, stop=True).then_inc(ms2_full, 1)

            def project_down(i):
                pe.wait_ge(o_ready, START + i)
                for j in range(FB):
                    pe.wait_ge(lo_ready, START + i * FB + j + 1)
                    w = down_t[:, j * P:(j + 1) * P]
                    mm(p_down[:, :], w, hid_hi[:, j, :], start=(j == 0), stop=False)
                    last = mm(p_down[:, :], w, hid_lo[:, j, :], start=False, stop=(j == FB - 1))
                last.then_inc(down_full, 1)

            def mean2(i):
                pe.wait_ge(lv2_ready, START + i)
                pe.wait_ge(s2_ready, START + i + 1)
                mm(p_back[:, :], mean_w[:, :], o[:, :], start=True, stop=True).then_inc(mean2_full, 1)

            def var2(i):
                pe.wait_ge(sq2_ready, START + i + 1)
                mm(p_back[:, :], mean_w[:, :], sq2[:, :], start=True, stop=True).then_inc(var2_full, 1)

            for i in range(NTILE):
                pe.wait_ge(sum_ready, START + i // NT + 1)
                mm(p_front[i][:, :], mean_w[:, :], of(x1, i), start=True, stop=True).then_inc(mean_full, 1)
            pe.wait_ge(s_weights, n_weights)
            pe.wait_ge(asum_ready, START + 2)
            mm(p_ms[:, 0:2], ones[:, :], asum[:, :], start=True, stop=True).then_inc(alpha_full, 1)
            for i in range(NTILE):
                pe.wait_ge(sq_ready, START + i + 1)
                mm(p_front[i][:, :], mean_w[:, :], of(sq, i), start=True, stop=True).then_inc(var_full, 1)
            pe.wait_ge(tern_ready, START + 2)
            pe.wait_ge(lnv_ready, START + NTILE)
            project_up(0, True)

            def body(i, first, last):
                if not first:
                    mean2(i - 1)
                if not last:
                    project_up(i + 1, False)
                mean_square2(i)
                if not first:
                    var2(i - 1)
                project_down(i)
            tiles(pe, body)
            mean2(NTILE - 1)
            var2(NTILE - 1)

        @block.scalar
        def _(act):
            f = nc.scalar.activation

            def hidden_scale(i):
                act.wait_ge(o_ready, START + i)
                act.wait_ge(ms2_full, START + i + 1)
                f(r2[:, :], p_ms[:, :], ACT.Ln, bias=tiny[:, :], scale=0.5).then_inc(r2_step, 1)
                act.wait_ge(r2_step, START + i * 3 + 1)
                f(r2[:, :], r2[:, :], ACT.Exp, scale=0.5).then_inc(r2_step, 1)
                act.wait_ge(r2_step, START + i * 3 + 2)
                f(r2[:, :], r2[:, :], ACT.Ln, bias=guard[:, :]).then_inc(r2_step, 1)
                act.wait_ge(r2_step, START + i * 3 + 3)
                f(r2[:, :], r2[:, :], ACT.Exp, scale=-1.0).then_inc(r2_ready, 1)

            def scale_back(i):
                act.wait_ge(var2_full, START + i + 1)
                act.wait_ge(x2_ready, START + i)
                f(rstd2[:, :], p_back[:, :], ACT.Ln, bias=eps[:, :]).then_inc(lv2_ready, 1)
                act.wait_ge(lv2_ready, START + i + 1)
                f(rstd2[:, :], rstd2[:, :], ACT.Exp, scale=-0.5).then_inc(rstd2_ready, 1)

            act.preload_act_table_set("natural_log_exp_and_others")
            act.wait_ge(s_eps, START + 1)
            for i in range(NTILE):
                act.wait_ge(xc_ready, START + i + 1)
                f(of(sq, i), of(x1, i), ACT.Square).then_inc(sq_ready, 1)
            for i in range(NTILE):
                act.wait_ge(var_full, START + i + 1)
                f(of(r, i), p_front[i][:, :], ACT.Ln, bias=eps[:, :]).then_inc(lv_ready, 1)
            for i in range(NTILE):
                f(of(hsq, i), p_front[i][:, :], ACT.Ln, bias=tiny[:, :]).then_inc(lnv_ready, 1)
            for i in range(NTILE):
                act.wait_ge(lv_ready, START + i + 1)
                f(of(sq, i), of(r, i), ACT.Exp, scale=-0.5).then_inc(rstd_ready, 1)
            for i in range(NTILE):
                act.wait_ge(ratio_ready, START + i + 1)
                f(of(hsq, i), of(hsq, i), ACT.Exp, scale=0.5).then_inc(root_ready, 1)
            for i in range(NTILE):
                act.wait_ge(root_ready, START + i + 1)
                f(of(hsq, i), of(hsq, i), ACT.Ln, bias=guard[:, :]).then_inc(lroot_ready, 1)
            for i in range(NTILE):
                act.wait_ge(lroot_ready, START + i + 1)
                f(of(hsq, i), of(hsq, i), ACT.Exp, scale=-1.0).then_inc(r_ready, 1)

            def body(i, first, last):
                act.preload_act_table_set("gelu_and_others")
                if not first:
                    act.wait_ge(hsq_ready, START + i * (FB // 2))
                    act.wait_ge(lo_ready, START + i * FB)
                for j in range(FB):
                    act.wait_ge(up_full, START + i * FB + j + 1)
                    f(hid[:, j, :], p_up[j][:, :], ACT.Gelu).then_inc(hid_ready, 1)
                if first:
                    act.wait_ge(xn_ready, START + NTILE)
                for j in range(FB // 2, FB):
                    act.wait_ge(hid_ready, START + i * FB + j + 1)
                    f(hsq[:, j, :], hid[:, j, :], ACT.Square).then_inc(hsq2_ready, 1)
                act.preload_act_table_set("natural_log_exp_and_others")
                hidden_scale(i)
                if not first:
                    scale_back(i - 1)
            tiles(act, body)
            scale_back(NTILE - 1)

        @block.vector
        def _(dve):
            v = nc.vector

            def halve(i, j):
                n = i * FB + j
                dve.wait_ge(hid_ready, START + n + 1)
                v.tensor_scalar(hid_hi[:, j, :], hid[:, j, :], 1.0, None, ALU.mult).then_inc(hi_ready, 1)
                dve.wait_ge(hi_ready, START + n + 1)
                v.tensor_tensor(hid_lo[:, j, :], hid[:, j, :], hid_hi[:, j, :].bitcast(F32), ALU.subtract).then_inc(lo_ready, 1)

            def sum_squares(i):
                dve.wait_ge(hsq_ready, START + (i + 1) * (FB // 2))
                dve.wait_ge(hsq2_ready, START + (i + 1) * (FB // 2))
                v.tensor_tensor(hsq[:, 0:2, :], hsq[:, 0:2, :], hsq[:, 2:4, :], ALU.add).then_inc(hsum_ready, 1)
                dve.wait_ge(hsum_ready, START + 2 * i + 1)
                v.tensor_tensor(hsq[:, 0, :], hsq[:, 0, :], hsq[:, 1, :], ALU.add).then_inc(hsum_ready, 1)

            def out_scale(i):
                dve.wait_ge(down_full, START + i + 1)
                dve.wait_ge(sq2_ready, START + i)
                dve.wait_ge(r2_ready, START + i + 1)
                dve.wait_ge(x2_ready, START + i)
                v.tensor_tensor(o[:, :], p_down[:, :], r2[:, :], ALU.mult).then_inc(o_ready, 1)
                dve.wait_ge(o_ready, START + i + 1)
                v.tensor_tensor(o[:, :], o[:, :], of(x1, i), ALU.add).then_inc(s2_ready, 1)

            def centre2(i):
                dve.wait_ge(mean2_full, START + i + 1)
                v.tensor_tensor(o[:, :], o[:, :], p_back[:, :], ALU.subtract).then_inc(xc2_ready, 1)

            def square2(i):
                dve.wait_ge(xc2_ready, START + i + 1)
                v.tensor_tensor(sq2[:, :], o[:, :], o[:, :], ALU.mult).then_inc(sq2_ready, 1)

            def norm2(i):
                dve.wait_ge(rstd2_ready, START + i + 1)
                v.tensor_tensor(XP[:, bass.ds(i, 1), 1:TT + 1].rearrange("p a n -> p (a n)"), o[:, :], rstd2[:, :], ALU.mult)\
                    .then_inc(x2_ready, 1)

            for b in range(NB):
                v.tensor_tensor(x1[:, b * NT:(b + 1) * NT, :].rearrange("p a n -> p (a n)"), X[:, b, :], H[:, b, :], ALU.add)\
                    .then_inc(sum_ready, 1)
            dve.wait_ge(s_weights, n_weights)
            parts = ((up[:, :], up_t), (down[:, :, :].rearrange("p k n -> p (k n)"), down_t))
            for k, (w, _) in enumerate(parts):
                v.tensor_reduce(asum[:, k:k + 1], w, AX.X, ALU.add, apply_absolute_value=True).then_inc(asum_ready, 1)
            for i in range(NTILE):
                dve.wait_ge(mean_full, START + i + 1)
                v.tensor_tensor(of(x1, i), of(x1, i), p_front[i][:, :], ALU.subtract).then_inc(xc_ready, 1)
            dve.wait_ge(alpha_full, START + 1)
            v.tensor_scalar(thr[:, :], p_ms[:, 0:2], 0.5 / (D * FB * P), None, ALU.mult)
            v.tensor_scalar(nthr[:, :], p_ms[:, 0:2], -0.5 / (D * FB * P), None, ALU.mult).then_inc(thr_ready, 1)
            dve.wait_ge(thr_ready, START + 1)
            for k, (w, w_t) in enumerate(parts):
                v.tensor_scalar(mneg[:, k, :], w, nthr[:, k:k + 1], None, ALU.is_lt).then_inc(neg_ready, 1)
            for k, (w, w_t) in enumerate(parts):
                dve.wait_ge(neg_ready, START + k + 1)
                v.scalar_tensor_tensor(w_t[:, :], w, thr[:, k:k + 1], mneg[:, k, :], ALU.is_gt, ALU.subtract).then_inc(tern_ready, 1)

            for i in range(NTILE):
                dve.wait_ge(lnv_ready, START + i + 1)
                v.tensor_tensor(of(hsq, i), of(hsq, i), of(r, i), ALU.subtract).then_inc(ratio_ready, 1)
            for i in range(NTILE):
                dve.wait_ge(rstd_ready, START + i + 1)
                v.tensor_tensor(of(x1, i), of(x1, i), of(sq, i), ALU.mult).then_inc(x1_ready, 1)
            for i in range(NTILE):
                dve.wait_ge(r_ready, START + i + 1)
                dve.wait_ge(x1_ready, START + i + 1)
                v.tensor_tensor(of(r, i), of(x1, i), of(hsq, i), ALU.mult).then_inc(xn_ready, 1)
                dve.wait_ge(xn_ready, START + i + 1)
                v.tensor_scalar(of(xn_hi, i), of(r, i), 1.0, None, ALU.mult).then_inc(xnhi_ready, 1)
                dve.wait_ge(xnhi_ready, START + i + 1)
                v.tensor_tensor(of(xn_lo, i), of(r, i), of(xn_hi, i).bitcast(F32), ALU.subtract).then_inc(xnlo_ready, 1)

            def body(i, first, last):
                halve(i, 0)
                sum_squares(i)
                if not first:
                    centre2(i - 1)
                    square2(i - 1)
                for j in range(1, FB):
                    halve(i, j)
                if not first:
                    norm2(i - 1)
                out_scale(i)
            tiles(dve, body)
            centre2(NTILE - 1)
            square2(NTILE - 1)
            norm2(NTILE - 1)
            dve.wait_ge(x2_ready, START + NTILE)
            for b in range(NB):
                for t in range(1, NT):
                    before, behind = XP[:, b * NT + t - 1, :], XP[:, b * NT + t, :]
                    v.tensor_copy(before[:, TT + 1:], behind[:, 1:2])
                    v.tensor_copy(behind[:, 0:1], before[:, TT:TT + 1])


EPS = math.exp(-1 / 12)
EPS_RKV = (EPS / 2, EPS + 0.3 / 11, EPS)
NF = 8
E_LO, E_HI = float(np.exp(np.float32(-20))), float(np.exp(np.float32(10)))
BIG = 2.0 ** 39
TP = TT + 2


def wkv(nc, X, XP, SCR, cst, wts):
    mean_w = cst[4]
    wr, wk, wv, wo, decay, t_rem, par, bo, keep, behind, s_weights, n_weights = wts
    U_, BK, BR, BV, DECAY = range(5)
    with ExitStack() as ctx:
        sb, ps, sem = tensors(nc, ctx)
        mix_kv = sb("w_mix_kv", [P, NTILE, 2, TT])
        t_in = sb("w_t_in", [2, TT], F32R)
        later = sb("w_later", [P, NF, NTILE])
        neg_w = sb("w_neg_w", [P, NF])
        dec_hi, dec_lo = sb("w_dec_hi", [2, NF * P], F32R), sb("w_dec_lo", [2, NF * P], F32R)
        ubk, nbr = sb("w_ubk", [P, NF]), sb("w_nbr", [P, NF])
        eps, onec = sb("w_eps", [P, 1]), sb("w_one", [P, 1])
        RING = 4
        ring = lambda name, shape: [sb(f"w_{name}{k}", shape) for k in range(RING)]
        V, er, G = ring("V", [P, TT]), ring("er", [P, TT]), ring("G", [P, 4, TT])
        AB, O = ring("AB", [P, 2, TT]), ring("O", [P, TT])
        CS = ring("CS", [P, 2, 1 + TT])
        carry = sb("w_carry", [P, NF, 2])
        s, sq, r = (SCR[:, :, :].rearrange("p b t -> p (b t)")[:, k * TT:(k + 1) * TT] for k in range(3))
        pk = [ps(f"w_pk{k}", [P, TT]) for k in range(2)]
        pv = [ps(f"w_pv{k}", [P, TT]) for k in range(2)]
        pr = [ps(f"w_pr{k}", [P, TT]) for k in range(2)]
        pacc, pst = ps("w_pacc", [P, TT]), ps("w_pst", [P, TT])
        (s_eps, s_small, s_prep, mix1, mix_ready, k_full, k_read, kw_full, kw_read, v_full, v_read, r_full, er_read, clip_ready, er1_ready,
         ev_ready, cs_ready, ab_ready, dn_ready, ln_ready, rd_ready, o_ready, o_used, s_ready, mean_full, xc_ready,
         sq_ready, var_full, lv_ready, rstd_ready, x3_ready, halo, carry_ready, dec_ready) = [sem(f"w_s{i}_{n}") for i, n in enumerate(
             "eps small prep mix1 mix k_full k_read kw_full kw_read v_full v_read r_full er clip er1 ev cs ab dn ln rd o o_used "
             "s mean xc sq var lv rstd x3 halo carry dec".split())]
        sem.start()
        block = ctx.enter_context(nc.Block())
        xp = XP[:, :, :]
        xf = X[:, :, :].rearrange("p b t -> p (b t)")

        def tiles(engine, body):
            body(0, True, False)
            with engine.Fori(1, NTILE - 1) as i:
                body(i, False, False)
            body(NTILE - 1, False, True)

        def mix(i, j):
            if j == 0:
                return xf[:, bass.ds(i * TT, TT)]
            return mix_kv[:, bass.ds(i, 1), j - 1, :].rearrange("p a t -> p (a t)")

        @block.gpsimd
        def _(pool):
            nc.gpsimd.memset(eps[:, :], LN_EPS)
            nc.gpsimd.memset(onec[:, :], 1.0).then_inc(s_eps, 1)

            def body(i, first, last):
                for f in range(NF):
                    k, n = f % RING, i * NF + f
                    pool.wait_ge(cs_ready, START + n + 1)
                    if not (first and f < RING):
                        pool.wait_ge(o_ready, START + n - RING + 1)
                    nc.gpsimd.tensor_tensor(AB[k][:, :, :], CS[k][:, :, 0:TT], G[k][:, 2:4, :], ALU.add).then_inc(ab_ready, 1)
                    pool.wait_ge(ab_ready, START + n + 1)
                    pool.wait_ge(er1_ready, START + n + 1)
                    nc.gpsimd.tensor_tensor(er[k][:, :], AB[k][:, 1, :], er[k][:, :], ALU.mult).then_inc(dn_ready, 1)
            tiles(pool, body)

        @block.tensor
        def _(pe):
            mm = nc.tensor.matmul

            def project(f, n, first, x):
                k, fs = f % 2, slice(f * P, (f + 1) * P)
                old = not (first and f < 2)
                if old:
                    pe.wait_ge(kw_read, START + n - 1)
                mm(pk[k][:, :], wk[:, fs], x(1), start=True, stop=True).then_inc(k_full, 1)
                if old:
                    pe.wait_ge(v_read, START + n - 1)
                mm(pv[k][:, :], wv[:, fs], x(2), start=True, stop=True).then_inc(v_full, 1)
                if old:
                    pe.wait_ge(er_read, START + n - 1)
                mm(pr[k][:, :], wr[:, fs], x(0), start=True, stop=True).then_inc(r_full, 1)
                pe.wait_ge(k_read, START + n + 1)
                if first and f == 0:
                    pe.wait_ge(s_prep, START + 1)
                mm(pk[k][:, :], dec_hi[:, fs], t_in[:, :], start=False, stop=True, skip_group_check=True)
                mm(pk[k][:, :], dec_lo[:, fs], t_in[:, :], start=False, stop=True, skip_group_check=True).then_inc(kw_full, 1)

            def collect(f, n, tile):
                pe.wait_ge(o_ready, START + n + 1)
                if f == 0 and tile is not None:
                    pe.wait_ge(s_ready, START + tile)
                mm(pacc[:, :], wo[:, f, :], O[f % RING][:, :], start=(f == 0), stop=(f == NF - 1)).then_inc(o_used, 1)

            def mix_of(i):
                return lambda j: mix(i, j)

            def mean(i):
                pe.wait_ge(s_ready, START + i + 1)
                mm(pst[:, :], mean_w[:, :], s[:, :], start=True, stop=True).then_inc(mean_full, 1)

            def var(i):
                pe.wait_ge(sq_ready, START + i + 1)
                mm(pst[:, :], mean_w[:, :], sq[:, :], start=True, stop=True).then_inc(var_full, 1)

            pe.wait_ge(s_weights, n_weights)
            pe.wait_ge(mix_ready, START + 1)
            project(0, 0, True, mix_of(0))

            def body(i, first, last):
                for f in range(NF):
                    n = i * NF + f
                    if f < NF - 1:
                        project(f + 1, n + 1, first, mix_of(i))
                    elif not last:
                        pe.wait_ge(mix_ready, START + i + 2)
                        project(0, n + 1, False, mix_of(i + 1))
                    if f >= 4:
                        for k in (0, 1) if f == 4 else (f - 3,):
                            collect(k, i * NF + k, None if first else i)
                    elif f < 3 and not first:
                        collect(f - 3 + NF, n - 3, None)
                    if not first:
                        if f == 4:
                            mean(i - 1)
                        if f == 6:
                            var(i - 1)
            tiles(pe, body)
            for f in range(NF - 3, NF):
                collect(f, (NTILE - 1) * NF + f, None)
            mean(NTILE - 1)
            var(NTILE - 1)

        @block.scalar
        def _(act):
            a = nc.scalar.activation

            def front(f, n, i, first):
                k, b = f % RING, f % 2
                old = not (first and f < RING)
                act.wait_ge(k_full, START + n + 1)
                if old:
                    act.wait_ge(ab_ready, START + n - RING + 1)
                a(G[k][:, 3, :], pk[b][:, :], ACT.Exp, bias=ubk[:, f:f + 1]).then_inc(k_read, 1)
                act.wait_ge(v_full, START + n + 1)
                a(V[k][:, :], pv[b][:, :], ACT.Identity, bias=par[:, f, BV:BV + 1]).then_inc(v_read, 1)
                act.wait_ge(r_full, START + n + 1)
                if old:
                    act.wait_ge(o_ready, START + n - RING + 1)
                a(er[k][:, :], pr[b][:, :], ACT.Exp, scale=-1.0, bias=nbr[:, f:f + 1]).then_inc(er_read, 1)
                act.wait_ge(kw_full, START + n + 1)
                a(G[k][:, 1, :], pk[b][:, :], ACT.Exp, bias=later[:, f, bass.ds(i, 1)]).then_inc(kw_read, 1)

            def back(f, n):
                k = f % RING
                act.wait_ge(dn_ready, START + n + 1)
                a(er[k][:, :], er[k][:, :], ACT.Ln).then_inc(ln_ready, 1)
                act.wait_ge(ln_ready, START + n + 1)
                a(er[k][:, :], er[k][:, :], ACT.Exp, scale=-1.0).then_inc(rd_ready, 1)

            def before(i):
                for j, e in enumerate(EPS_RKV):
                    a(mix(i, j), xp[:, bass.ds(i, 1), 0:TT].rearrange("p a t -> p (a t)"), ACT.Copy, scale=e).then_inc(mix1, 1)

            def square(i):
                act.wait_ge(xc_ready, START + i + 1)
                a(sq[:, :], s[:, :], ACT.Square).then_inc(sq_ready, 1)

            def rstd(i):
                act.wait_ge(var_full, START + i + 1)
                a(r[:, :], pst[:, :], ACT.Ln, bias=eps[:, :]).then_inc(lv_ready, 1)
                act.wait_ge(lv_ready, START + i + 1)
                a(r[:, :], r[:, :], ACT.Exp, scale=-0.5).then_inc(rstd_ready, 1)

            act.preload_act_table_set("natural_log_exp_and_others")
            before(0)
            act.wait_ge(s_eps, START + 1)
            act.wait_ge(s_small, START + 1)

            def body(i, first, last):
                for f in range(NF):
                    n = i * NF + f
                    front(f, n, i, first)
                    if f >= 2:
                        back(f - 2, n - 2)
                    elif not first:
                        back(f - 2 + NF, n - 2)
                    if f == 3 and not last:
                        before(i + 1)
                    if not first:
                        if f == 5:
                            square(i - 1)
                        if f == 7:
                            rstd(i - 1)
            tiles(act, body)
            for f in range(NF - 2, NF):
                back(f, (NTILE - 1) * NF + f)
            square(NTILE - 1)
            rstd(NTILE - 1)

        @block.vector
        def _(dve):
            v = nc.vector

            def blend(i):
                for j, e in enumerate(EPS_RKV):
                    dve.wait_ge(mix1, START + i * 3 + j + 1)
                    last = v.scalar_tensor_tensor(mix(i, j),
                                                  xp[:, bass.ds(i, 1), 2:].rearrange("p a t -> p (a t)"), 1.0 - e,
                                                  mix(i, j), ALU.mult, ALU.add)
                last.then_inc(mix_ready, 1)

            def front(f, n, i, first):
                k = f % RING
                dve.wait_ge(kw_read, START + n + 1)
                v.tensor_scalar(G[k][:, 1::2, :], G[k][:, 1::2, :], E_LO, E_HI, ALU.max, ALU.min).then_inc(clip_ready, 1)
                dve.wait_ge(er_read, START + n + 1)
                v.tensor_scalar(er[k][:, :], er[k][:, :], BIG, 1.0, ALU.min, ALU.add).then_inc(er1_ready, 1)
                if not first:
                    dve.wait_ge(carry_ready, START + n - NF + 1)
                if not (first and f < RING):
                    dve.wait_ge(ab_ready, START + n - RING + 1)
                v.tensor_tensor(CS[k][:, :, 0], carry[:, f, :], keep[:, bass.ds(i, 1)].broadcast_to([P, 2]), ALU.mult).then_inc(halo, 1)
                dve.wait_ge(clip_ready, START + n + 1)
                dve.wait_ge(v_read, START + n + 1)
                v.tensor_tensor(G[k][:, 0::2, :], G[k][:, 1::2, :], V[k][:, :].unsqueeze(1).broadcast_to([P, 2, TT]), ALU.mult)\
                    .then_inc(ev_ready, 1)
                dve.wait_ge(halo, START + n + 1)
                for j in (1, 0):
                    if j == 0:
                        dve.wait_ge(ev_ready, START + n + 1)
                    last = v.tensor_tensor_scan(CS[k][:, j, 1:], onec[:, :].broadcast_to([P, TT]), G[k][:, j, :],
                                                CS[k][:, j, 0:1], ALU.mult, ALU.add)
                last.then_inc(cs_ready, 1)

            def back(f, n, first):
                k = f % RING
                dve.wait_ge(cs_ready, START + n + 1)
                v.tensor_copy(carry[:, f, :], CS[k][:, :, TT]).then_inc(carry_ready, 1)
                dve.wait_ge(rd_ready, START + n + 1)
                if not (first and f < RING):
                    dve.wait_ge(o_used, START + n - RING + 1)
                v.tensor_tensor(O[k][:, :], AB[k][:, 0, :], er[k][:, :], ALU.mult).then_inc(o_ready, 1)

            def total(i):
                dve.wait_ge(o_used, START + (i + 1) * NF)
                dve.wait_ge(x3_ready, START + i)
                v.scalar_tensor_tensor(s[:, :], pacc[:, :], bo[:, :], xp[:, bass.ds(i, 1), 1:TT + 1].rearrange("p a t -> p (a t)"),
                                       ALU.add, ALU.add).then_inc(s_ready, 1)

            def centre(i):
                dve.wait_ge(mean_full, START + i + 1)
                v.tensor_tensor(s[:, :], s[:, :], pst[:, :], ALU.subtract).then_inc(xc_ready, 1)

            def scale(i):
                dve.wait_ge(rstd_ready, START + i + 1)
                v.tensor_tensor(xf[:, bass.ds(i * TT, TT)], s[:, :], r[:, :], ALU.mult).then_inc(x3_ready, 1)

            dve.wait_ge(s_weights, n_weights)
            v.tensor_scalar(neg_w[:, :], par[:, :, DECAY], 0.0, -1.0, ALU.max, ALU.mult).then_inc(dec_ready, 1)
            v.tensor_tensor(ubk[:, :], par[:, :, U_], par[:, :, BK], ALU.add)
            v.tensor_scalar(nbr[:, :], par[:, :, BR], -1.0, None, ALU.mult)
            v.memset(carry[:, :, :], 0.0)
            dve.wait_ge(dec_ready, START + 1)
            v.tensor_tensor(later[:, :, :], neg_w[:, :].unsqueeze(2).broadcast_to([P, NF, NTILE]),
                            behind[:, :].unsqueeze(1).broadcast_to([P, NF, NTILE]), ALU.mult).then_inc(s_small, 1)
            blend(0)
            v.tensor_scalar(decay[0:1, :], decay[0:1, :], 0.0, -1.0, ALU.max, ALU.mult).then_inc(dec_ready, 1)
            v.tensor_copy(t_in[:, :], t_rem[:, :])
            dve.wait_ge(dec_ready, START + 2)
            v.tensor_copy(dec_hi[:, :], decay[:, :]).then_inc(dec_ready, 1)
            dve.wait_ge(dec_ready, START + 3)
            v.tensor_tensor(dec_lo[:, :], decay[:, :], dec_hi[:, :].bitcast(F32), ALU.subtract).then_inc(s_prep, 1)
            dve.wait_ge(s_small, START + 1)
            dve.wait_ge(s_eps, START + 1)

            def body(i, first, last):
                for f in range(NF):
                    n = i * NF + f
                    front(f, n, i, first)
                    if f >= 2:
                        back(f - 2, n - 2, first)
                    elif not first:
                        back(f - 2 + NF, n - 2, False)
                    if not first:
                        if f == 2:
                            total(i - 1)
                        if f == 4:
                            centre(i - 1)
                        if f == 7:
                            scale(i - 1)
                    if f == 5 and not last:
                        blend(i + 1)
            tiles(dve, body)
            for f in range(NF - 2, NF):
                back(f, (NTILE - 1) * NF + f, False)
            total(NTILE - 1)
            centre(NTILE - 1)
            scale(NTILE - 1)


NE, NG, I = 16, 4, 64
NPR = NE * I // P
GE = NE // NG
TOP_K, TOP_G = 4, 2
LO = 64


def moe(nc, X, OUT, cst, wts, out_dram):
    ident, mean_w = cst[3:5]
    gw, ebias, (gp_hi, gp_lo), (up_hi, up_lo), (dp_hi, dp_lo), sel, inner, below, s_weights, n_weights = wts
    with ExitStack() as ctx:
        sb, ps, sem = tensors(nc, ctx)
        eps = sb("e_eps", [P, 1])
        x_hi, x_lo = sb("e_x_hi", [P, NTILE * TT], F32R), sb("e_x_lo", [P, NTILE * TT], F32R)
        sel2 = sb("e_sel2", [P, NE * I], F32R)
        logit = [sb(f"e_logit{k}", [NE, TT]) for k in range(2)]
        comb_f, comb_t = sb("e_comb_f", [NE, TT]), sb("e_comb_t", [P, NTILE * TT], F32R)
        tok = lambda name, *n: sb(f"e_{name}", [P, NTILE * NC, *n])
        ex, sc, sfc = tok("ex", NE), tok("sc", NE), tok("sfc", NE)
        mx, mn = tok("mx", NE // 2), tok("mn", NE // 2)
        t1, t2, t3, gs = tok("t1", NG), tok("t2", NG), tok("t3", NG), tok("gs", NG)
        ggt, geq, gcnt, masked = tok("ggt", NG, NG), tok("geq", NG, NG), tok("gcnt", NG), tok("masked", NE)
        top8, above, n_above, equal, count, chosen = (tok("top8", 8), tok("above", NE), tok("n_above"), tok("equal", NE),
                                                      tok("count", NE), tok("chosen", NE))
        comb_now = sb("e_comb_now", [P, NC, NE])
        w, den, rden, comb = tok("w", NE), tok("den"), tok("rden"), tok("comb", NE)
        RING = 4
        ring = lambda name, dt=F32: [sb(f"e_{name}{k}", [P, TT], dt) for k in range(RING)]
        sg, gu, av, av_hi, av_lo = ring("sg"), ring("gu"), ring("av"), ring("av_hi", F32R), ring("av_lo", F32R)
        s, sq, r = sb("e_s", [P, TT]), sb("e_sq", [P, TT]), sb("e_r", [P, TT])
        pg = [ps(f"e_pg{k}", [P, TT]) for k in range(2)]
        pu = [ps(f"e_pu{k}", [P, TT]) for k in range(2)]
        pc, py, pm, pl = ps("e_pc", [P, TT]), ps("e_py", [P, TT]), ps("e_pm", [P, TT]), ps("e_pl", [P, TT])
        (s_eps, x_hi_ready, x_lo_ready, sel_ready, comb0, chain, lg_full, lg_ready, lt_full, ex_ready, all_ready, comb_ready, ct_full,
         cf_ready, chi_ready, ct_ready, g_full, g_read, u_full, c_full, gu_ready, av_ready, hi_ready, lo_ready, y_step, s_ready,
         mean_full, xc_ready, sq_ready, var_full, lv_ready, rstd_ready, out_ready, s_out) = [
             sem(f"e_s{i}_{n}") for i, n in enumerate(
                 "eps x_hi x_lo sel comb0 chain lg_f lg lt_f ex all comb ct_f cf chi ct g_f g_r u_f c_f gu av hi lo y s mean xc sq "
                 "var lv rstd out store".split())]
        sem.start(but=(s_out,))
        block = ctx.enter_context(nc.Block())
        xf, of = X[:, :, :].rearrange("p b t -> p (b t)"), OUT[:, :, :].rearrange("p b t -> p (b t)")

        def tiles(engine, body):
            body(0, True, False)
            with engine.Fori(1, NTILE - 1) as i:
                body(i, False, False)
            body(NTILE - 1, False, True)

        @block.sync
        def _(sp):
            with sp.Fori(0, NTILE) as i:
                sp.wait_ge(out_ready, START + i + 1)
                sp.dma_start(out_dram[:, bass.ds(i * TT, TT)], of[:, bass.ds(i * TT, TT)]).then_inc(s_out, 16)
            sp.wait_ge(s_out, 16 * NTILE)

        @block.gpsimd
        def _(pool):
            nc.gpsimd.memset(eps[:, :], LN_EPS).then_inc(s_eps, 1)
            with pool.Fori(0, NTILE) as i:
                t = bass.ds(i * TT, TT)
                pool.wait_ge(x_hi_ready, START + i + 1)
                nc.gpsimd.tensor_tensor(x_lo[:, t], xf[:, t], x_hi[:, t].bitcast(F32), ALU.subtract).then_inc(x_lo_ready, 1)

            def body(i, first, last):
                for j in range(NPR):
                    k, n = j % RING, i * NPR + j
                    pool.wait_ge(hi_ready, START + n + 1)
                    if not (first and j < RING):
                        pool.wait_ge(y_step, START + n - RING + 1)
                    nc.gpsimd.tensor_tensor(av_lo[k][:, :], av[k][:, :], av_hi[k][:, :].bitcast(F32), ALU.subtract)\
                        .then_inc(lo_ready, 1)
            tiles(pool, body)

        @block.tensor
        def _(pe):
            mm = nc.tensor.matmul

            def three(out, w_hi, w_lo, v_hi, v_lo, start, stop):
                mm(out, w_hi, v_hi, start=start, stop=False)
                mm(out, w_hi, v_lo, start=False, stop=False)
                return mm(out, w_lo, v_hi, start=False, stop=stop)

            def expert(j, n, i, first):
                k, js, x = j % 2, slice(j * P, (j + 1) * P), bass.ds(i * TT, TT)
                old = not (first and j < 2)
                if j == 0:
                    pe.wait_ge(x_lo_ready, START + i + 1)
                if old:
                    pe.wait_ge(g_read, START + n - 1)
                three(pg[k][:, :], gp_hi[:, js], gp_lo[:, js], x_hi[:, x], x_lo[:, x], True, True).then_inc(g_full, 1)
                if old:
                    pe.wait_ge(gu_ready, START + n - 1)
                three(pu[k][:, :], up_hi[:, js], up_lo[:, js], x_hi[:, x], x_lo[:, x], True, True).then_inc(u_full, 1)

            def weights(j, n, i, first):
                if j == 0:
                    pe.wait_ge(ct_ready, START + i + 1)
                if not (first and j < 1):
                    pe.wait_ge(av_ready, START + n)
                mm(pc[:, :], sel2[:, j * P:(j + 1) * P], comb_t[:, bass.ds(i * TT, TT)], start=True, stop=True).then_inc(c_full, 1)

            def collect(j, n, i):
                pe.wait_ge(lo_ready, START + n + 1)
                if j == 0 and i is not None:
                    pe.wait_ge(s_ready, START + i)
                k = j % RING
                three(py[:, :], dp_hi[:, j, :], dp_lo[:, j, :], av_hi[k][:, :], av_lo[k][:, :], j == 0, j == NPR - 1)\
                    .then_inc(y_step, 1)

            def logits(i):
                mm((pl, py)[i % 2][0:NE, :], gw[:, :], xf[:, i * TT:(i + 1) * TT], start=True, stop=True).then_inc(lg_full, 1)

            def to_tokens(i):
                pe.wait_ge(lg_ready, START + i + 1)
                for c in range(NC):
                    last = mm((pl, py)[i % 2][:, c * NE:(c + 1) * NE], logit[i % 2][:, c * Q:(c + 1) * Q], ident[0:NE, 0:NE],
                              start=True, stop=True)
                last.then_inc(lt_full, 1)

            def to_experts(i):
                pe.wait_ge(comb_ready, START + i + 1)
                for c in range(NC):
                    last = nc.tensor.transpose(pl[0:NE, c * Q:(c + 1) * Q], comb_now[:, c, :], ident[:, :])
                last.then_inc(ct_full, 1)

            def mean(i):
                pe.wait_ge(s_ready, START + i + 1)
                mm(pm[:, :], mean_w[:, :], s[:, :], start=True, stop=True).then_inc(mean_full, 1)

            def var(i):
                pe.wait_ge(sq_ready, START + i + 1)
                mm(pm[:, :], mean_w[:, :], sq[:, :], start=True, stop=True).then_inc(var_full, 1)

            pe.wait_ge(s_weights, n_weights)
            for i in range(NTILE):
                if i >= 2:
                    pe.wait_ge(ex_ready, START + i - 1)
                logits(i)
                if i % 2:
                    to_tokens(i - 1)
                    to_tokens(i)
            expert(0, 0, 0, True)
            expert(1, 1, 0, True)
            pe.wait_ge(ex_ready, START + NTILE)
            to_experts(0)
            pe.wait_ge(sel_ready, START + 1)

            def body(i, first, last):
                for j in range(NPR):
                    n = i * NPR + j
                    weights(j, n, i, first)
                    if j < NPR - 2:
                        expert(j + 2, n + 2, i, first)
                    elif not last:
                        expert(j + 2 - NPR, n + 2, i + 1, False)
                    if j >= 2:
                        collect(j - 2, n - 2, None if first else i)
                    elif not first:
                        collect(j - 2 + NPR, n - 2, None)
                    if not first and j == 2:
                        mean(i - 1)
                    if not first and j == 3:
                        var(i - 1)
                    if not last and j == (NPR - 1 if first else 5):
                        pe.wait_ge(cf_ready, START + i + 1)
                        to_experts(i + 1)
            tiles(pe, body)
            for j in range(NPR - 2, NPR):
                collect(j, (NTILE - 1) * NPR + j, None)
            mean(NTILE - 1)
            var(NTILE - 1)

        @block.scalar
        def _(act):
            a = nc.scalar.activation

            def silu(j, n, first):
                k = j % RING
                act.wait_ge(g_full, START + n + 1)
                if not (first and j < RING):
                    act.wait_ge(gu_ready, START + n - RING + 1)
                a(sg[k][:, :], pg[j % 2][:, :], ACT.Silu).then_inc(g_read, 1)

            def high(j, n, first):
                k = j % RING
                act.wait_ge(av_ready, START + n + 1)
                if not (first and j < RING):
                    act.wait_ge(y_step, START + n - RING + 1)
                a(av_hi[k][:, :], av[k][:, :], ACT.Copy).then_inc(hi_ready, 1)

            def take_logits(i):
                act.wait_ge(lg_full, START + i + 1)
                if i >= 2:
                    act.wait_ge(lt_full, START + i - 1)
                a(logit[i % 2][:, :], (pl, py)[i % 2][0:NE, :], ACT.Copy).then_inc(lg_ready, 1)

            def exp_logits(i):
                act.wait_ge(lt_full, START + i + 1)
                a(ex[:, i * NC:(i + 1) * NC, :].rearrange("p c e -> p (c e)"), (pl, py)[i % 2][:, 0:NC * NE], ACT.Exp, scale=-1.0)\
                    .then_inc(ex_ready, 1)

            def take_weights(i):
                act.wait_ge(ct_full, START + i + 1)
                act.wait_ge(ct_ready, START + i)
                a(comb_f[:, :], pl[0:NE, :], ACT.Copy).then_inc(cf_ready, 1)
                act.wait_ge(cf_ready, START + i + 1)
                a(comb_t[0:NE, bass.ds(i * TT, TT)], comb_f[:, :], ACT.Copy).then_inc(chi_ready, 1)

            def square(i):
                act.wait_ge(xc_ready, START + i + 1)
                a(sq[:, :], s[:, :], ACT.Square).then_inc(sq_ready, 1)

            def rstd(i):
                act.wait_ge(var_full, START + i + 1)
                a(r[:, :], pm[:, :], ACT.Ln, bias=eps[:, :]).then_inc(lv_ready, 1)
                act.wait_ge(lv_ready, START + i + 1)
                a(r[:, :], r[:, :], ACT.Exp, scale=-0.5).then_inc(rstd_ready, 1)

            act.preload_act_table_set("natural_log_exp_and_others")
            act.wait_ge(s_eps, START + 1)
            for i in range(0, NTILE, 2):
                take_logits(i)
                take_logits(i + 1)
                if i == 0:
                    a(x_hi[:, 0:TT], xf[:, 0:TT], ACT.Copy).then_inc(x_hi_ready, 1)
                exp_logits(i)
                exp_logits(i + 1)
            with act.Fori(1, NTILE) as i:
                t = bass.ds(i * TT, TT)
                a(x_hi[:, t], xf[:, t], ACT.Copy).then_inc(x_hi_ready, 1)
            act.wait_ge(s_weights, n_weights)
            act.wait_ge(comb0, START + 2)
            a(sel2[0:NE, :], sel[:, :], ACT.Copy)
            a(sel2[LO:LO + NE, :], sel[:, :], ACT.Copy).then_inc(sel_ready, 1)
            act.preload_act_table_set("silu_and_others")
            silu(0, 0, True)
            silu(1, 1, True)
            take_weights(0)

            def body(i, first, last):
                for j in range(NPR):
                    n = i * NPR + j
                    if j < NPR - 2:
                        silu(j + 2, n + 2, first)
                    elif not last:
                        silu(j + 2 - NPR, n + 2, False)
                    high(j, n, first)
                    if not first and j == 2:
                        square(i - 1)
                    if not first and j == 3:
                        act.preload_act_table_set("natural_log_exp_and_others")
                        rstd(i - 1)
                        act.preload_act_table_set("silu_and_others")
                    if not last and j == (NPR - 1 if first else 5):
                        take_weights(i + 1)
            tiles(act, body)
            act.preload_act_table_set("natural_log_exp_and_others")
            square(NTILE - 1)
            rstd(NTILE - 1)

        @block.vector
        def _(dve):
            v = nc.vector
            STEPS = 29
            every = (ex, sc, sfc, mx, mn, t1, t2, t3, gs, gcnt, masked, top8, above, equal, count, chosen, w, comb,
                     n_above, den, rden, ggt, geq)

            def route(group, lo, hi):
                n, k, chunks = [0], (hi - lo) * NC, slice(lo * NC, hi * NC)
                ex, sc, sfc, mx, mn, t1, t2, t3, gs, gcnt, masked, top8, above, equal, count, chosen, w, comb = (
                    x[:, chunks, :] for x in every[:18])
                n_above, den, rden = (x[:, chunks] for x in every[18:21])
                ggt, geq = (x[:, chunks, :, :] for x in every[21:])

                def step(ins):
                    n[0] += 1
                    ins.then_inc(chain, 1)
                    dve.wait_ge(chain, START + group * STEPS + n[0])

                dve.wait_ge(ex_ready, START + hi)
                step(v.tensor_scalar(ex, ex, 1.0, None, ALU.add))
                yield
                step(v.reciprocal(sc, ex))
                yield
                step(v.tensor_tensor(sfc, sc, ebias[:, :].unsqueeze(1).broadcast_to([P, k, NE]), ALU.add))
                yield
                pairs = sfc.rearrange("p c (n two) -> p c n two", two=2)
                step(v.tensor_tensor(mx, pairs[:, :, :, 0], pairs[:, :, :, 1], ALU.max))
                yield
                step(v.tensor_tensor(mn, pairs[:, :, :, 0], pairs[:, :, :, 1], ALU.min))
                yield
                hi = mx.rearrange("p c (g two) -> p c g two", two=2)
                lo = mn.rearrange("p c (g two) -> p c g two", two=2)
                step(v.tensor_tensor(t1, hi[:, :, :, 0], hi[:, :, :, 1], ALU.max))
                yield
                step(v.tensor_tensor(t2, hi[:, :, :, 0], hi[:, :, :, 1], ALU.min))
                yield
                step(v.tensor_tensor(t3, lo[:, :, :, 0], lo[:, :, :, 1], ALU.max))
                yield
                step(v.tensor_tensor(t2, t2, t3, ALU.max))
                yield
                step(v.tensor_tensor(gs, t1, t2, ALU.add))
                yield
                other = gs.unsqueeze(2).broadcast_to([P, k, NG, NG])
                own = gs.unsqueeze(3).broadcast_to([P, k, NG, NG])
                before = below[:, :, :].unsqueeze(1).broadcast_to([P, k, NG, NG])
                step(v.tensor_tensor(geq, other, own, ALU.is_equal))
                yield
                step(v.tensor_tensor(ggt, other, own, ALU.is_gt))
                yield
                step(v.tensor_tensor(geq, geq, before, ALU.mult))
                yield
                step(v.tensor_tensor(ggt, ggt, geq, ALU.add))
                yield
                step(v.tensor_reduce(gcnt, ggt, AX.X, ALU.add))
                yield
                step(v.tensor_scalar(gcnt, gcnt, TOP_G - 0.5, None, ALU.is_lt))
                yield
                step(v.tensor_tensor(masked.rearrange("p c (g e) -> p c g e", g=NG), sfc.rearrange("p c (g e) -> p c g e", g=NG),
                                     gcnt.unsqueeze(3).broadcast_to([P, k, NG, GE]), ALU.mult))
                yield
                v.memset(n_above, 0.0)
                for c in range(k):
                    last = v.max(top8[:, c, :], masked[:, c, :])
                step(last)
                yield
                kth = top8[:, :, TOP_K - 1:TOP_K].broadcast_to([P, k, NE])
                step(v.tensor_tensor(above, masked, kth, ALU.is_gt))
                yield
                step(v.tensor_reduce(n_above, above, AX.X, ALU.add))
                yield
                step(v.tensor_tensor(equal, masked, kth, ALU.is_equal))
                yield
                flat = lambda x: x.rearrange("p c e -> p (c e)")
                step(v.tensor_tensor_scan(flat(count), inner[:, 0:k * NE], flat(equal), 0.0, ALU.mult, ALU.add))
                yield
                step(v.tensor_tensor(count, count, n_above.unsqueeze(2).broadcast_to([P, k, NE]), ALU.add))
                yield
                step(v.scalar_tensor_tensor(chosen, count, TOP_K + 0.5, equal, ALU.is_lt, ALU.mult))
                yield
                step(v.tensor_tensor(chosen, chosen, above, ALU.add))
                yield
                step(v.tensor_tensor(w, sc, chosen, ALU.mult))
                yield
                step(v.tensor_reduce(den, w, AX.X, ALU.add))
                yield
                step(v.tensor_scalar(den, den, 1e-20, None, ALU.add))
                yield
                step(v.reciprocal(rden, den))
                yield
                v.tensor_tensor(comb, w, rden.unsqueeze(2).broadcast_to([P, k, NE]), ALU.mult).then_inc(all_ready, 1)
                assert n[0] == STEPS, n[0]

            def choose(i, first):
                dve.wait_ge(all_ready, START + (1 if first else 2))
                dve.wait_ge(ct_full, START + i)
                v.tensor_copy(comb_now[:, :, :], comb[:, bass.ds(i * NC, NC), :]).then_inc(comb_ready, 1)

            def low_weights(i):
                dve.wait_ge(chi_ready, START + i + 1)
                t = bass.ds(i * TT, TT)
                v.tensor_tensor(comb_t[LO:LO + NE, t], comb_f[:, :], comb_t[0:NE, t].bitcast(F32), ALU.subtract).then_inc(ct_ready, 1)

            def gate(j, n):
                k = j % RING
                dve.wait_ge(g_read, START + n + 1)
                dve.wait_ge(u_full, START + n + 1)
                v.tensor_tensor(gu[k][:, :], sg[k][:, :], pu[j % 2][:, :], ALU.mult).then_inc(gu_ready, 1)

            def weigh(j, n, first):
                k = j % RING
                dve.wait_ge(gu_ready, START + n + 1)
                dve.wait_ge(c_full, START + n + 1)
                if not (first and j < RING):
                    dve.wait_ge(lo_ready, START + n - RING + 1)
                v.tensor_tensor(av[k][:, :], gu[k][:, :], pc[:, :], ALU.mult).then_inc(av_ready, 1)

            def total(i):
                dve.wait_ge(y_step, START + (i + 1) * NPR)
                v.tensor_tensor(s[:, :], py[:, :], xf[:, bass.ds(i * TT, TT)], ALU.add).then_inc(s_ready, 1)

            def centre(i):
                dve.wait_ge(mean_full, START + i + 1)
                v.tensor_tensor(s[:, :], s[:, :], pm[:, :], ALU.subtract).then_inc(xc_ready, 1)

            def scale(i):
                dve.wait_ge(rstd_ready, START + i + 1)
                v.tensor_tensor(of[:, bass.ds(i * TT, TT)], s[:, :], r[:, :], ALU.mult).then_inc(out_ready, 1)

            v.memset(comb_t[:, :].bitcast(F32), 0.0).then_inc(comb0, 1)
            v.memset(sel2[:, :].bitcast(F32), 0.0).then_inc(comb0, 1)
            dve.wait_ge(s_weights, n_weights)
            for _ in route(0, 0, 1):
                pass
            choose(0, True)
            gate(0, 0)
            low_weights(0)

            def body(i, first, last):
                steps = route(1, 1, NTILE) if first else iter(())
                for j in range(NPR):
                    n = i * NPR + j
                    weigh(j, n, first)
                    for _ in range(2):
                        next(steps, None)
                    if j < NPR - 1:
                        gate(j + 1, n + 1)
                    elif not last:
                        gate(0, n + 1)
                    if j < NPR - 1:
                        for _ in range(3):
                            next(steps, None)
                    if not first:
                        if j == 1:
                            total(i - 1)
                        if j == 2:
                            centre(i - 1)
                        if j == 4:
                            scale(i - 1)
                    if not last and j == (NPR - 1 if first else 4):
                        for _ in steps:
                            pass
                        choose(i + 1, False)
                    if not last and j == (NPR - 1 if first else 6):
                        low_weights(i + 1)
            tiles(dve, body)
            total(NTILE - 1)
            centre(NTILE - 1)
            scale(NTILE - 1)


def constants():
    i = np.arange(P)
    le, gt = i[:, None] <= i[None, :], i[:, None] > i[None, :]
    parts = [le, gt, np.ones((P, P)), np.eye(P), np.full((P, P), 1 / D), np.full((P, P), 1 / DI)]
    return np.stack(parts, 1).astype(np.float32)


def program(nc, d):
    with ExitStack() as ctx:
        def sb(name, shape, dt=F32, scope=ctx):
            return scope.enter_context(nc.sbuf_tensor(name, shape, dt))

        full = lambda x: x[tuple(slice(None) for _ in x.shape)]
        XP = sb("XP", [P, NTILE, TP])
        C = sb("C", [P, 6, P])
        cst = tuple(C[:, k, :] for k in range(6))
        late = ["wr", "wk", "wv", "wo", "decay", "t_rem", "w_par", "bo", "keep", "behind", "gw", "ebias", "sel", "inner", "below"]
        split = ["gp", "eup", "dp"]
        W = {n: sb("W_" + n, list(d[n].shape)) for n in late}
        halves = {n: (sb(f"W_{n}_hi", list(d[n].shape), F32R), sb(f"W_{n}_lo", list(d[n].shape), F32R)) for n in split}
        s_weights = ctx.enter_context(nc.semaphore("s_weights"))

        with ExitStack() as early:
            XH = sb("XH", [P, NB, (1 + NL) * T], scope=early)
            for n in ["f_up", "f_down"] + split:
                W[n] = sb("W_" + n, list(d[n].shape), scope=early)
            n_weights = 16 * len(W)
            mamba(nc, XH, cst, d["x"], d["win"], d["wout"], d["par"], d["row"], d["again"], [(C[:, :, :], d["cst"])],
                  [(full(w), d[n]) for n, w in W.items()], s_weights)
            ffn(nc, XH[:, :, 0:T], XH[:, :, NL * T:], XP, cst,
                (W["f_up"], W["f_down"], [(full(W[n]), *map(full, halves[n])) for n in split], s_weights, n_weights))
        X, H = sb("X", [P, NB, T]), sb("H", [P, NB, T])
        wkv(nc, X, XP, H, cst, tuple(W[n] for n in ("wr", "wk", "wv", "wo", "decay", "t_rem", "w_par", "bo", "keep", "behind"))
            + (s_weights, n_weights))
        moe(nc, X, H, cst, (W["gw"], W["ebias"], *(halves[n] for n in split), W["sel"], W["inner"], W["below"], s_weights, n_weights),
            d["out"])


def kernel(**inputs):
    from concourse import bacc
    from concourse.bass_utils import run_bass_kernel_spmd

    z = {k: np.asarray(v) for k, v in inputs.items()}
    f = np.ascontiguousarray
    feat = lambda x: f(x.reshape(-1, P).T)
    blocks = lambda w: f(w.T.reshape(-1, P, w.shape[0]).transpose(1, 0, 2))
    its = lambda x: np.repeat(x, NT, axis=0)
    per = lambda x: x.reshape(NL, -1, P).transpose(0, 2, 1)
    arrays = {
        "x": feat(z["L0_attn_x"]).reshape(P, NB, T),
        "win": its(f(z["L0_attn_in_proj_w"].transpose(0, 2, 1))),
        "wout": its(f(z["L0_attn_out_proj_w"].transpose(0, 2, 1).reshape(NL, 2, P, D).transpose(0, 2, 1, 3))),
        "par": f(its(np.concatenate([
            per(z["L0_attn_ln_w"]), per(z["L0_attn_ln_b"]),
            z["L0_attn_conv_w"].reshape(NL, 3, P, DC).transpose(0, 2, 1, 3).reshape(NL, P, 3 * DC),
            per(z["L0_attn_conv_b"]), per(np.repeat(z["L0_attn_D"], DS, axis=1)), per(z["L0_attn_rms_w"])], 2)).transpose(1, 0, 2)),
        "row": f(np.broadcast_to(its(np.stack([z["L0_attn_dt_bias"], z["L0_attn_A_log"]], 1)).transpose(1, 0, 2), (P, 2, N_IT, NH))),
        "again": f(np.broadcast_to(np.arange(N_IT + 1) % NT > 0, (P, N_IT + 1)).astype(np.float32)),
        "cst": constants(),
        "f_up": f(z["L0_ffn_w_up"].T), "f_down": blocks(z["L0_ffn_w_down"]),
        "wr": f(z["L1_attn_Wr"].T), "wk": f(z["L1_attn_Wk"].T), "wv": f(z["L1_attn_Wv"].T), "wo": blocks(z["L1_attn_Wo"]),
        "decay": f(np.stack([z["L1_attn_time_decay"], z["L1_attn_bk"]])),
        "t_rem": np.stack([TT - 1 - np.arange(TT), np.ones(TT)]).astype(np.float32),
        "w_par": f(np.stack([z["L1_attn_U"], z["L1_attn_bk"], z["L1_attn_br"], z["L1_attn_bv"],
                             z["L1_attn_time_decay"]], -1).reshape(NF, P, 5).transpose(1, 0, 2)),
        "bo": f(z["L1_attn_bo"][:, None]),
        "keep": f(np.broadcast_to(np.arange(NTILE) % NT > 0, (P, NTILE)).astype(np.float32)),
        "behind": f(np.broadcast_to(T - TT * (np.arange(NTILE) % NT + 1), (P, NTILE)).astype(np.float32)),
        "gw": f(z["L1_ffn_gate_weight"].T), "ebias": f(np.broadcast_to(z["L1_ffn_e_bias"], (P, NE))),
        "gp": f(z["L1_ffn_gate_proj"].reshape(NE * I, D).T), "eup": f(z["L1_ffn_up_proj"].reshape(NE * I, D).T),
        "dp": f(z["L1_ffn_down_proj"].transpose(0, 2, 1).reshape(NPR, P, D).transpose(1, 0, 2)),
        "sel": f(np.repeat(np.eye(NE), I, axis=1).astype(np.float32)),
        "inner": f(np.broadcast_to(np.arange(NTILE * NC * NE) % NE > 0, (P, NTILE * NC * NE)).astype(np.float32)),
        "below": f(np.broadcast_to(np.arange(NG)[:, None] > np.arange(NG)[None, :], (P, NG, NG)).astype(np.float32)),
    }
    nc = bacc.Bacc("TRN2", target_bir_lowering=False, num_devices=1)
    d = {n: nc.dram_tensor(f"in_{n}", a.shape, mybir.dt.from_np(a.dtype), kind="ExternalInput").ap() for n, a in arrays.items()}
    d["out"] = nc.dram_tensor("out_y", (P, NB * T), F32, kind="ExternalOutput").ap()
    program(nc, d)
    r = run_bass_kernel_spmd(nc, [{f"in_{n}": a for n, a in arrays.items()}], core_ids=[0])
    y = np.asarray(r.results[0]["out_y"])
    return f(y.T.reshape(NB, T, D))
```
